# Optimizing a Trainium2 kernel written in Bass

```python
import numpy as np
import jax
import jax.numpy as jnp

def _softmax(x, axis=-1):
    return jax.nn.softmax(x, axis=axis)

def _gelu(x):
    return jax.nn.gelu(x, approximate=True)

def _silu(x):
    return jax.nn.silu(x)

def _sigmoid(x):
    return jax.nn.sigmoid(x)

def _layernorm(x, axis=-1, eps=1e-05):
    m = jnp.mean(x, axis=axis, keepdims=True)
    v = jnp.var(x, axis=axis, keepdims=True)
    return (x - m) / jnp.sqrt(v + eps)

def _scatter_add(tgt, idx, src, axis=0):
    return tgt.at[idx].add(src)

def _segment_sum(src, seg, n):
    return jax.ops.segment_sum(src, seg, n)
kernel_name = 'mk_sandwich_d1_jaxref_r4_06d1b7'

def setup_inputs(seed: int=0):
    np.random.seed(seed)
    _w = jnp.asarray

    def _L0_attn_setup():
        import jax, jax.numpy as jnp
        import numpy as np
        D_MODEL = 256
        D_STATE = 16
        D_CONV = 4
        EXPAND = 2
        D_INNER = D_MODEL * EXPAND
        B = 1
        L = 512
        key = jax.random.key(seed)
        ks = jax.random.split(key, 8)
        s = lambda k, shape, scale: jax.random.normal(k, shape, dtype=jnp.float32) * scale
        return {'x': jax.random.normal(ks[0], (B, L, D_MODEL), dtype=jnp.float32), 'in_proj_w': s(ks[1], (D_INNER * 2, D_MODEL), D_MODEL ** (-0.5)), 'conv_w': s(ks[2], (D_INNER, 1, D_CONV), D_CONV ** (-0.5)), 'conv_b': jnp.zeros((D_INNER,), jnp.float32), 'x_proj_w': s(ks[3], (2 * D_STATE + 1, D_INNER), D_INNER ** (-0.5)), 'dt_proj_w': s(ks[4], (D_INNER, 1), 1.0), 'dt_proj_b': jnp.zeros((D_INNER,), jnp.float32), 'A_log': jnp.log(jnp.broadcast_to(jnp.arange(1, D_STATE + 1, dtype=jnp.float32), (D_INNER, D_STATE))), 'D': jnp.ones((D_INNER,), jnp.float32), 'out_proj_w': s(ks[5], (D_MODEL, D_INNER), D_INNER ** (-0.5))}
    _L0_attn_in = _L0_attn_setup()

    def _L0_ffn_setup():
        import jax, jax.numpy as jnp
        import numpy as np
        D, H, P, E, K, F = (256, 16, 64, 8, 2, 1024)
        B, S = (2, 512)
        NROT = 32
        BASE = 10000.0
        EPS = 1e-05

        def _ln(x, g, b):
            m = jnp.mean(x, -1, keepdims=True)
            v = jnp.mean(jnp.square(x - m), -1, keepdims=True)
            return (x - m) * jax.lax.rsqrt(v + EPS) * g + b

        def _rope(x):
            xr, xp = (x[..., :NROT], x[..., NROT:])
            half = NROT // 2
            inv = BASE ** (-jnp.arange(half, dtype=jnp.float32) / half)
            ang = jnp.arange(x.shape[2], dtype=jnp.float32)[:, None] * inv[None, :]
            cos, sin = (jnp.cos(ang), jnp.sin(ang))
            x1, x2 = (xr[..., :half], xr[..., half:])
            xr = jnp.concatenate([x1 * cos - x2 * sin, x1 * sin + x2 * cos], -1)
            return jnp.concatenate([xr, xp], -1)

        def _gate(x, Wsel):
            s = jax.nn.sigmoid(jnp.einsum('bsd,hed->bhse', x, Wsel))
            _, idx = jax.lax.top_k(s, K)
            mask = jax.nn.one_hot(idx, E, dtype=s.dtype).sum(-2)
            return s * mask

        def _moe_attn(x, Wq, Wk, Wv, Wo, Wsel_v, Wsel_o):
            q = _rope(jnp.einsum('bsd,hdp->bhsp', x, Wq))
            k = _rope(jnp.einsum('bsd,hdp->bhsp', x, Wk))
            gv = _gate(x, Wsel_v)
            v = jnp.einsum('bsd,bhse,hedp->bhsp', x, gv, Wv)
            att = jax.nn.softmax(jnp.einsum('bhsp,bhtp->bhst', q, k) / np.sqrt(P), axis=-1)
            o = jnp.einsum('bhst,bhtp->bhsp', att, v)
            go = _gate(x, Wsel_o)
            return jnp.einsum('bhsp,bhse,hepd->bsd', o, go, Wo)
        key = jax.random.key(seed)
        ks = jax.random.split(key, 10)
        f = lambda k, sh: jax.random.normal(k, sh, jnp.float32) * 0.02
        return dict(src=jax.random.normal(ks[0], (B, S, D), jnp.float32), Wq=f(ks[1], (H, D, P)), Wk=f(ks[2], (H, D, P)), Wv=f(ks[3], (H, E, D, P)), Wo=f(ks[4], (H, E, P, D)), Wsel_v=f(ks[5], (H, E, D)), Wsel_o=f(ks[6], (H, E, D)), ln1_g=jnp.ones(D, jnp.float32), ln1_b=jnp.zeros(D, jnp.float32), ln2_g=jnp.ones(D, jnp.float32), ln2_b=jnp.zeros(D, jnp.float32), W1=f(ks[7], (D, F)), b1=jnp.zeros(F, jnp.float32), W2=f(ks[8], (F, D)), b2=jnp.zeros(D, jnp.float32))
    _L0_ffn_in = _L0_ffn_setup()
    _d = {'L0_attn_x': _L0_attn_in['x'], 'L0_attn_in_proj_w': _L0_attn_in['in_proj_w'], 'L0_attn_conv_w': _L0_attn_in['conv_w'], 'L0_attn_conv_b': _L0_attn_in['conv_b'], 'L0_attn_x_proj_w': _L0_attn_in['x_proj_w'], 'L0_attn_dt_proj_w': _L0_attn_in['dt_proj_w'], 'L0_attn_dt_proj_b': _L0_attn_in['dt_proj_b'], 'L0_attn_A_log': _L0_attn_in['A_log'], 'L0_attn_D': _L0_attn_in['D'], 'L0_attn_out_proj_w': _L0_attn_in['out_proj_w'], 'L0_ffn_Wq': _L0_ffn_in['Wq'], 'L0_ffn_Wk': _L0_ffn_in['Wk'], 'L0_ffn_Wv': _L0_ffn_in['Wv'], 'L0_ffn_Wo': _L0_ffn_in['Wo'], 'L0_ffn_Wsel_v': _L0_ffn_in['Wsel_v'], 'L0_ffn_Wsel_o': _L0_ffn_in['Wsel_o'], 'L0_ffn_ln1_g': _L0_ffn_in['ln1_g'], 'L0_ffn_ln1_b': _L0_ffn_in['ln1_b'], 'L0_ffn_ln2_g': _L0_ffn_in['ln2_g'], 'L0_ffn_ln2_b': _L0_ffn_in['ln2_b'], 'L0_ffn_W1': _L0_ffn_in['W1'], 'L0_ffn_b1': _L0_ffn_in['b1'], 'L0_ffn_W2': _L0_ffn_in['W2'], 'L0_ffn_b2': _L0_ffn_in['b2']}
    _x0 = _d['L0_attn_x']
    _d['L0_attn_x'] = jax.random.normal(jax.random.fold_in(jax.random.key(seed), 1), (8, 512, 256), dtype=_x0.dtype)
    del _x0
    return _d

def reference(L0_attn_x, L0_attn_in_proj_w, L0_attn_conv_w, L0_attn_conv_b, L0_attn_x_proj_w, L0_attn_dt_proj_w, L0_attn_dt_proj_b, L0_attn_A_log, L0_attn_D, L0_attn_out_proj_w, L0_ffn_Wq, L0_ffn_Wk, L0_ffn_Wv, L0_ffn_Wo, L0_ffn_Wsel_v, L0_ffn_Wsel_o, L0_ffn_ln1_g, L0_ffn_ln1_b, L0_ffn_ln2_g, L0_ffn_ln2_b, L0_ffn_W1, L0_ffn_b1, L0_ffn_W2, L0_ffn_b2):

    def _L0_attn_ref(x, in_proj_w, conv_w, conv_b, x_proj_w, dt_proj_w, dt_proj_b, A_log, D, out_proj_w):
        import jax, jax.numpy as jnp
        import numpy as np
        D_MODEL = 256
        D_STATE = 16
        D_CONV = 4
        EXPAND = 2
        D_INNER = D_MODEL * EXPAND
        B = 1
        L = 512
        Bb = x.shape[0]
        xz = x @ in_proj_w.T
        x_ssm, z = jnp.split(xz, 2, axis=-1)
        xt = jnp.swapaxes(x_ssm, 1, 2)
        xc = jax.lax.conv_general_dilated(xt, conv_w, window_strides=(1,), padding=[(D_CONV - 1, 0)], feature_group_count=D_INNER, dimension_numbers=('NCH', 'OIH', 'NCH'))
        xc = xc + conv_b[None, :, None]
        xc = jax.nn.silu(jnp.swapaxes(xc, 1, 2))
        A = -jnp.exp(A_log)
        xp = xc @ x_proj_w.T
        dt_r = xp[..., :1]
        Bv = xp[..., 1:1 + D_STATE]
        Cv = xp[..., 1 + D_STATE:]
        dt = jax.nn.softplus(dt_r @ dt_proj_w.T + dt_proj_b)
        dA = jnp.exp(dt[..., None] * A)
        dBx = dt[..., None] * Bv[:, :, None, :] * xc[..., None]

        def step(h, inps):
            dA_t, dBx_t, C_t = inps
            h = dA_t * h + dBx_t
            y = jnp.einsum('bdn,bn->bd', h, C_t)
            return (h, y)
        h0 = jnp.zeros((Bb, D_INNER, D_STATE), x.dtype)
        _, ys = jax.lax.scan(step, h0, (jnp.swapaxes(dA, 0, 1), jnp.swapaxes(dBx, 0, 1), jnp.swapaxes(Cv, 0, 1)))
        y = jnp.swapaxes(ys, 0, 1) + xc * D
        return y * jax.nn.silu(z) @ out_proj_w.T

    def _L0_ffn_ref(src, Wq, Wk, Wv, Wo, Wsel_v, Wsel_o, ln1_g, ln1_b, ln2_g, ln2_b, W1, b1, W2, b2):
        import jax, jax.numpy as jnp
        import numpy as np
        D, H, P, E, K, F = (256, 16, 64, 8, 2, 1024)
        B, S = (2, 512)
        NROT = 32
        BASE = 10000.0
        EPS = 1e-05

        def _ln(x, g, b):
            m = jnp.mean(x, -1, keepdims=True)
            v = jnp.mean(jnp.square(x - m), -1, keepdims=True)
            return (x - m) * jax.lax.rsqrt(v + EPS) * g + b

        def _rope(x):
            xr, xp = (x[..., :NROT], x[..., NROT:])
            half = NROT // 2
            inv = BASE ** (-jnp.arange(half, dtype=jnp.float32) / half)
            ang = jnp.arange(x.shape[2], dtype=jnp.float32)[:, None] * inv[None, :]
            cos, sin = (jnp.cos(ang), jnp.sin(ang))
            x1, x2 = (xr[..., :half], xr[..., half:])
            xr = jnp.concatenate([x1 * cos - x2 * sin, x1 * sin + x2 * cos], -1)
            return jnp.concatenate([xr, xp], -1)

        def _gate(x, Wsel):
            s = jax.nn.sigmoid(jnp.einsum('bsd,hed->bhse', x, Wsel))
            _, idx = jax.lax.top_k(s, K)
            mask = jax.nn.one_hot(idx, E, dtype=s.dtype).sum(-2)
            return s * mask

        def _moe_attn(x, Wq, Wk, Wv, Wo, Wsel_v, Wsel_o):
            q = _rope(jnp.einsum('bsd,hdp->bhsp', x, Wq))
            k = _rope(jnp.einsum('bsd,hdp->bhsp', x, Wk))
            gv = _gate(x, Wsel_v)
            v = jnp.einsum('bsd,bhse,hedp->bhsp', x, gv, Wv)
            att = jax.nn.softmax(jnp.einsum('bhsp,bhtp->bhst', q, k) / np.sqrt(P), axis=-1)
            o = jnp.einsum('bhst,bhtp->bhsp', att, v)
            go = _gate(x, Wsel_o)
            return jnp.einsum('bhsp,bhse,hepd->bsd', o, go, Wo)
        src2 = _moe_attn(src, Wq, Wk, Wv, Wo, Wsel_v, Wsel_o)
        src = src + src2
        src = _ln(src, ln1_g, ln1_b)
        src2 = jax.nn.relu(src @ W1 + b1) @ W2 + b2
        src = src + src2
        return _ln(src, ln2_g, ln2_b)
    x = L0_attn_x
    x = x + _layernorm(_L0_attn_ref(_layernorm(x, axis=-1), L0_attn_in_proj_w, L0_attn_conv_w, L0_attn_conv_b, L0_attn_x_proj_w, L0_attn_dt_proj_w, L0_attn_dt_proj_b, L0_attn_A_log, L0_attn_D, L0_attn_out_proj_w), axis=-1)
    x = x + _layernorm(_L0_ffn_ref(_layernorm(x, axis=-1), L0_ffn_Wq, L0_ffn_Wk, L0_ffn_Wv, L0_ffn_Wo, L0_ffn_Wsel_v, L0_ffn_Wsel_o, L0_ffn_ln1_g, L0_ffn_ln1_b, L0_ffn_ln2_g, L0_ffn_ln2_b, L0_ffn_W1, L0_ffn_b1, L0_ffn_W2, L0_ffn_b2), axis=-1)
    return x

_drawn_inputs = setup_inputs


def setup_inputs(seed=0):
    import zlib

    import numpy as np

    out = dict(_drawn_inputs(seed))
    spreads = {'L0_attn_conv_b': (0.0, 0.1),
     'L0_attn_dt_proj_b': (0.0, 0.1),
     'L0_attn_D': (1.0, 0.2),
     'L0_ffn_ln1_g': (1.0, 0.2),
     'L0_ffn_ln1_b': (0.0, 0.1),
     'L0_ffn_ln2_g': (1.0, 0.2),
     'L0_ffn_ln2_b': (0.0, 0.1),
     'L0_ffn_b1': (0.0, 0.487),
     'L0_ffn_b2': (0.0, 0.1)}
    factors = {'L0_ffn_Wq': 8.0,
     'L0_ffn_Wk': 8.0,
     'L0_ffn_Wv': 8.0,
     'L0_ffn_Wo': 8.0,
     'L0_ffn_Wsel_v': 8.0,
     'L0_ffn_Wsel_o': 8.0}
    for name, (base, spread) in spreads.items():
        noise = np.random.default_rng([zlib.crc32(name.encode()), seed]).standard_normal(out[name].shape)
        drawn = base * np.exp(spread * noise) if base else spread * noise
        out[name] = jnp.asarray(drawn.astype(out[name].dtype))
    for name, factor in factors.items():
        out[name] = (out[name] * factor).astype(out[name].dtype)
    return out
```

```python
from contextlib import ExitStack

import numpy as np

import concourse.bass as bass
from concourse import mybir

F32 = mybir.dt.float32
ALU = mybir.AluOpType
ACT = mybir.ActivationFunctionType
AX = mybir.AxisListType

P = 128
NB, S, D = 8, 512, 256
TT = S // P
KD = D // P
DI = 512
CB = DI // P
NS = 16
TAPS = 4
XP = 2 * NS + 1
H, E, HP, F = 16, 8, 64, 1024
PAIRS = H // 2
EP = E // 2
FB = F // P
NROT, BASE = 32, 10000.0
EPS = 1e-5
G = 2 * H * E
CREDIT = 1


class Norm:

    def __init__(self, ctx, nc, name, eps):
        sem = lambda what: ctx.enter_context(nc.semaphore(f"{name}_{what}"))
        buf = lambda what, n: ctx.enter_context(nc.sbuf_tensor(f"{name}_{what}b", [P, n], F32))
        self.eps = eps
        self.stats_done, self.combine_done = sem("stats"), sem("combine")
        self.stats_done_avg = sem("avg")
        self.log_done, self.guess_done, self.newton_done = sem("log"), sem("guess"), sem("newton")
        self.out_done = sem("out")
        self.stats = buf("stats", TT * 6)
        self.avg, self.var, self.apart, self.spread = (buf(w, TT) for w in ("avg", "var", "apart", "spread"))
        self.logv, self.guess, self.step, self.rstd = (buf(w, TT) for w in ("log", "guess", "step", "rstd"))

    COMBINE = 5

    def mean(self, t):
        return self.avg[:, t:t + 1]

    def variances(self):
        return self.var[:, :]

    def statistics(self, dve, i, rows):
        for t in range(TT):
            dve.bn_stats(self.stats[:, 6 * t:6 * t + 6], rows(t)).then_inc(self.stats_done, 1)
        _, mean_e, m2_e, _, mean_o, m2_o = (self.stats[:, :].rearrange("p (t w) -> p w t", w=6)[:, w, :] for w in range(6))
        done, at = self.combine_done, i * self.COMBINE
        dve.wait_ge(self.stats_done, i * TT + TT)
        dve.tensor_tensor(self.avg[:, :], mean_e, mean_o, ALU.add).then_inc(done, 1)
        dve.tensor_tensor(self.apart[:, :], mean_e, mean_o, ALU.subtract).then_inc(done, 1)
        dve.tensor_tensor(self.spread[:, :], m2_e, m2_o, ALU.add).then_inc(done, 1)
        dve.wait_ge(done, at + 2)
        dve.scalar_tensor_tensor(self.apart[:, :], self.apart[:, :], D / 4.0, self.apart[:, :],
                                 ALU.mult, ALU.mult).then_inc(done, 1)
        dve.tensor_scalar(self.avg[:, :], self.avg[:, :], 0.5, None, ALU.mult).then_inc(self.stats_done_avg, 1)
        dve.wait_ge(done, at + 4)
        dve.tensor_tensor(self.var[:, :], self.spread[:, :], self.apart[:, :], ALU.add).then_inc(done, 1)

    def first_guess(self, act, i):
        act.wait_ge(self.combine_done, i * self.COMBINE + self.COMBINE)
        act.activation(self.logv[:, :], self.variances(), ACT.Ln, bias=self.eps, scale=1.0 / D).then_inc(self.log_done, 1)
        act.wait_ge(self.log_done, i + 1)
        act.activation(self.guess[:, :], self.logv[:, :], ACT.Exp, scale=-0.5).then_inc(self.guess_done, 1)

    def newton(self, dve, i):
        done, at = self.newton_done, i * 5
        dve.wait_ge(self.guess_done, i + 1)
        dve.tensor_scalar(self.step[:, :], self.variances(), 1.0 / D, EPS, ALU.mult, ALU.add).then_inc(done, 1)
        dve.wait_ge(done, at + 1)
        dve.tensor_tensor(self.step[:, :], self.step[:, :], self.guess[:, :], ALU.mult).then_inc(done, 1)
        dve.wait_ge(done, at + 2)
        dve.tensor_tensor(self.step[:, :], self.step[:, :], self.guess[:, :], ALU.mult).then_inc(done, 1)
        dve.wait_ge(done, at + 3)
        dve.tensor_scalar(self.step[:, :], self.step[:, :], -0.5, 1.5, ALU.mult, ALU.add).then_inc(done, 1)
        dve.wait_ge(done, at + 4)
        dve.tensor_tensor(self.rstd[:, :], self.guess[:, :], self.step[:, :], ALU.mult).then_inc(done, 1)
        dve.wait_ge(self.stats_done_avg, i + 1)
        dve.wait_ge(done, at + 5)

    def normalise(self, dve, rows, out):
        for t in range(TT):
            dve.tensor_scalar(out(t), rows(t), self.mean(t), self.rstd[:, t:t + 1],
                              ALU.subtract, ALU.mult).then_inc(self.out_done, 1)


def stage_a(nc, d, const):
    with ExitStack() as ctx:
        def sb(name, shape):
            return ctx.enter_context(nc.sbuf_tensor(name, shape, F32))

        def sem(name):
            return ctx.enter_context(nc.semaphore(name))

        ps = ctx.enter_context(nc.psum_tensor("ps_a", [P, 8, S], F32))
        ident = const["ident"]
        w_in = sb("w_in", [P, KD, 2 * DI])
        w_xp = sb("w_xp", [P, CB, XP])
        w_dt = sb("w_dt", [XP + 1, DI])
        w_out = sb("w_out", [P, CB, D])
        w_sel = sb("w_sel", [P, KD, G])
        conv_w = sb("conv_w", [P, CB, TAPS])
        conv_b = sb("conv_b", [P, CB])
        d_skip = sb("d_skip", [P, CB])
        a_log = sb("a_log", [P, CB * NS])
        a_exp = sb("a_exp", [P, CB * NS])
        a_neg = sb("a_neg", [P, CB, NS])
        first = sb("first", [P, E])
        ones = sb("ones", [P, 1])
        eps = sb("eps_a", [P, 1])

        x_in, x_res, x1 = (sb(n, [P, TT, D]) for n in ("x_in", "x_res", "x1"))
        xn = sb("xn", [P, TT, D])
        xnT = sb("xnT", [P, KD, S])
        conv = sb("conv", [P, CB, S])
        xc = sb("xc", [P, CB, S])
        zs = sb("zs", [P, CB, S])
        xp = sb("xp", [XP + 1, S])
        soft = sb("soft", [P, CB, S])
        dt = sb("dt", [P, CB, S])
        du = sb("du", [P, CB, S])
        dA = [sb(f"dA{n}", [P, CB, S]) for n in range(2)]
        dBx = [sb(f"dBx{n}", [P, CB, S]) for n in range(2)]
        hs = [sb(f"hs{n}", [P, CB, S]) for n in range(2)]
        hc = [sb(f"hc{n}", [P, CB, S]) for n in range(2)]
        mo = sb("mo", [P, TT, D])
        x2 = sb("x2", [P, TT, D])
        x2T = sb("x2T", [P, KD, S])
        sg = sb("sg", [P, TT * G])
        left = sb("left", [P, TT * G])
        pick = sb("pick", [P, TT * G])
        rank = sb("rank", [P, TT * G])
        best = sb("best", [P, TT * G // E])
        gate = sb("gate", [P, TT * G])

        def groups(t):
            return t[:, :].rearrange("p (g e) -> p g e", e=E)

        best_e = best[:, :].unsqueeze(2).to_broadcast([P, TT * G // E, E])
        first_g = first[:, :].unsqueeze(1).to_broadcast([P, TT * G // E, E])

        ln_x, ln_m, ln_a = (Norm(ctx, nc, n, eps[:, 0:1]) for n in ("ln_x", "ln_m", "ln_a"))
        consts = ["w_in", "w_xp", "w_dt", "w_out", "w_sel", "conv_w", "conv_b", "d_skip", "a_log", "first"]
        const_tiles = dict(w_in=w_in, w_xp=w_xp, w_dt=w_dt, w_out=w_out, w_sel=w_sel, conv_w=conv_w,
                           conv_b=conv_b, d_skip=d_skip, a_log=a_log, first=first)
        consts_loaded = sem("consts_loaded")
        all_consts = 16 * (len(consts) + 1)
        x_loaded, x_res_loaded = sem("x_loaded"), sem("x_res_loaded")
        fills = sem("fills")
        all_fills = 5
        a_exp_done, a_done = sem("a_exp_done"), sem("a_done")
        xnT_psum, xnT_done = sem("xnT_psum"), sem("xnT_done")
        xs_psum, z_psum = sem("xs_psum"), sem("z_psum")
        tap0_done, taps_done, xc_done, zs_done = sem("tap0_done"), sem("taps_done"), sem("xc_done"), sem("zs_done")
        xp_psum, xp_done, dt_psum = sem("xp_psum"), sem("xp_done"), sem("dt_psum")
        soft_done, relu_done, dt_done, du_done = sem("soft_done"), sem("relu_done"), sem("dt_done"), sem("du_done")
        b_psum, c_psum = sem("b_psum"), sem("c_psum")
        dA_done, dBx_done, scan_done, hc_done = sem("dA_done"), sem("dBx_done"), sem("scan_done"), sem("hc_done")
        y_psum, skip_done, yz_done = sem("y_psum"), sem("skip_done"), sem("yz_done")
        mo_psum, x1_done = sem("mo_psum"), sem("x1_done")
        x2T_psum, x2T_done = sem("x2T_psum"), sem("x2T_done")
        sel_psum, sg_done, top_step, gate_done = sem("sel_psum"), sem("sg_done"), sem("top_step"), sem("gate_done")
        x1_stored, x2T_stored, gate_stored = sem("x1_stored"), sem("x2T_stored"), sem("gate_stored")
        TOP = 12

        def mo_bank(t):
            return ps[:, 4 + t // 2, (t % 2) * D:(t % 2 + 1) * D]

        block = ctx.enter_context(nc.Block())

        @block.sync
        def _(sp):
            for s in (x1_done, x1_stored, x2T_stored, gate_stored):
                sp.sem_inc(s, CREDIT)
            sp.dma_start(ident[:, :], d["ident"]).then_inc(consts_loaded, 16)
            for n in consts:
                sp.dma_start(const_tiles[n][:], d[n]).then_inc(consts_loaded, 16)
            def tiles(name, i):
                return d[name][bass.ds(i, 1)].rearrange("b (t p) c -> p b t c", p=P)

            def batch(i, more):
                sp.wait_ge(x1_done, CREDIT + i)
                sp.dma_start(x_res[:, :, :].unsqueeze(1), tiles("x", i)).then_inc(x_res_loaded, 16)
                if more:
                    sp.wait_ge(ln_x.out_done, i * TT + TT)
                    sp.dma_start(x_in[:, :, :].unsqueeze(1), tiles("x", i + 1)).then_inc(x_loaded, 16)
                sp.wait_ge(x1_done, CREDIT + i + 1)
                sp.dma_start(tiles("x1", i), x1[:, :, :].unsqueeze(1)).then_inc(x1_stored, 16)
                sp.wait_ge(x2T_done, i * KD + KD)
                sp.dma_start(d["xT"][bass.ds(i, 1)].rearrange("b p k s -> p b k s"), x2T[:, :, :].unsqueeze(1)).then_inc(x2T_stored, 16)
                sp.wait_ge(gate_done, i + 1)
                sp.dma_start(d["gates"][bass.ds(i, 1)].rearrange("b p n -> p b n"), gate[:, :].unsqueeze(1)).then_inc(gate_stored, 16)

            sp.dma_start(x_in[:, :, :].unsqueeze(1), tiles("x", 0)).then_inc(x_loaded, 16)
            if NB > 1:
                with sp.Fori(0, NB - 1) as i:
                    batch(i, True)
            batch(NB - 1, False)
            sp.wait_ge(x1_stored, CREDIT + 16 * NB)
            sp.wait_ge(x2T_stored, CREDIT + 16 * NB)
            sp.wait_ge(gate_stored, CREDIT + 16 * NB)

        @block.gpsimd
        def _(pool):
            pool.memset(eps[:, :], EPS).then_inc(fills, 1)
            pool.memset(ones[:, :], 1.0).then_inc(fills, 1)
            pool.memset(xp[:, :], 1.0).then_inc(fills, 1)
            for n in range(2):
                pool.memset(dA[n][:, :, :], 0.0).then_inc(fills, 1)

        @block.tensor
        def _(pe):
            pe.wait_ge(consts_loaded, all_consts)
            pe.wait_ge(fills, all_fills)
            with pe.Fori(0, NB) as i:
                for t in range(TT):
                    pe.wait_ge(ln_x.out_done, i * TT + t + 1)
                    for k in range(KD):
                        mm = pe.transpose(ps[:, k, t * P:(t + 1) * P], xn[:, t, k * P:(k + 1) * P], ident[:, :])
                mm.then_inc(xnT_psum, 1)
                pe.wait_ge(xnT_done, i + 1)
                for m in range(2 * CB):
                    for k in range(KD):
                        mm = pe.matmul(ps[:, m, :], w_in[:, k, m * P:(m + 1) * P], xnT[:, k, :],
                                       start=(k == 0), stop=(k == KD - 1))
                    mm.then_inc(xs_psum if m < CB else z_psum, 1)
                pe.wait_ge(zs_done, i * CB + CB)
                for k in range(CB):
                    pe.wait_ge(xc_done, i * CB + k + 1)
                    mm = pe.matmul(ps[0:XP, 4, :], w_xp[:, k, :], xc[:, k, :], start=(k == 0), stop=(k == CB - 1))
                mm.then_inc(xp_psum, 1)
                pe.wait_ge(xp_done, i + 1)
                for m in range(CB):
                    mm = pe.matmul(ps[:, m, :], w_dt[:, m * P:(m + 1) * P], xp[:, :], start=True, stop=True)
                mm.then_inc(dt_psum, 1)

                def spread(n):
                    if n >= 2:
                        pe.wait_ge(dBx_done, i * NS + n - 1)
                    pe.matmul(ps[:, 4 + n % 2, :], ident[0:XP + 1, 1 + n:2 + n].to_broadcast([XP + 1, P]), xp[:, :],
                              start=True, stop=True).then_inc(b_psum, 1)
                    if n >= 2:
                        pe.wait_ge(hc_done, i * NS + n - 1)
                    pe.matmul(ps[:, 6 + n % 2, :], ident[0:XP + 1, 1 + NS + n:2 + NS + n].to_broadcast([XP + 1, P]), xp[:, :],
                              start=True, stop=True).then_inc(c_psum, 1)

                spread(0)
                spread(1)
                for n in range(NS):
                    pe.wait_ge(hc_done, i * NS + n + 1)
                    for m in range(CB):
                        mm = pe.matmul(ps[:, m, :], ident[:, :], hc[n % 2][:, m, :], start=(n == 0), stop=(n == NS - 1))
                    mm.then_inc(y_psum, 1)
                    if n + 2 < NS:
                        spread(n + 2)
                pe.wait_ge(yz_done, i + 1)
                for t in range(TT):
                    for k in range(CB):
                        mm = pe.matmul(mo_bank(t), conv[:, k, t * P:(t + 1) * P], w_out[:, k, :],
                                       start=(k == 0), stop=(k == CB - 1))
                mm.then_inc(mo_psum, 1)
                for t in range(TT):
                    pe.wait_ge(ln_a.out_done, i * TT + t + 1)
                    for k in range(KD):
                        mm = pe.transpose(ps[:, 6 + k, t * P:(t + 1) * P], x2[:, t, k * P:(k + 1) * P], ident[:, :])
                mm.then_inc(x2T_psum, 1)
                pe.wait_ge(x2T_done, i * KD + KD)
                for t in range(TT):
                    for k in range(KD):
                        mm = pe.matmul(mo_bank(t), x2T[:, k, t * P:(t + 1) * P], w_sel[:, k, :],
                                       start=(k == 0), stop=(k == KD - 1))
                mm.then_inc(sel_psum, 1)

        @block.scalar
        def _(act):
            act.wait_ge(consts_loaded, all_consts)
            act.wait_ge(fills, all_fills)
            act.activation(a_exp[:, :], a_log[:, :], ACT.Exp).then_inc(a_exp_done, 1)
            act.wait_ge(a_exp_done, 1)
            act.mul(a_neg[:, :, :].rearrange("p c n -> p (c n)"), a_exp[:, :], -1.0).then_inc(a_done, 1)
            act.wait_ge(a_done, 1)
            with act.Fori(0, NB) as i:
                ln_x.first_guess(act, i)
                act.wait_ge(xnT_psum, i + 1)
                act.activation(xnT[:, :, :], ps[:, 0:KD, :], ACT.Copy).then_inc(xnT_done, 1)
                for m in range(CB):
                    act.wait_ge(xs_psum, i * CB + m + 1)
                    act.activation(conv[:, m, :], ps[:, m, :], ACT.Identity, bias=conv_b[:, m:m + 1],
                                   scale=conv_w[:, m, TAPS - 1:TAPS]).then_inc(tap0_done, 1)
                for m in range(CB):
                    act.wait_ge(z_psum, i * CB + m + 1)
                    act.activation(zs[:, m, :], ps[:, CB + m, :], ACT.Silu).then_inc(zs_done, 1)
                for m in range(CB):
                    act.wait_ge(taps_done, i * CB * (TAPS - 1) + CB * (TAPS - 2) + m + 1)
                    act.activation(xc[:, m, :], conv[:, m, :], ACT.Silu).then_inc(xc_done, 1)
                act.wait_ge(xp_psum, i + 1)
                act.activation(xp[0:XP, :], ps[0:XP, 4, :], ACT.Copy).then_inc(xp_done, 1)
                act.wait_ge(dt_psum, i + 1)
                act.activation(soft[:, :, :], ps[:, 0:CB, :], ACT.Abs).then_inc(soft_done, 1)
                act.wait_ge(soft_done, i * 3 + 1)
                act.activation(soft[:, :, :], soft[:, :, :], ACT.Exp, scale=-1.0).then_inc(soft_done, 1)
                act.wait_ge(soft_done, i * 3 + 2)
                act.activation(soft[:, :, :], soft[:, :, :], ACT.Ln, bias=ones[:, 0:1]).then_inc(soft_done, 1)
                act.wait_ge(dt_done, i + 1)
                for n in range(NS):
                    if n >= 2:
                        act.wait_ge(scan_done, i * NS + n - 1)
                    for m in range(CB):
                        act.activation(dA[n % 2][:, m, 1:S], dt[:, m, 1:S], ACT.Exp,
                                       scale=a_neg[:, m, n:n + 1]).then_inc(dA_done, 1)
                ln_m.first_guess(act, i)
                ln_a.first_guess(act, i)
                act.wait_ge(x2T_psum, i + 1)
                act.wait_ge(x2T_stored, CREDIT + i * 16)
                for k in range(KD):
                    act.activation(x2T[:, k, :], ps[:, 6 + k, :], ACT.Copy).then_inc(x2T_done, 1)
                act.wait_ge(sel_psum, i + 1)
                act.activation(sg[:, :], ps[:, 4:6, :].rearrange("p a n -> p (a n)"), ACT.Sigmoid).then_inc(sg_done, 1)

        @block.vector
        def _(dve):
            dve.wait_ge(consts_loaded, all_consts)
            dve.wait_ge(fills, all_fills)
            with dve.Fori(0, NB) as i:
                dve.wait_ge(x_loaded, i * 16 + 16)
                ln_x.statistics(dve, i, lambda t: x_in[:, t, :])
                ln_x.newton(dve, i)
                ln_x.normalise(dve, lambda t: x_in[:, t, :], lambda t: xn[:, t, :])
                for r in range(TAPS - 1):
                    sh = r + 1
                    for m in range(CB):
                        if r == 0:
                            dve.wait_ge(tap0_done, i * CB + m + 1)
                        else:
                            dve.wait_ge(taps_done, i * CB * (TAPS - 1) + (r - 1) * CB + m + 1)
                        dve.scalar_tensor_tensor(conv[:, m, sh:S], ps[:, m, 0:S - sh], conv_w[:, m, TAPS - 1 - sh:TAPS - sh],
                                                 conv[:, m, sh:S], ALU.mult, ALU.add).then_inc(taps_done, 1)
                dve.wait_ge(soft_done, i * 3 + 1)
                dve.tensor_scalar(dt[:, :, :], ps[:, 0:CB, :], 0.0, None, ALU.max).then_inc(relu_done, 1)
                dve.wait_ge(relu_done, i + 1)
                dve.wait_ge(soft_done, i * 3 + 3)
                dve.tensor_tensor(dt[:, :, :], dt[:, :, :], soft[:, :, :], ALU.add).then_inc(dt_done, 1)
                dve.wait_ge(dt_done, i + 1)
                dve.wait_ge(xc_done, i * CB + CB)
                dve.tensor_tensor(du[:, :, :], dt[:, :, :], xc[:, :, :], ALU.mult).then_inc(du_done, 1)
                dve.wait_ge(du_done, i + 1)

                def inputs(n):
                    dve.wait_ge(b_psum, i * NS + n + 1)
                    dve.tensor_tensor(dBx[n % 2][:, :, :], du[:, :, :],
                                      ps[:, 4 + n % 2, :].unsqueeze(1).to_broadcast([P, CB, S]), ALU.mult).then_inc(dBx_done, 1)

                inputs(0)
                for n in range(NS):
                    dve.wait_ge(dA_done, i * NS * CB + (n + 1) * CB)
                    dve.wait_ge(dBx_done, i * NS + n + 1)
                    if n >= 2:
                        dve.wait_ge(hc_done, i * NS + n - 1)
                    dve.tensor_tensor_scan(hs[n % 2][:, :, :].rearrange("p c s -> p (c s)"),
                                           dA[n % 2][:, :, :].rearrange("p c s -> p (c s)"),
                                           dBx[n % 2][:, :, :].rearrange("p c s -> p (c s)"),
                                           0.0, ALU.mult, ALU.add).then_inc(scan_done, 1)
                    if n + 1 < NS:
                        inputs(n + 1)
                    dve.wait_ge(scan_done, i * NS + n + 1)
                    dve.wait_ge(c_psum, i * NS + n + 1)
                    if n >= 2:
                        dve.wait_ge(y_psum, i * NS + n - 1)
                    dve.tensor_tensor(hc[n % 2][:, :, :], hs[n % 2][:, :, :],
                                      ps[:, 6 + n % 2, :].unsqueeze(1).to_broadcast([P, CB, S]), ALU.mult).then_inc(hc_done, 1)
                dve.wait_ge(y_psum, i * NS + NS)
                for m in range(CB):
                    dve.scalar_tensor_tensor(soft[:, m, :], xc[:, m, :], d_skip[:, m:m + 1], ps[:, m, :],
                                             ALU.mult, ALU.add).then_inc(skip_done, 1)
                dve.wait_ge(skip_done, i * CB + CB)
                dve.wait_ge(zs_done, i * CB + CB)
                dve.tensor_tensor(conv[:, :, :], soft[:, :, :], zs[:, :, :], ALU.mult).then_inc(yz_done, 1)
                dve.wait_ge(mo_psum, i + 1)
                ln_m.statistics(dve, i, mo_bank)
                ln_m.newton(dve, i)
                ln_m.normalise(dve, mo_bank, lambda t: mo[:, t, :])
                dve.wait_ge(ln_m.out_done, i * TT + TT)
                dve.wait_ge(x_res_loaded, i * 16 + 16)
                dve.wait_ge(x1_stored, CREDIT + i * 16)
                dve.tensor_tensor(x1[:, :, :], x_res[:, :, :], mo[:, :, :], ALU.add).then_inc(x1_done, 1)
                dve.wait_ge(x1_done, CREDIT + i + 1)
                ln_a.statistics(dve, i, lambda t: x1[:, t, :])
                ln_a.newton(dve, i)
                ln_a.normalise(dve, lambda t: x1[:, t, :], lambda t: x2[:, t, :])
                dve.wait_ge(sg_done, i + 1)
                step = i * TOP

                def best_first(src, k):
                    dve.tensor_reduce(best[:, :], groups(src), AX.X, ALU.max).then_inc(top_step, 1)
                    dve.wait_ge(top_step, step + k + 1)
                    dve.tensor_tensor(groups(pick), groups(src), best_e, ALU.is_equal).then_inc(top_step, 1)
                    dve.wait_ge(top_step, step + k + 2)
                    dve.tensor_tensor(groups(rank), groups(pick), first_g, ALU.mult).then_inc(top_step, 1)
                    dve.wait_ge(top_step, step + k + 3)
                    dve.tensor_reduce(best[:, :], groups(rank), AX.X, ALU.max).then_inc(top_step, 1)
                    dve.wait_ge(top_step, step + k + 4)
                    dve.tensor_tensor(groups(pick), groups(rank), best_e, ALU.is_equal).then_inc(top_step, 1)
                    dve.wait_ge(top_step, step + k + 5)
                    dve.scalar_tensor_tensor(left[:, :], pick[:, :], -2.0, src[:, :], ALU.mult, ALU.add).then_inc(top_step, 1)
                    dve.wait_ge(top_step, step + k + 6)

                best_first(sg, 0)
                best_first(left, 6)
                dve.wait_ge(gate_stored, CREDIT + i * 16)
                dve.scalar_tensor_tensor(gate[:, :], left[:, :], 0.0, sg[:, :], ALU.is_lt, ALU.mult).then_inc(gate_done, 1)


def stage_b(nc, d, const, acc):
    with ExitStack() as ctx:
        def sb(name, shape):
            return ctx.enter_context(nc.sbuf_tensor(name, shape, F32))

        def sem(name):
            return ctx.enter_context(nc.semaphore(name))

        ps = ctx.enter_context(nc.psum_tensor("ps_b", [P, 8, S], F32))
        ident = const["ident"]
        gates = sb("gates", [P, NB * TT, G])
        wqk = sb("wqk", [P, KD, 4, P])
        wv = sb("wv", [P, 2, KD, E * HP])
        wo = sb("wo", [P, 2, EP, D])
        cos_q, sin_q, cos_k, sin_k = (sb(n, [P, S]) for n in ("cos_q", "sin_q", "cos_k", "sin_k"))
        xT = sb("xT", [P, KD, S])
        rot = sb("rot", [P, 4, S])
        q, k = sb("q", [P, S]), sb("k", [P, S])
        vg = sb("vg", [P, TT, E, HP])
        v4 = sb("v4", [P, TT, E // 2, HP])
        v2 = sb("v2", [P, TT, E // 4, HP])
        v = sb("v", [P, 2, TT, HP])
        negmax = sb("negmax", [P, 2, TT])
        total = sb("total", [P, 2, TT])
        share = sb("share", [P, 2, TT])
        og_gate = sb("og_gate", [P, 2, TT, E])
        prob = [sb(f"prob{h}", [P, TT, S]) for h in range(2)]
        probT = [sb(f"probT{h}", [P, TT, S]) for h in range(2)]
        og = prob
        ogT = probT

        tables_loaded, gates_loaded, acc_loaded = sem("tables_loaded"), sem("gates_loaded"), sem("acc_loaded")
        w_loaded, xT_loaded = sem("w_loaded"), sem("xT_loaded")
        qk_psum, rot_done, qk_done = sem("qk_psum"), sem("rot_done"), sem("qk_done")
        v_psum, vg_done, vsum_done = sem("v_psum"), sem("vg_done"), sem("vsum_done")
        s_psum, max_done, exp_done = sem("s_psum"), sem("max_done"), sem("exp_done")
        pT_psum, pT_done = sem("pT_psum"), sem("pT_done")
        o_psum, share_step, og_done = sem("o_psum"), sem("share_step"), sem("og_done")
        oT_psum, oT_done = sem("oT_psum"), sem("oT_done")
        out_psum, acc_done = sem("out_psum"), sem("acc_done")
        block = ctx.enter_context(nc.Block())

        @block.sync
        def _(sp):
            for s in (out_psum, v_psum, s_psum, o_psum, acc_done, qk_done, vsum_done):
                sp.sem_inc(s, CREDIT)
            for n, t in (("cos_q", cos_q), ("sin_q", sin_q), ("cos_k", cos_k), ("sin_k", sin_k)):
                sp.dma_start(t[:, :], d[n]).then_inc(tables_loaded, 16)
            with sp.Fori(0, PAIRS) as j:
                sp.wait_ge(out_psum, CREDIT + j * 2 * NB)
                sp.dma_start(wqk[:, :, :, :].unsqueeze(1), d["wqk"][bass.ds(j, 1)].rearrange("j p k w m -> p j k w m")).then_inc(w_loaded, 16)
                sp.dma_start(wv[:, :, :, :].unsqueeze(1), d["wv"][bass.ds(j, 1)].rearrange("j p h k n -> p j h k n")).then_inc(w_loaded, 16)
                sp.dma_start(wo[:, :, :, :].unsqueeze(1), d["wo"][bass.ds(j, 1)].rearrange("j p h e n -> p j h e n")).then_inc(w_loaded, 16)
                with sp.Fori(0, NB) as b:
                    it = j * NB + b
                    sp.wait_ge(v_psum, CREDIT + it * 2 * TT)
                    sp.dma_start(xT[:, :, :].unsqueeze(1), d["xT"][bass.ds(b, 1)].rearrange("b p k s -> p b k s")).then_inc(xT_loaded, 16)

        @block.gpsimd
        def _(pool):
            pool.dma_start(gates[:, :, :].rearrange("p (b t) g -> p b (t g)", b=NB), d["gates"].rearrange("b p n -> p b n")).then_inc(gates_loaded, 16)
            pool.dma_start(acc[:, :, :, :], d["xT"].rearrange("b p k s -> p b k s")).then_inc(acc_loaded, 16)
            with pool.Fori(0, PAIRS) as j, pool.Fori(0, NB) as b:
                it = j * NB + b
                for w, t in ((0, q), (1, k)):
                    pool.wait_ge(rot_done, it * 4 + 2 * w + 2)
                    if w == 0:
                        pool.wait_ge(s_psum, CREDIT + it * 2 * TT)
                    pool.tensor_tensor(t[:, :], rot[:, 2 * w, :], rot[:, 2 * w + 1, :], ALU.add).then_inc(qk_done, 1)
                for h in range(2):
                    pool.wait_ge(vg_done, it * 2 * TT + h * TT + TT)
                    at = it * 6 + h * 3
                    pool.tensor_tensor(v4[:, :, :, :], vg[:, :, 0:4, :], vg[:, :, 4:8, :], ALU.add).then_inc(vsum_done, 1)
                    pool.wait_ge(vsum_done, CREDIT + at + 1)
                    pool.tensor_tensor(v2[:, :, :, :], v4[:, :, 0:2, :], v4[:, :, 2:4, :], ALU.add).then_inc(vsum_done, 1)
                    pool.wait_ge(vsum_done, CREDIT + at + 2)
                    pool.wait_ge(o_psum, CREDIT + it * 2 + h)
                    pool.tensor_tensor(v[:, h, :, :], v2[:, :, 0, :], v2[:, :, 1, :], ALU.add).then_inc(vsum_done, 1)

        @block.tensor
        def _(pe):
            with pe.Fori(0, PAIRS) as j, pe.Fori(0, NB) as b:
                it = j * NB + b
                pe.wait_ge(w_loaded, j * 48 + 48)
                pe.wait_ge(xT_loaded, it * 16 + 16)
                for w in range(4):
                    for c in range(KD):
                        mm = pe.matmul(ps[:, w, :], wqk[:, c, w, :], xT[:, c, :], start=(c == 0), stop=(c == KD - 1))
                    mm.then_inc(qk_psum, 1)

                def values(h):
                    for t in range(TT):
                        if h or t >= 2:
                            pe.wait_ge(vg_done, it * 2 * TT + h * TT + t - 1)
                        for c in range(KD):
                            mm = pe.matmul(ps[:, 4 + t % 2, :], xT[:, c, t * P:(t + 1) * P], wv[:, h, c, :],
                                           start=(c == 0), stop=(c == KD - 1))
                        mm.then_inc(v_psum, 1)

                def scores(h):
                    if h == 0:
                        pe.wait_ge(qk_done, CREDIT + it * 2 + 2)
                    for t in range(TT):
                        if h:
                            pe.wait_ge(exp_done, it * 2 * TT + t + 1)
                        pe.matmul(ps[:, t, :], q[h * HP:(h + 1) * HP, t * P:(t + 1) * P], k[h * HP:(h + 1) * HP, :],
                                  start=True, stop=True).then_inc(s_psum, 1)

                def turn_probabilities(h):
                    pe.wait_ge(exp_done, it * 2 * TT + h * TT + TT)
                    for c in range(TT):
                        if c < 2:
                            if h == 0:
                                pe.wait_ge(vg_done, it * 2 * TT + 2 * TT)
                            else:
                                pe.wait_ge(pT_done, it * 2 * TT + h * TT + c - 1)
                        else:
                            pe.wait_ge(pT_done, it * 2 * TT + h * TT + c - 1)
                        for t in range(TT):
                            mm = pe.transpose(ps[:, 4 + c % 2, t * P:(t + 1) * P], prob[h][:, t, c * P:(c + 1) * P], ident[:, :])
                        mm.then_inc(pT_psum, 1)

                def attend(h):
                    pe.wait_ge(vsum_done, CREDIT + it * 6 + h * 3 + 3)
                    pe.wait_ge(pT_done, it * 2 * TT + h * TT + TT)
                    if h == 0:
                        pe.wait_ge(acc_done, CREDIT + it * 2)
                    for t in range(TT):
                        for c in range(TT):
                            mm = pe.matmul(ps[:, 6 - 6 * h, t * HP:(t + 1) * HP], probT[h][:, c, t * P:(t + 1) * P],
                                           v[:, h, c, :], start=(c == 0), stop=(c == TT - 1))
                    mm.then_inc(o_psum, 1)

                def turn_outputs(h):
                    pe.wait_ge(og_done, it * 2 + h + 1)
                    for e in range(EP):
                        if h == 0 and e < 2:
                            pe.wait_ge(pT_done, it * 2 * TT + 2 * TT)
                        else:
                            pe.wait_ge(oT_done, it * 2 * EP + h * EP + e - 1)
                        for t in range(TT):
                            mm = pe.transpose(ps[:, 4 + e % 2, t * P:(t + 1) * P], og[h][:, t, e * P:(e + 1) * P], ident[:, :])
                        mm.then_inc(oT_psum, 1)

                def project(h, c):
                    for e in range(EP):
                        pe.wait_ge(oT_done, it * 2 * EP + h * EP + e + 1)
                        mm = pe.matmul(ps[:, 7 - c, :], wo[:, h, e, c * P:(c + 1) * P], ogT[h][:, e, :],
                                       start=(h == 0 and e == 0), stop=(h == 1 and e == EP - 1))
                    if h == 1:
                        mm.then_inc(out_psum, 1)

                values(0)
                scores(0)
                values(1)
                scores(1)
                turn_probabilities(0)
                attend(0)
                turn_probabilities(1)
                attend(1)
                turn_outputs(0)
                pe.wait_ge(acc_done, CREDIT + it * 2)
                project(0, 0)
                turn_outputs(1)
                project(1, 0)
                project(0, 1)
                project(1, 1)

        @block.scalar
        def _(act):
            with act.Fori(0, PAIRS) as j, act.Fori(0, NB) as b:
                it = j * NB + b

                def exps(h):
                    for t in range(TT):
                        act.wait_ge(max_done, it * 2 * TT + h * TT + t + 1)
                        act.activation(prob[h][:, t, :], ps[:, t, :], ACT.Exp, bias=negmax[:, h, t:t + 1],
                                       accum_out=total[:, h, t:t + 1]).then_inc(exp_done, 1)

                def keep(h, psum, done, dst):
                    for c in range(TT):
                        act.wait_ge(psum, it * 2 * TT + h * TT + c + 1)
                        act.activation(dst[h][:, c, :], ps[:, 4 + c % 2, :], ACT.Copy).then_inc(done, 1)

                exps(0)
                keep(0, pT_psum, pT_done, probT)
                exps(1)
                keep(1, pT_psum, pT_done, probT)
                keep(0, oT_psum, oT_done, ogT)
                keep(1, oT_psum, oT_done, ogT)

        @block.vector
        def _(dve):
            dve.wait_ge(tables_loaded, 64)
            dve.wait_ge(gates_loaded, 16)
            dve.wait_ge(acc_loaded, 16)
            with dve.Fori(0, PAIRS) as j, dve.Fori(0, NB) as b:
                it = j * NB + b
                for w, table in enumerate((cos_q, sin_q, cos_k, sin_k)):
                    dve.wait_ge(qk_psum, it * 4 + w + 1)
                    if w == 0:
                        dve.wait_ge(qk_done, CREDIT + it * 2)
                    dve.tensor_tensor(rot[:, w, :], ps[:, w, :], table[:, :], ALU.mult).then_inc(rot_done, 1)

                def gate_values(h):
                    dve.wait_ge(vsum_done, CREDIT + it * 6 + h * 3)
                    for t in range(TT):
                        dve.wait_ge(v_psum, CREDIT + it * 2 * TT + h * TT + t + 1)
                        dve.tensor_tensor(vg[:, t, :, :], ps[:, 4 + t % 2, :].rearrange("p (e n) -> p e n", e=E),
                                          gates[:, bass.ds(b * TT + t, 1), bass.ds(j * 2 * E + h * E, E)].rearrange("p a e -> p (a e)")
                                          .unsqueeze(2).to_broadcast([P, E, HP]), ALU.mult).then_inc(vg_done, 1)

                def maxima(h):
                    for t in range(TT):
                        dve.wait_ge(s_psum, CREDIT + it * 2 * TT + h * TT + t + 1)
                        dve.tensor_reduce(negmax[:, h, t:t + 1], ps[:, t, :], AX.X, ALU.max, negate=True).then_inc(max_done, 1)

                def gate_outputs(h):
                    at = it * 4 + h * 2
                    dve.wait_ge(exp_done, it * 2 * TT + h * TT + TT)
                    dve.reciprocal(share[:, h, :], total[:, h, :]).then_inc(share_step, 1)
                    dve.wait_ge(share_step, at + 1)
                    dve.tensor_tensor(og_gate[:, h, :, :], gates[:, bass.ds(b * TT, TT), bass.ds(j * 2 * E + h * E + H * E, E)],
                                      share[:, h, :].unsqueeze(2).to_broadcast([P, TT, E]), ALU.mult).then_inc(share_step, 1)
                    dve.wait_ge(share_step, at + 2)
                    dve.wait_ge(o_psum, CREDIT + it * 2 + h + 1)
                    dve.tensor_tensor(og[h][:, :, :].rearrange("p t (e n) -> p t e n", e=E),
                                      ps[:, 6 - 6 * h, 0:TT * HP].rearrange("p (t n) -> p t n", t=TT).unsqueeze(2).to_broadcast([P, TT, E, HP]),
                                      og_gate[:, h, :, :].unsqueeze(3).to_broadcast([P, TT, E, HP]), ALU.mult).then_inc(og_done, 1)

                gate_values(0)
                maxima(0)
                gate_values(1)
                maxima(1)
                gate_outputs(0)
                gate_outputs(1)
                for c in range(KD):
                    dve.wait_ge(out_psum, CREDIT + it * 2 + c + 1)
                    dve.tensor_tensor(acc[:, bass.ds(b, 1), c, :], acc[:, bass.ds(b, 1), c, :], ps[:, 7 - c, :].unsqueeze(1),
                                      ALU.add).then_inc(acc_done, 1)


def stage_c(nc, d, const, acc):
    with ExitStack() as ctx:
        def sb(name, shape):
            return ctx.enter_context(nc.sbuf_tensor(name, shape, F32))

        def sem(name):
            return ctx.enter_context(nc.semaphore(name))

        ps = ctx.enter_context(nc.psum_tensor("ps_c", [P, 8, S], F32))
        ident = const["ident"]
        w1, w2 = sb("w1", [P, KD, F]), sb("w2", [P, FB, D])
        b1, b2 = sb("b1", [P, FB]), sb("b2", [P, D])
        g1, h1, g2, h2 = (sb(n, [P, D]) for n in ("g1", "h1", "g2", "h2"))
        eps = sb("eps_c", [P, 1])
        accT = sb("accT", [P, KD, S])
        a, an = sb("a", [P, TT, D]), sb("an", [P, TT, D])
        ab = sb("ab", [P, TT, D])
        aT = sb("aT", [P, KD, S])
        hT = sb("hT", [P, FB, S])
        f, fn = sb("f", [P, TT, D]), sb("fn", [P, TT, D])
        x1 = sb("x1_c", [P, TT, D])
        o, y = sb("o", [P, TT, D]), sb("y", [P, TT, D])
        ln1, ln2, ln3 = (Norm(ctx, nc, n, eps[:, 0:1]) for n in ("ln_1", "ln_2", "ln_3"))
        consts = dict(w1=w1, w2=w2, b1=b1, b2=b2, g1=g1, h1=h1, g2=g2, h2=h2)
        ffn_loaded, fill = sem("ffn_loaded"), sem("fill_c")
        accT_done, acc_psum, aff1_done, a_done = sem("accT_done"), sem("acc_psum"), sem("aff1_done"), sem("a_rows")
        ab_done, aT_psum, aT_done = sem("ab_done"), sem("aT_psum"), sem("aT_done")
        h_psum, h_done, f_psum, f_done = sem("h_psum"), sem("h_done"), sem("f_psum"), sem("f_done")
        aff2_done, o_done, x1_loaded, y_done, y_stored = sem("aff2_done"), sem("o_done"), sem("x1_loaded"), sem("y_done"), sem("y_stored")
        block = ctx.enter_context(nc.Block())

        def half(bank, t):
            return ps[:, bank + t // 2, (t % 2) * D:(t % 2 + 1) * D]

        def rows(v):
            return v[:, :].unsqueeze(1).to_broadcast([P, TT, D])

        @block.sync
        def _(sp):
            for s in (y_done, y_stored, acc_psum):
                sp.sem_inc(s, CREDIT)
            for n, t in consts.items():
                sp.dma_start(t[:], d[n].partition_broadcast(P) if n in ("b2", "g1", "h1", "g2", "h2") else d[n]).then_inc(ffn_loaded, 16)
            with sp.Fori(0, NB) as i:
                sp.wait_ge(y_done, CREDIT + i)
                sp.dma_start(x1[:, :, :].unsqueeze(1), d["x1"][bass.ds(i, 1)].rearrange("b (t p) c -> p b t c", p=P)).then_inc(x1_loaded, 16)
                sp.wait_ge(y_done, CREDIT + i + 1)
                sp.dma_start(d["out"][bass.ds(i, 1)].rearrange("b (t p) c -> p b t c", p=P), y[:, :, :].unsqueeze(1)).then_inc(y_stored, 16)
            sp.wait_ge(y_stored, CREDIT + 16 * NB)

        @block.gpsimd
        def _(pool):
            pool.memset(eps[:, :], EPS).then_inc(fill, 1)
            pool.wait_ge(ffn_loaded, 16 * len(consts))
            with pool.Fori(0, NB) as i:
                pool.wait_ge(acc_psum, CREDIT + i)
                pool.tensor_copy(accT[:, :, :].unsqueeze(1), acc[:, bass.ds(i, 1)]).then_inc(accT_done, 1)
                pool.wait_ge(ln1.out_done, i * TT + TT)
                pool.tensor_tensor(an[:, :, :], an[:, :, :], rows(g1), ALU.mult).then_inc(aff1_done, 1)
                pool.wait_ge(aff1_done, i + 1)
                pool.tensor_tensor(a[:, :, :], an[:, :, :], rows(h1), ALU.add).then_inc(a_done, 1)
                pool.wait_ge(a_done, i + 1)
                pool.tensor_tensor(ab[:, :, :], a[:, :, :], rows(b2), ALU.add).then_inc(ab_done, 1)
                pool.wait_ge(ln2.out_done, i * TT + TT)
                pool.tensor_tensor(fn[:, :, :], fn[:, :, :], rows(g2), ALU.mult).then_inc(aff2_done, 1)
                pool.wait_ge(aff2_done, i + 1)
                pool.tensor_tensor(o[:, :, :], fn[:, :, :], rows(h2), ALU.add).then_inc(o_done, 1)
                pool.wait_ge(ln3.out_done, i * TT + TT)
                pool.wait_ge(x1_loaded, i * 16 + 16)
                pool.wait_ge(y_stored, CREDIT + i * 16)
                pool.tensor_tensor(y[:, :, :], fn[:, :, :], x1[:, :, :], ALU.add).then_inc(y_done, 1)

        @block.tensor
        def _(pe):
            pe.wait_ge(ffn_loaded, 16 * len(consts))
            with pe.Fori(0, NB) as i:
                pe.wait_ge(accT_done, i + 1)
                for t in range(TT):
                    for k in range(KD):
                        mm = pe.transpose(ps[:, t // 2, (t % 2) * D + k * P:(t % 2) * D + (k + 1) * P], accT[:, k, t * P:(t + 1) * P], ident[:, :])
                mm.then_inc(acc_psum, 1)
                pe.wait_ge(a_done, i + 1)
                for k in range(KD):
                    for t in range(TT):
                        mm = pe.transpose(ps[:, 2 + k, t * P:(t + 1) * P], a[:, t, k * P:(k + 1) * P], ident[:, :])
                mm.then_inc(aT_psum, 1)
                pe.wait_ge(aT_done, i + 1)
                for m in range(FB):
                    if m >= 4:
                        pe.wait_ge(h_done, i * FB + m - 3)
                    for k in range(KD):
                        mm = pe.matmul(ps[:, 4 + m % 4, :], w1[:, k, m * P:(m + 1) * P], aT[:, k, :], start=(k == 0), stop=(k == KD - 1))
                    mm.then_inc(h_psum, 1)
                pe.wait_ge(h_done, i * FB + FB)
                for t in range(TT):
                    for m in range(FB):
                        mm = pe.matmul(half(0, t), hT[:, m, t * P:(t + 1) * P], w2[:, m, :], start=(m == 0), stop=(m == FB - 1))
                mm.then_inc(f_psum, 1)

        @block.scalar
        def _(act):
            act.wait_ge(fill, 1)
            act.wait_ge(ffn_loaded, 16 * len(consts))
            with act.Fori(0, NB) as i:
                ln1.first_guess(act, i)
                act.wait_ge(aT_psum, i + 1)
                act.activation(aT[:, :, :], ps[:, 2:4, :], ACT.Copy).then_inc(aT_done, 1)
                for m in range(FB):
                    act.wait_ge(h_psum, i * FB + m + 1)
                    act.activation(hT[:, m, :], ps[:, 4 + m % 4, :], ACT.Relu, bias=b1[:, m:m + 1]).then_inc(h_done, 1)
                ln2.first_guess(act, i)
                ln3.first_guess(act, i)

        @block.vector
        def _(dve):
            with dve.Fori(0, NB) as i:
                dve.wait_ge(acc_psum, CREDIT + i + 1)
                s1 = lambda t: half(0, t)
                ln1.statistics(dve, i, s1)
                ln1.newton(dve, i)
                ln1.normalise(dve, s1, lambda t: an[:, t, :])
                dve.wait_ge(f_psum, i + 1)
                dve.wait_ge(ab_done, i + 1)
                dve.tensor_tensor(f[:, :, :], ps[:, 0:2, :].rearrange("p a (h n) -> p (a h) n", h=2), ab[:, :, :], ALU.add).then_inc(f_done, 1)
                dve.wait_ge(f_done, i + 1)
                s2 = lambda t: f[:, t, :]
                ln2.statistics(dve, i, s2)
                ln2.newton(dve, i)
                ln2.normalise(dve, s2, lambda t: fn[:, t, :])
                dve.wait_ge(o_done, i + 1)
                s3 = lambda t: o[:, t, :]
                ln3.statistics(dve, i, s3)
                ln3.newton(dve, i)
                ln3.normalise(dve, s3, lambda t: fn[:, t, :])


def layout(inputs):
    g = {n: np.asarray(v) for n, v in inputs.items()}

    def rows(w, k):
        return np.ascontiguousarray(w.reshape(k, P, -1).transpose(1, 0, 2))

    def cols(v):
        return np.ascontiguousarray(v.reshape(-1, P).T)

    a = {n[len("L0_attn_"):]: v for n, v in g.items() if n.startswith("L0_attn_")}
    f = {n[len("L0_ffn_"):]: v for n, v in g.items() if n.startswith("L0_ffn_")}
    out = {"x": a["x"]}
    out["w_in"] = rows(a["in_proj_w"].T, KD)
    out["w_xp"] = rows(a["x_proj_w"].T, CB)
    w_dt = np.zeros((XP + 1, DI), np.float32)
    w_dt[0], w_dt[XP] = a["dt_proj_w"][:, 0], a["dt_proj_b"]
    out["w_dt"] = w_dt
    out["w_out"] = rows(a["out_proj_w"].T, CB)
    out["conv_w"] = rows(a["conv_w"][:, 0, :], CB)
    out["conv_b"], out["d_skip"] = cols(a["conv_b"]), cols(a["D"])
    out["a_log"] = rows(a["A_log"], CB).reshape(P, CB * NS)
    out["first"] = np.tile(np.arange(E, 0, -1, dtype=np.float32), (P, 1))
    out["ident"] = np.eye(P, dtype=np.float32)
    sel = np.concatenate([f["Wsel_v"].reshape(H * E, D), f["Wsel_o"].reshape(H * E, D)])
    out["w_sel"] = rows(sel.T, KD)

    half = NROT // 2
    swap = np.concatenate([np.arange(half, NROT), np.arange(half), np.arange(NROT, HP)])
    wqk = np.stack([w[..., c] for w in (f["Wq"], f["Wk"]) for c in (np.arange(HP), swap)])
    wqk = wqk.reshape(4, PAIRS, 2, KD, P, HP).transpose(1, 4, 3, 0, 2, 5)
    out["wqk"] = np.ascontiguousarray(wqk).reshape(PAIRS, P, KD, 4, P)
    wv = f["Wv"].reshape(PAIRS, 2, E, KD, P, HP).transpose(0, 4, 1, 3, 2, 5)
    out["wv"] = np.ascontiguousarray(wv).reshape(PAIRS, P, 2, KD, E * HP)
    wo = f["Wo"].reshape(PAIRS, 2, EP, 2 * HP, D).transpose(0, 3, 1, 2, 4)
    out["wo"] = np.ascontiguousarray(wo)
    inv = np.float32(BASE) ** (-np.arange(half, dtype=np.float32) / np.float32(half))
    ang = np.arange(S, dtype=np.float32)[:, None] * inv[None, :]
    cos, sin = np.cos(ang).T.astype(np.float32), np.sin(ang).T.astype(np.float32)
    flat = np.ones((HP - NROT, S), np.float32)
    c = np.tile(np.concatenate([cos, cos, flat]), (2, 1))
    s = np.tile(np.concatenate([-sin, sin, 0 * flat]), (2, 1))
    scale = np.float32(HP ** -0.5)
    out["cos_k"], out["sin_k"], out["cos_q"], out["sin_q"] = c, s, c * scale, s * scale

    out["w1"], out["w2"] = rows(f["W1"], KD), rows(f["W2"], FB)
    out["b1"], out["b2"] = cols(f["b1"]), f["b2"]
    out["g1"], out["h1"], out["g2"], out["h2"] = f["ln1_g"], f["ln1_b"], f["ln2_g"], f["ln2_b"]
    return {n: np.ascontiguousarray(v) for n, v in out.items()}


def program(nc, d):
    d["xT"] = nc.dram_tensor("xT_scratch", (NB, P, KD, S), F32, kind="Internal").ap()
    d["x1"] = nc.dram_tensor("x1_scratch", (NB, S, D), F32, kind="Internal").ap()
    d["gates"] = nc.dram_tensor("gates_scratch", (NB, P, TT * G), F32, kind="Internal").ap()
    with nc.sbuf_tensor("ident", [P, P], F32) as ident:
        const = {"ident": ident}
        stage_a(nc, d, const)
        with nc.sbuf_tensor("acc", [P, NB, KD, S], F32) as acc:
            stage_b(nc, d, const, acc)
            stage_c(nc, d, const, acc)


def kernel(**inputs):
    import concourse.bacc as bacc
    from concourse.bass_utils import run_bass_kernel_spmd

    nc = bacc.Bacc("TRN2", target_bir_lowering=False, num_devices=1)
    arrays = {f"in_{n}": v for n, v in layout(inputs).items()}
    d = {n[3:]: nc.dram_tensor(n, v.shape, mybir.dt.from_np(v.dtype), kind="ExternalInput").ap() for n, v in arrays.items()}
    d["out"] = nc.dram_tensor("out_0", (NB, S, D), F32, kind="ExternalOutput").ap()
    program(nc, d)
    result = run_bass_kernel_spmd(nc, [arrays], core_ids=[0])
    return result.results[0]["out_0"]
```

```python
from contextlib import ExitStack

import numpy as np

import concourse.bass as bass
from concourse import mybir

F32, F32R = mybir.dt.float32, mybir.dt.float32r
ALU = mybir.AluOpType
ACT = mybir.ActivationFunctionType
AX = mybir.AxisListType

P = 128
NB, S, D = 8, 512, 256
TT = S // P
KD = D // P
DI = 512
CB = DI // P
NS = 16
TAPS = 4
XP = 2 * NS + 1
H, E, HP, F = 16, 8, 64, 1024
PAIRS = H // 2
EP = E // 2
FB = F // P
NROT, BASE = 32, 10000.0
EPS = 1e-5
G = 2 * H * E
GP = G // PAIRS
CREDIT = 1


class Norm:

    def __init__(self, ctx, nc, name, eps):
        sem = lambda what: ctx.enter_context(nc.semaphore(f"{name}_{what}"))
        buf = lambda what, n: ctx.enter_context(nc.sbuf_tensor(f"{name}_{what}b", [P, n], F32))
        self.eps = eps
        self.stats_done, self.combine_done = sem("stats"), sem("combine")
        self.stats_done_avg = sem("avg")
        self.log_done, self.guess_done, self.newton_done = sem("log"), sem("guess"), sem("newton")
        self.out_done = sem("out")
        self.stats = buf("stats", TT * 6)
        self.avg, self.var, self.apart, self.spread = (buf(w, TT) for w in ("avg", "var", "apart", "spread"))
        self.logv, self.guess, self.step, self.rstd = (buf(w, TT) for w in ("log", "guess", "step", "rstd"))

    COMBINE = 5

    def mean(self, t):
        return self.avg[:, t:t + 1]

    def variances(self):
        return self.var[:, :]

    def statistics(self, dve, i, rows):
        for t in range(TT):
            dve.bn_stats(self.stats[:, 6 * t:6 * t + 6], rows(t)).then_inc(self.stats_done, 1)
        _, mean_e, m2_e, _, mean_o, m2_o = (self.stats[:, :].rearrange("p (t w) -> p w t", w=6)[:, w, :] for w in range(6))
        done, at = self.combine_done, i * self.COMBINE
        dve.wait_ge(self.stats_done, i * TT + TT)
        dve.tensor_tensor(self.avg[:, :], mean_e, mean_o, ALU.add).then_inc(done, 1)
        dve.tensor_tensor(self.apart[:, :], mean_e, mean_o, ALU.subtract).then_inc(done, 1)
        dve.tensor_tensor(self.spread[:, :], m2_e, m2_o, ALU.add).then_inc(done, 1)
        dve.wait_ge(done, at + 2)
        dve.scalar_tensor_tensor(self.apart[:, :], self.apart[:, :], D / 4.0, self.apart[:, :],
                                 ALU.mult, ALU.mult).then_inc(done, 1)
        dve.tensor_scalar(self.avg[:, :], self.avg[:, :], 0.5, None, ALU.mult).then_inc(self.stats_done_avg, 1)
        dve.wait_ge(done, at + 4)
        dve.tensor_tensor(self.var[:, :], self.spread[:, :], self.apart[:, :], ALU.add).then_inc(done, 1)

    def first_guess(self, act, i):
        act.wait_ge(self.combine_done, i * self.COMBINE + self.COMBINE)
        act.activation(self.logv[:, :], self.variances(), ACT.Ln, bias=self.eps, scale=1.0 / D).then_inc(self.log_done, 1)
        act.wait_ge(self.log_done, i + 1)
        act.activation(self.guess[:, :], self.logv[:, :], ACT.Exp, scale=-0.5).then_inc(self.guess_done, 1)

    def newton(self, dve, i):
        done, at = self.newton_done, i * 5
        dve.wait_ge(self.guess_done, i + 1)
        dve.tensor_scalar(self.step[:, :], self.variances(), 1.0 / D, EPS, ALU.mult, ALU.add).then_inc(done, 1)
        dve.wait_ge(done, at + 1)
        dve.tensor_tensor(self.step[:, :], self.step[:, :], self.guess[:, :], ALU.mult).then_inc(done, 1)
        dve.wait_ge(done, at + 2)
        dve.tensor_tensor(self.step[:, :], self.step[:, :], self.guess[:, :], ALU.mult).then_inc(done, 1)
        dve.wait_ge(done, at + 3)
        dve.tensor_scalar(self.step[:, :], self.step[:, :], -0.5, 1.5, ALU.mult, ALU.add).then_inc(done, 1)
        dve.wait_ge(done, at + 4)
        dve.tensor_tensor(self.rstd[:, :], self.guess[:, :], self.step[:, :], ALU.mult).then_inc(done, 1)
        dve.wait_ge(self.stats_done_avg, i + 1)
        dve.wait_ge(done, at + 5)

    def normalise(self, dve, rows, out):
        for t in range(TT):
            dve.tensor_scalar(out(t), rows(t), self.mean(t), self.rstd[:, t:t + 1],
                              ALU.subtract, ALU.mult).then_inc(self.out_done, 1)


def stage_a(nc, d, const):
    with ExitStack() as ctx:
        def sb(name, shape, dtype=F32):
            return ctx.enter_context(nc.sbuf_tensor(name, shape, dtype))

        def sem(name):
            return ctx.enter_context(nc.semaphore(name))

        ps = ctx.enter_context(nc.psum_tensor("ps_a", [P, 8, S], F32))
        ident = const["ident"]
        B_BANK, C_BANK, TAIL, HEAD = 4, 5, 6, 7
        w_in = sb("w_in", [P, KD, 2 * DI])
        w_xp = sb("w_xp", [P, CB, XP])
        w_dt = sb("w_dt", [XP + 1, DI])
        w_out = sb("w_out", [P, CB, D])
        w_sel = sb("w_sel", [P, KD, G])
        conv_w = sb("conv_w", [P, CB, TAPS])
        conv_b = sb("conv_b", [P, CB])
        conv_diag = sb("conv_diag", [P, CB * TAPS, P])
        ident_r = sb("ident_r", [P, P], F32R)
        d_skip = sb("d_skip", [P, CB])
        a_log = sb("a_log", [P, CB * NS])
        a_exp = sb("a_exp", [P, CB * NS])
        a_neg = sb("a_neg", [P, CB, NS])
        first = sb("first", [P, E])
        ones = sb("ones", [P, 1])
        eps = sb("eps_a", [P, 1])

        x_in, xn = sb("x_in", [P, TT, D]), sb("xn", [P, TT, D])
        xnT = sb("xnT", [P, KD, S])
        work = sb("work", [P, CB, S])
        zs = sb("zs", [P, CB, S])
        xp = sb("xp", [XP + 1, S])
        xp_high, xp_low = ([sb(f"xp_{part}{n}", [XP, S], F32R) for n in range(2)] for part in ("high", "low"))
        xc, dt, du = ([sb(f"{name}{n}", [P, CB, S]) for n in range(2)] for name in ("xc", "dt", "du"))
        dA, dBx, h = ([sb(f"{name}{n}", [P, CB, S]) for n in range(2)] for name in ("dA", "dBx", "state"))
        x_res, x1, mo = (sb(name, [P, TT, D]) for name in ("x_res", "x1", "mo"))
        x2 = sb("x2", [P, TT, D])
        x2T = sb("x2T", [P, KD, S])
        sg, left = sb("sg", [P, TT * G]), sb("left", [P, TT * G])
        pick = mo[:, :, :].rearrange("p t c -> p (t c)")
        rank = x2[:, :, :].rearrange("p t c -> p (t c)")
        best = sb("best", [P, TT * G // E])
        gate = sb("gate", [P, PAIRS, TT, GP])

        def groups(v):
            return v.rearrange("p (g e) -> p g e", e=E)

        def by_pair(v, t):
            return v[:, t * G:(t + 1) * G].rearrange("p (j c) -> p j c", j=PAIRS)

        best_e = best[:, :].unsqueeze(2).to_broadcast([P, TT * G // E, E])
        first_g = first[:, :].unsqueeze(1).to_broadcast([P, TT * G // E, E])

        ln_x, ln_m, ln_a = (Norm(ctx, nc, n, eps[:, 0:1]) for n in ("ln_x", "ln_m", "ln_a"))
        const_tiles = dict(w_in=w_in, w_xp=w_xp, w_dt=w_dt, w_out=w_out, w_sel=w_sel, conv_w=conv_w,
                           conv_b=conv_b, d_skip=d_skip, a_log=a_log, first=first)
        consts_loaded = sem("consts_loaded")
        all_consts = 16 * (len(const_tiles) + 1)
        x_loaded, x_res_loaded = sem("x_loaded"), sem("x_res_loaded")
        fills, all_fills = sem("fills"), 5
        a_exp_done, a_done, diag_done, ident_r_done = sem("a_exp_done"), sem("a_done"), sem("diag_done"), sem("ident_r_done")
        xnT_psum, xnT_done, z_psum, zs_done = sem("xnT_psum"), sem("xnT_done"), sem("z_psum"), sem("zs_done")
        xs_psum, xs_done, conv_psum, xc_done = sem("xs_psum"), sem("xs_done"), sem("conv_psum"), sem("xc_done")
        xp_psum, xp_done, xp_low_done, dt_psum = sem("xp_psum"), sem("xp_done"), sem("xp_low_done"), sem("dt_psum")
        soft_done, relu_done, dt_done, du_done = sem("soft_done"), sem("relu_done"), sem("dt_done"), sem("du_done")
        b_psum, c_psum = sem("b_psum"), sem("c_psum")
        dA_done, dBx_done, scan_done, hc_done = sem("dA_done"), sem("dBx_done"), sem("scan_done"), sem("hc_done")
        y_psum, skip_done, yz_done = sem("y_psum"), sem("skip_done"), sem("yz_done")
        mo_psum, mo_done, x1_done = sem("mo_psum"), sem("mo_done"), sem("x1_done")
        x2T_psum, x2T_done = sem("x2T_psum"), sem("x2T_done")
        sel_psum, sg_done, top_step, gate_done = sem("sel_psum"), sem("sg_done"), sem("top_step"), sem("gate_done")
        x1_stored, x2T_stored, gate_stored = sem("x1_stored"), sem("x2T_stored"), sem("gate_stored")
        TOP = 12
        SOFT = CB + 2

        def turns(eng, turn):
            turn(0, 0, False, True)
            with eng.Fori(0, NB // 2 - 1) as pair:
                turn(pair * 2 + 1, 1, True, True)
                turn(pair * 2 + 2, 0, True, True)
            turn(NB - 1, 1, True, False)

        block = ctx.enter_context(nc.Block())

        @block.sync
        def _(sp):
            for s in (x1_done, x1_stored, x2T_stored, gate_stored, gate_done, sg_done):
                sp.sem_inc(s, CREDIT)

            def tiles(name, i):
                return d[name][bass.ds(i, 1)].rearrange("b (t p) c -> p b t c", p=P)

            def load_x(i):
                sp.dma_start(x_in[:, :, :].unsqueeze(1), tiles("x", i)).then_inc(x_loaded, 16)

            def tail(c):
                sp.wait_ge(x1_done, CREDIT + c)
                sp.dma_start(x_res[:, :, :].unsqueeze(1), tiles("x", c)).then_inc(x_res_loaded, 16)
                sp.wait_ge(x1_done, CREDIT + c + 1)
                sp.dma_start(tiles("x1", c), x1[:, :, :].unsqueeze(1)).then_inc(x1_stored, 16)
                sp.wait_ge(x2T_done, c * KD + KD)
                sp.dma_start(d["xT"][bass.ds(c, 1)].rearrange("b p k s -> p b k s"), x2T[:, :, :].unsqueeze(1)).then_inc(x2T_stored, 16)
                sp.wait_ge(gate_done, CREDIT + c * TT + TT)
                sp.dma_start(d["gates"][:, :, bass.ds(c, 1)].rearrange("j p b t c -> p b j (t c)"),
                             gate[:, :, :, :].rearrange("p j t c -> p j (t c)").unsqueeze(1)).then_inc(gate_stored, 16)

            def turn(i, par, has_tail, has_head):
                if has_head:
                    sp.wait_ge(ln_x.out_done, i * TT + TT)
                    load_x(i + 1)
                if has_tail:
                    tail(i - 1)

            load_x(0)
            sp.dma_start(ident[:, :], d["ident"]).then_inc(consts_loaded, 16)
            for n, t in const_tiles.items():
                sp.dma_start(t[:], d[n]).then_inc(consts_loaded, 16)
            turns(sp, turn)
            tail(NB - 1)
            sp.wait_ge(x1_stored, CREDIT + 16 * NB)
            sp.wait_ge(x2T_stored, CREDIT + 16 * NB)
            sp.wait_ge(gate_stored, CREDIT + 16 * NB)

        @block.gpsimd
        def _(pool):
            pool.memset(eps[:, :], EPS).then_inc(fills, 1)
            pool.memset(ones[:, :], 1.0).then_inc(fills, 1)
            pool.memset(xp[:, :], 1.0).then_inc(fills, 1)
            for n in range(2):
                pool.memset(dA[n][:, :, :], 0.0).then_inc(fills, 1)

            def low_xp(b, par):
                pool.wait_ge(xp_done, b * 2 + 2)
                pool.tensor_tensor(xp_low[par][:, :], xp[0:XP, :], xp_high[par][:, :].bitcast(F32), ALU.subtract).then_inc(xp_low_done, 1)

            def step_sizes(b, par):
                pool.wait_ge(relu_done, b * CB + CB)
                pool.wait_ge(soft_done, b * SOFT + SOFT)
                pool.tensor_tensor(dt[par][:, :, :], dt[par][:, :, :], work[:, :, :], ALU.add).then_inc(dt_done, 1)
                pool.wait_ge(dt_done, b + 1)
                pool.tensor_tensor(du[par][:, :, :], dt[par][:, :, :], xc[par][:, :, :], ALU.mult).then_inc(du_done, 1)

            def tail(c):
                pool.wait_ge(skip_done, c * CB + CB)
                pool.wait_ge(zs_done, c * CB + CB)
                pool.tensor_tensor(work[:, :, :], work[:, :, :], zs[:, :, :], ALU.mult).then_inc(yz_done, 1)
                pool.wait_ge(ln_m.out_done, c * TT + TT)
                pool.wait_ge(x_res_loaded, c * 16 + 16)
                pool.wait_ge(x1_stored, CREDIT + c * 16)
                pool.tensor_tensor(x1[:, :, :], x_res[:, :, :], mo[:, :, :], ALU.add).then_inc(x1_done, 1)

            def turn(i, par, has_tail, has_head):
                if has_tail:
                    tail(i - 1)
                if has_head:
                    low_xp(i + 1, 1 - par)
                    step_sizes(i + 1, 1 - par)

            low_xp(0, 0)
            step_sizes(0, 0)
            turns(pool, turn)
            tail(NB - 1)

        @block.tensor
        def _(pe):
            def turn_input(b, first):
                pe.wait_ge(ln_x.out_done, b * TT + TT)
                for k in range(KD):
                    if k:
                        pe.wait_ge(xnT_done, b * KD + k)
                    elif not first:
                        pe.wait_ge(zs_done, b * CB)
                    for t in range(TT):
                        mm = pe.transpose(ps[:, HEAD, t * P:(t + 1) * P], xn[:, t, k * P:(k + 1) * P], ident[:, :])
                    mm.then_inc(xnT_psum, 1)

            def project_block(block_of, done):
                for k in range(KD):
                    mm = pe.matmul(ps[:, HEAD, :], w_in[:, k, block_of * P:(block_of + 1) * P], xnT[:, k, :],
                                   start=(k == 0), stop=(k == KD - 1))
                mm.then_inc(done, 1)

            def project_x(b, m):
                if m:
                    pe.wait_ge(xs_done, b * CB + m)
                else:
                    pe.wait_ge(xnT_done, b * KD + KD)
                project_block(m, xs_psum)

            def project_z(i, m):
                if m:
                    pe.wait_ge(zs_done, i * CB + m)
                else:
                    pe.wait_ge(relu_done, i * CB + CB)
                project_block(CB + m, z_psum)

            def convolve(b, m):
                if m:
                    pe.wait_ge(xc_done, b * CB + m)
                else:
                    pe.wait_ge(xs_done, b * CB + CB)
                for far in range(TAPS):
                    mm = pe.matmul(ps[:, HEAD, far:S], conv_diag[:, m * TAPS + TAPS - 1 - far, :], work[:, m, 0:S - far],
                                   start=(far == 0), stop=(far == TAPS - 1))
                mm.then_inc(conv_psum, 1)

            def project_xp(b, par):
                pe.wait_ge(xc_done, b * CB + CB)
                for k in range(CB):
                    mm = pe.matmul(ps[0:XP, HEAD, :], w_xp[:, k, :], xc[par][:, k, :], start=(k == 0), stop=(k == CB - 1))
                mm.then_inc(xp_psum, 1)

            def project_dt(b, m):
                if m:
                    pe.wait_ge(relu_done, b * CB + m)
                else:
                    pe.wait_ge(xp_done, b * 2 + 2)
                pe.matmul(ps[:, HEAD, :], w_dt[:, m * P:(m + 1) * P], xp[:, :], start=True, stop=True).then_inc(dt_psum, 1)

            def spread(bank, r, par, done):
                one = ident_r[0:XP, r:r + 1].to_broadcast([XP, P])
                pe.matmul(ps[:, bank, :], one, xp_high[par][:, :], start=True, stop=False)
                pe.matmul(ps[:, bank, :], one, xp_low[par][:, :], start=False, stop=True).then_inc(done, 1)

            def spread_b(b, n, par, first=False):
                if n == 0:
                    pe.wait_ge(xp_low_done, b + 1)
                if not first:
                    pe.wait_ge(dBx_done, b * NS + n)
                spread(B_BANK, 1 + n, par, b_psum)

            def spread_c(b, n, par, first=False):
                if not first:
                    pe.wait_ge(hc_done, b * NS + n)
                spread(C_BANK, 1 + NS + n, par, c_psum)

            def sum_y(i, n, par, has_tail):
                pe.wait_ge(hc_done, i * NS + n + 1)
                if n == 0 and has_tail:
                    pe.wait_ge(skip_done, i * CB)
                for m in range(CB):
                    mm = pe.matmul(ps[:, m, :], ident[:, :], h[n % 2][:, m, :], start=(n == 0), stop=(n == NS - 1))
                mm.then_inc(y_psum, 1)

            def project_out(c, half):
                if half:
                    pe.wait_ge(mo_done, c * 2 + 1)
                else:
                    pe.wait_ge(yz_done, c + 1)
                    pe.wait_ge(sg_done, CREDIT + c * 2)
                for t in range(2):
                    at = slice((2 * half + t) * P, (2 * half + t + 1) * P)
                    for k in range(CB):
                        mm = pe.matmul(ps[:, TAIL, t * D:(t + 1) * D], work[:, k, at], w_out[:, k, :],
                                       start=(k == 0), stop=(k == CB - 1))
                mm.then_inc(mo_psum, 1)

            def turn_x2(c):
                pe.wait_ge(ln_a.out_done, c * TT + TT)
                for k in range(KD):
                    if k:
                        pe.wait_ge(x2T_done, c * KD + k)
                    else:
                        pe.wait_ge(mo_done, c * 2 + 2)
                    for t in range(TT):
                        mm = pe.transpose(ps[:, TAIL, t * P:(t + 1) * P], x2[:, t, k * P:(k + 1) * P], ident[:, :])
                    mm.then_inc(x2T_psum, 1)

            def select(c, half):
                pe.wait_ge(x2T_done, c * KD + KD)
                if half:
                    pe.wait_ge(sg_done, CREDIT + c * 2 + 1)
                for t in range(2):
                    at = slice((2 * half + t) * P, (2 * half + t + 1) * P)
                    for k in range(KD):
                        mm = pe.matmul(ps[:, TAIL, t * G:(t + 1) * G], x2T[:, k, at], w_sel[:, k, :], start=(k == 0), stop=(k == KD - 1))
                mm.then_inc(sel_psum, 1)

            def turn(i, par, has_tail, has_head):
                b, c = i + 1, i - 1
                for n in range(NS):
                    if n + 2 < NS:
                        spread_b(i, n + 2, par)
                    elif has_head:
                        spread_b(b, n + 2 - NS, 1 - par)
                    if n + 1 < NS:
                        spread_c(i, n + 1, par)
                    elif has_head:
                        spread_c(b, 0, 1 - par)
                    sum_y(i, n, par, has_tail)
                    if n == 1:
                        project_z(i, 0)
                        project_z(i, 1)
                    elif n == 2:
                        project_z(i, 2)
                        project_z(i, 3)
                    if has_tail:
                        if n in (3, 4):
                            project_out(c, n - 3)
                        elif n == 8:
                            turn_x2(c)
                        elif n in (9, 10):
                            select(c, n - 9)
                    if has_head:
                        if n == 3:
                            turn_input(b, False)
                        elif n == 4:
                            project_x(b, 0)
                        elif n == 5:
                            project_x(b, 1)
                            project_x(b, 2)
                        elif n == 6:
                            project_x(b, 3)
                            convolve(b, 0)
                        elif n in (7, 8, 9):
                            convolve(b, n - 6)
                        elif n == 10:
                            project_xp(b, 1 - par)
                        elif n == 11:
                            for m in range(CB):
                                project_dt(b, m)

            pe.wait_ge(consts_loaded, all_consts)
            pe.wait_ge(fills, all_fills)
            turn_input(0, True)
            for m in range(CB):
                project_x(0, m)
            pe.wait_ge(diag_done, 1)
            for m in range(CB):
                convolve(0, m)
            project_xp(0, 0)
            for m in range(CB):
                project_dt(0, m)
            pe.wait_ge(ident_r_done, 1)
            spread_b(0, 0, 0, first=True)
            spread_c(0, 0, 0, first=True)
            spread_b(0, 1, 0)
            turns(pe, turn)
            project_out(NB - 1, 0)
            project_out(NB - 1, 1)
            turn_x2(NB - 1)
            select(NB - 1, 0)
            select(NB - 1, 1)

        @block.scalar
        def _(act):
            def exps():
                act.preload_act_table_set("natural_log_exp_and_others")

            def keep_input(b):
                for k in range(KD):
                    act.wait_ge(xnT_psum, b * KD + k + 1)
                    act.activation(xnT[:, k, :], ps[:, HEAD, :], ACT.Copy).then_inc(xnT_done, 1)

            def keep_x(b, m):
                act.wait_ge(xs_psum, b * CB + m + 1)
                act.activation(work[:, m, :], ps[:, HEAD, :], ACT.Copy).then_inc(xs_done, 1)

            def silu_z(i, m, has_tail):
                if m == 0 and has_tail:
                    act.wait_ge(yz_done, i)
                act.wait_ge(z_psum, i * CB + m + 1)
                act.activation(zs[:, m, :], ps[:, HEAD, :], ACT.Silu).then_inc(zs_done, 1)

            def silu_x(b, m, par):
                act.wait_ge(conv_psum, b * CB + m + 1)
                act.activation(xc[par][:, m, :], ps[:, HEAD, :], ACT.Silu, bias=conv_b[:, m:m + 1]).then_inc(xc_done, 1)

            def keep_xp(b, par):
                act.wait_ge(xp_psum, b + 1)
                act.activation(xp_high[par][:, :], ps[0:XP, HEAD, :], ACT.Copy).then_inc(xp_done, 1)
                act.activation(xp[0:XP, :], ps[0:XP, HEAD, :], ACT.Copy).then_inc(xp_done, 1)

            def magnitudes(b, m, par):
                act.wait_ge(dt_psum, b * CB + m + 1)
                act.activation(work[:, m, :], ps[:, HEAD, :], ACT.Abs).then_inc(soft_done, 1)
                act.activation(dt[par][:, m, :], ps[:, HEAD, :], ACT.Relu).then_inc(relu_done, 1)

            def softplus_exp(b):
                act.wait_ge(soft_done, b * SOFT + CB)
                act.activation(work[:, :, :], work[:, :, :], ACT.Exp, scale=-1.0).then_inc(soft_done, 1)

            def softplus_ln(b):
                act.wait_ge(soft_done, b * SOFT + CB + 1)
                act.activation(work[:, :, :], work[:, :, :], ACT.Ln, bias=ones[:, 0:1]).then_inc(soft_done, 1)

            def decay(b, n, par, first=False):
                if n == 0:
                    act.wait_ge(dt_done, b + 1)
                if not first:
                    act.wait_ge(scan_done, b * NS + n - 1)
                for m in range(CB):
                    act.activation(dA[n % 2][:, m, 1:S], dt[par][:, m, 1:S], ACT.Exp,
                                   scale=a_neg[:, m, n:n + 1]).then_inc(dA_done, 1)

            def keep_out(c, half):
                if half == 0:
                    act.wait_ge(gate_done, CREDIT + c * TT)
                act.wait_ge(mo_psum, c * 2 + half + 1)
                act.activation(mo[:, 2 * half:2 * half + 2, :].rearrange("p t c -> p (t c)"), ps[:, TAIL, :], ACT.Copy).then_inc(mo_done, 1)

            def keep_x2(c):
                act.wait_ge(x2T_stored, CREDIT + c * 16)
                for k in range(KD):
                    act.wait_ge(x2T_psum, c * KD + k + 1)
                    act.activation(x2T[:, k, :], ps[:, TAIL, :], ACT.Copy).then_inc(x2T_done, 1)

            def sigmoid(c, half):
                act.wait_ge(sel_psum, c * 2 + half + 1)
                act.activation(sg[:, half * S:(half + 1) * S], ps[:, TAIL, :], ACT.Sigmoid).then_inc(sg_done, 1)

            def turn(i, par, has_tail, has_head):
                b, c = i + 1, i - 1
                exps()
                for n in range(NS):
                    if n + 2 < NS:
                        decay(i, n + 2, par)
                    elif has_head:
                        decay(b, n + 2 - NS, 1 - par)
                    if n in (1, 2):
                        silu_z(i, 2 * n - 2, has_tail)
                        silu_z(i, 2 * n - 1, has_tail)
                        exps()
                    if has_tail:
                        if n in (3, 4):
                            keep_out(c, n - 3)
                        elif n == 5:
                            ln_m.first_guess(act, c)
                        elif n == 7:
                            ln_a.first_guess(act, c)
                        elif n == 8:
                            keep_x2(c)
                        elif n in (9, 10):
                            sigmoid(c, n - 9)
                            if n == 10:
                                exps()
                    if has_head:
                        if n == 1:
                            ln_x.first_guess(act, b)
                        elif n == 3:
                            keep_input(b)
                        elif n == 4:
                            keep_x(b, 0)
                        elif n == 5:
                            keep_x(b, 1)
                            keep_x(b, 2)
                        elif n == 6:
                            keep_x(b, 3)
                            silu_x(b, 0, 1 - par)
                            exps()
                        elif n in (7, 8, 9):
                            silu_x(b, n - 6, 1 - par)
                            exps()
                        elif n == 10:
                            keep_xp(b, 1 - par)
                        elif n == 11:
                            for m in range(CB):
                                magnitudes(b, m, 1 - par)
                            softplus_exp(b)
                        elif n == 12:
                            softplus_ln(b)

            act.wait_ge(consts_loaded, all_consts)
            act.wait_ge(fills, all_fills)
            exps()
            act.activation(a_exp[:, :], a_log[:, :], ACT.Exp).then_inc(a_exp_done, 1)
            act.wait_ge(a_exp_done, 1)
            act.mul(a_neg[:, :, :].rearrange("p c n -> p (c n)"), a_exp[:, :], -1.0).then_inc(a_done, 1)
            act.activation(ident_r[:, :], ident[:, :], ACT.Copy).then_inc(ident_r_done, 1)
            act.wait_ge(a_done, 1)
            ln_x.first_guess(act, 0)
            keep_input(0)
            for m in range(CB):
                keep_x(0, m)
            for m in range(CB):
                silu_x(0, m, 0)
            exps()
            keep_xp(0, 0)
            for m in range(CB):
                magnitudes(0, m, 0)
            softplus_exp(0)
            softplus_ln(0)
            decay(0, 0, 0, first=True)
            decay(0, 1, 0, first=True)
            turns(act, turn)
            keep_out(NB - 1, 0)
            keep_out(NB - 1, 1)
            ln_m.first_guess(act, NB - 1)
            ln_a.first_guess(act, NB - 1)
            keep_x2(NB - 1)
            sigmoid(NB - 1, 0)
            sigmoid(NB - 1, 1)

        @block.vector
        def _(dve):
            rows_in, rows_n = (lambda t: x_in[:, t, :]), (lambda t: xn[:, t, :])
            rows_m, rows_1, rows_2 = (lambda t: mo[:, t, :]), (lambda t: x1[:, t, :]), (lambda t: x2[:, t, :])

            def stats_x(b):
                dve.wait_ge(x_loaded, b * 16 + 16)
                ln_x.statistics(dve, b, rows_in)

            def norm_x(b):
                ln_x.newton(dve, b)
                ln_x.normalise(dve, rows_in, rows_n)

            def inputs(b, n, par, first=False):
                if n == 0:
                    dve.wait_ge(du_done, b + 1)
                if not first:
                    dve.wait_ge(scan_done, b * NS + n - 1)
                dve.wait_ge(b_psum, b * NS + n + 1)
                dve.tensor_tensor(dBx[n % 2][:, :, :], du[par][:, :, :],
                                  ps[:, B_BANK, :].unsqueeze(1).to_broadcast([P, CB, S]), ALU.mult).then_inc(dBx_done, 1)

            def scan(i, n, first):
                dve.wait_ge(dA_done, (i * NS + n + 1) * CB)
                dve.wait_ge(dBx_done, i * NS + n + 1)
                if not (first and n < 2):
                    dve.wait_ge(y_psum, i * NS + n - 1)
                dve.tensor_tensor_scan(h[n % 2][:, :, :].rearrange("p c s -> p (c s)"),
                                       dA[n % 2][:, :, :].rearrange("p c s -> p (c s)"),
                                       dBx[n % 2][:, :, :].rearrange("p c s -> p (c s)"),
                                       0.0, ALU.mult, ALU.add).then_inc(scan_done, 1)

            def weigh(i, n):
                dve.wait_ge(scan_done, i * NS + n + 1)
                dve.wait_ge(c_psum, i * NS + n + 1)
                dve.tensor_tensor(h[n % 2][:, :, :], h[n % 2][:, :, :],
                                  ps[:, C_BANK, :].unsqueeze(1).to_broadcast([P, CB, S]), ALU.mult).then_inc(hc_done, 1)

            def skip(c, par):
                dve.wait_ge(y_psum, c * NS + NS)
                for m in range(CB):
                    dve.scalar_tensor_tensor(work[:, m, :], xc[par][:, m, :], d_skip[:, m:m + 1], ps[:, m, :],
                                             ALU.mult, ALU.add).then_inc(skip_done, 1)

            def stats_m(c):
                dve.wait_ge(mo_done, c * 2 + 2)
                ln_m.statistics(dve, c, rows_m)

            def norm_m(c):
                ln_m.newton(dve, c)
                ln_m.normalise(dve, rows_m, rows_m)

            def stats_a(c):
                dve.wait_ge(x1_done, CREDIT + c + 1)
                ln_a.statistics(dve, c, rows_1)

            def norm_a(c):
                ln_a.newton(dve, c)
                ln_a.normalise(dve, rows_1, rows_2)

            def best_of(c, src, k):
                step = c * TOP + k
                if k == 0:
                    dve.wait_ge(sg_done, CREDIT + c * 2 + 2)
                else:
                    dve.wait_ge(top_step, step)
                dve.tensor_reduce(best[:, :], groups(src), AX.X, ALU.max).then_inc(top_step, 1)
                dve.wait_ge(top_step, step + 1)
                dve.tensor_tensor(groups(pick), groups(src), best_e, ALU.is_equal).then_inc(top_step, 1)
                dve.wait_ge(top_step, step + 2)
                dve.tensor_tensor(groups(rank), groups(pick), first_g, ALU.mult).then_inc(top_step, 1)

            def first_of(c, src, k):
                step = c * TOP + k
                dve.wait_ge(top_step, step + 3)
                dve.tensor_reduce(best[:, :], groups(rank), AX.X, ALU.max).then_inc(top_step, 1)
                dve.wait_ge(top_step, step + 4)
                dve.tensor_tensor(groups(pick), groups(rank), best_e, ALU.is_equal).then_inc(top_step, 1)
                dve.wait_ge(top_step, step + 5)
                dve.scalar_tensor_tensor(left[:, :], pick, -2.0, src, ALU.mult, ALU.add).then_inc(top_step, 1)

            def gates(c):
                dve.wait_ge(top_step, c * TOP + TOP)
                dve.wait_ge(gate_stored, CREDIT + c * 16)
                for t in range(TT):
                    dve.scalar_tensor_tensor(gate[:, :, t, :], by_pair(left, t), 0.0, by_pair(sg, t),
                                             ALU.is_lt, ALU.mult).then_inc(gate_done, 1)

            def turn(i, par, has_tail, has_head):
                b, c = i + 1, i - 1
                for n in range(NS):
                    scan(i, n, not has_tail)
                    if n + 1 < NS:
                        inputs(i, n + 1, par, first=not has_tail and n == 0)
                    elif has_head:
                        inputs(b, 0, 1 - par)
                    if n == 0 and has_tail:
                        skip(c, 1 - par)
                    weigh(i, n)
                    if has_tail:
                        if n == 5:
                            stats_m(c)
                        elif n == 6:
                            norm_m(c)
                        elif n == 7:
                            stats_a(c)
                        elif n == 8:
                            norm_a(c)
                        elif n == 12:
                            best_of(c, sg[:, :], 0)
                        elif n == 13:
                            first_of(c, sg[:, :], 0)
                        elif n == 14:
                            best_of(c, left[:, :], 6)
                        elif n == 15:
                            first_of(c, left[:, :], 6)
                            gates(c)
                    if has_head:
                        if n == 1:
                            stats_x(b)
                        elif n == 2:
                            norm_x(b)

            dve.wait_ge(fills, all_fills)
            stats_x(0)
            norm_x(0)
            dve.wait_ge(consts_loaded, all_consts)
            dve.tensor_tensor(conv_diag[:, :, :], ident[:, :].unsqueeze(1).to_broadcast([P, CB * TAPS, P]),
                              conv_w[:, :, :].rearrange("p m r -> p (m r)").unsqueeze(2).to_broadcast([P, CB * TAPS, P]),
                              ALU.mult).then_inc(diag_done, 1)
            inputs(0, 0, 0, first=True)
            turns(dve, turn)
            last = NB - 1
            skip(last, last % 2)
            stats_m(last)
            norm_m(last)
            stats_a(last)
            norm_a(last)
            best_of(last, sg[:, :], 0)
            first_of(last, sg[:, :], 0)
            best_of(last, left[:, :], 6)
            first_of(last, left[:, :], 6)
            gates(last)


def stage_b(nc, d, const, acc):
    with ExitStack() as ctx:
        def sb(name, shape, dtype=F32):
            return ctx.enter_context(nc.sbuf_tensor(name, shape, dtype))

        def parts(name, shape):
            return [sb(f"{name}_{part}", shape, F32R) for part in ("high", "low")]

        def sem(name):
            return ctx.enter_context(nc.semaphore(name))

        ps = ctx.enter_context(nc.psum_tensor("ps_b", [P, 8, S], F32))
        ident = const["ident"]
        gates = sb("gates", [P, NB * TT, GP])
        shapes = dict(wqk=[P, KD, 4, P], wv=[P, 2, KD, E * HP], wo=[P, 2, EP, D])
        w_in = {n: sb(n, s) for n, s in shapes.items()}
        w = {n: parts(n, s) for n, s in shapes.items()}
        wqk, wv, wo = w["wqk"], w["wv"], w["wo"]
        cos_q, sin_q, cos_k, sin_k = (sb(n, [P, S]) for n in ("cos_q", "sin_q", "cos_k", "sin_k"))
        xT_in = sb("xT", [P, KD, S])
        xT = parts("xT", [P, KD, S])
        rot = sb("rot", [P, 4, S])
        qk_full = [sb("q", [P, S]), sb("k", [P, S])]
        q, k = parts("q", [P, S]), parts("k", [P, S])
        vg = sb("vg", [P, TT, E, HP])
        v4 = sb("v4", [P, TT, E // 2, HP])
        v2 = sb("v2", [P, TT, E // 4, HP])
        v = sb("v", [P, 2, TT, HP])
        negmax = sb("negmax", [P, 2, TT])
        total = sb("total", [P, 2, TT])
        share = sb("share", [P, 2, TT])
        og_gate = sb("og_gate", [P, 2, TT, E])
        prob = [sb(f"prob{h}", [P, TT, S]) for h in range(2)]
        probT = [sb(f"probT{h}", [P, TT, S]) for h in range(2)]
        og = prob
        ogT = parts("ogT", [P, EP, S])

        tables_loaded, gates_loaded, acc_loaded = sem("tables_loaded"), sem("gates_loaded"), sem("acc_loaded")
        w_loaded, w_high, w_low = ({n: sem(f"{n}_{what}") for n in shapes} for what in ("loaded", "high_done", "low_done"))
        xT_loaded, xT_high, xT_low = sem("xT_loaded"), sem("xT_high_done"), sem("xT_low_done")
        qk_psum, rot_done, qk_done = sem("qk_psum"), sem("rot_done"), sem("qk_done")
        qk_high, qk_low = sem("qk_high_done"), sem("qk_low_done")
        v_psum, vg_done, vsum_done = sem("v_psum"), sem("vg_done"), sem("vsum_done")
        s_psum, max_done, exp_done = sem("s_psum"), sem("max_done"), sem("exp_done")
        pT_psum, pT_done = sem("pT_psum"), sem("pT_done")
        o_psum, share_step, og_done = sem("o_psum"), sem("share_step"), sem("og_done")
        oT_psum, oT_high, oT_low = sem("oT_psum"), sem("oT_high_done"), sem("oT_low_done")
        e_psum, out_psum, acc_done = sem("e_psum"), sem("out_psum"), sem("acc_done")
        turn_bank = [7, 4, 5, 1, 2, 3, 4, 5]
        out_bank = [4, 5, 1, 2, 3, 4, 5, 1]
        OG = 2 * 2
        block = ctx.enter_context(nc.Block())

        @block.sync
        def _(sp):
            for s in (qk_psum, v_psum, s_psum, o_psum, e_psum, out_psum, acc_done, qk_done, qk_low, vsum_done, og_done, xT_low):
                sp.sem_inc(s, CREDIT)

            def load_weights(j):
                for n, t in w_in.items():
                    sp.dma_start(t[:].unsqueeze(1),
                                 d[n][bass.ds(j, 1)].rearrange("j p a b c -> p j a b c")).then_inc(w_loaded[n], 16)

            def load_xT(b):
                sp.dma_start(xT_in[:, :, :].unsqueeze(1), d["xT"][bass.ds(b, 1)].rearrange("b p k s -> p b k s")).then_inc(xT_loaded, 16)

            def pair(j, more):
                sp.wait_ge(og_done, CREDIT + j * NB * OG)
                sp.dma_start(gates[:, :, :].unsqueeze(1), d["gates"][bass.ds(j, 1)].rearrange("j p b t c -> p j (b t) c")).then_inc(gates_loaded, 16)
                if more:
                    for n in shapes:
                        sp.wait_ge(w_low[n], j + 1)
                    load_weights(j + 1)
                with sp.Fori(0, NB - 1) as b:
                    sp.wait_ge(xT_low, CREDIT + j * NB + b + 1)
                    load_xT(b + 1)
                sp.wait_ge(xT_low, CREDIT + j * NB + NB)
                load_xT(0)

            load_xT(0)
            load_weights(0)
            for n, t in (("cos_q", cos_q), ("sin_q", sin_q), ("cos_k", cos_k), ("sin_k", sin_k)):
                sp.dma_start(t[:, :], d[n]).then_inc(tables_loaded, 16)
            with sp.Fori(0, PAIRS - 1) as j:
                pair(j, True)
            pair(PAIRS - 1, False)

        @block.gpsimd
        def _(pool):
            pool.dma_start(acc[:, :, :, :], d["xT"].rearrange("b p k s -> p b k s")).then_inc(acc_loaded, 16)

            def low_x(it):
                pool.wait_ge(xT_high, it + 1)
                pool.tensor_tensor(xT[1][:, :, :], xT_in[:, :, :], xT[0][:, :, :].bitcast(F32), ALU.subtract).then_inc(xT_low, 1)

            low_x(0)
            with pool.Fori(0, PAIRS) as j:
                for n in shapes:
                    pool.wait_ge(w_high[n], j + 1)
                    pool.tensor_tensor(w[n][1][:], w_in[n][:], w[n][0][:].bitcast(F32), ALU.subtract).then_inc(w_low[n], 1)
                with pool.Fori(0, NB) as b:
                    it = j * NB + b
                    for r in range(2):
                        pool.wait_ge(rot_done, it * 4 + 2 * r + 2)
                        if r == 0:
                            pool.wait_ge(qk_low, CREDIT + it * 2)
                        pool.tensor_tensor(qk_full[r][:, :], rot[:, 2 * r, :], rot[:, 2 * r + 1, :], ALU.add).then_inc(qk_done, 1)
                    for h in range(2):
                        pool.wait_ge(vg_done, it * 2 * TT + h * TT + TT)
                        at = it * 6 + h * 3
                        pool.tensor_tensor(v4[:, :, :, :], vg[:, :, 0:4, :], vg[:, :, 4:8, :], ALU.add).then_inc(vsum_done, 1)
                        pool.wait_ge(vsum_done, CREDIT + at + 1)
                        pool.tensor_tensor(v2[:, :, :, :], v4[:, :, 0:2, :], v4[:, :, 2:4, :], ALU.add).then_inc(vsum_done, 1)
                        pool.wait_ge(vsum_done, CREDIT + at + 2)
                        pool.wait_ge(o_psum, CREDIT + it * 2)
                        pool.tensor_tensor(v[:, h, :, :], v2[:, :, 0, :], v2[:, :, 1, :], ALU.add).then_inc(vsum_done, 1)
                    low_x(it + 1)

        @block.tensor
        def _(pe):
            def product(out, left, right, start, stop):
                pe.matmul(out, left(0), right(0), start=start, stop=False)
                pe.matmul(out, left(0), right(1), start=False, stop=False)
                return pe.matmul(out, left(1), right(0), start=False, stop=stop)

            with pe.Fori(0, PAIRS) as j, pe.Fori(0, NB) as b:
                it = j * NB + b
                pe.wait_ge(w_low["wqk"], j + 1)
                pe.wait_ge(xT_low, CREDIT + it + 1)
                pe.wait_ge(og_done, CREDIT + it * OG)
                for r in range(4):
                    for c in range(KD):
                        mm = product(ps[:, r, :], lambda u: wqk[u][:, c, r, :], lambda u: xT[u][:, c, :], c == 0, c == KD - 1)
                    mm.then_inc(qk_psum, 1)

                def values(h, tiles):
                    for t in tiles:
                        if h or t >= 2:
                            pe.wait_ge(vg_done, it * 2 * TT + h * TT + t - 1)
                        for c in range(KD):
                            mm = product(ps[:, 4 + t % 2, :], lambda u: xT[u][:, c, t * P:(t + 1) * P], lambda u: wv[u][:, h, c, :],
                                         c == 0, c == KD - 1)
                        mm.then_inc(v_psum, 1)

                def scores(h):
                    if h == 0:
                        pe.wait_ge(qk_low, CREDIT + it * 2 + 2)
                    at = slice(h * HP, (h + 1) * HP)
                    for t in range(TT):
                        if h:
                            pe.wait_ge(exp_done, it * 2 * TT + t + 1)
                        product(ps[:, t, :], lambda u: q[u][at, t * P:(t + 1) * P], lambda u: k[u][at, :],
                                True, True).then_inc(s_psum, 1)

                def turn_probabilities(h, c):
                    n = h * TT + c
                    if c == 0:
                        pe.wait_ge(exp_done, it * 2 * TT + h * TT + TT)
                    if n == 0:
                        pe.wait_ge(acc_done, CREDIT + it * 2)
                    elif n in (1, 2):
                        pe.wait_ge(vg_done, it * 2 * TT + 2 * TT - 2 + n)
                    elif n == 3:
                        pe.wait_ge(exp_done, it * 2 * TT + 2 * TT)
                    elif n >= 6:
                        pe.wait_ge(pT_done, it * 2 * TT + n - 4)
                    for t in range(TT):
                        mm = pe.transpose(ps[:, turn_bank[n], t * P:(t + 1) * P], prob[h][:, t, c * P:(c + 1) * P], ident[:, :])
                    mm.then_inc(pT_psum, 1)

                def attend(h):
                    pe.wait_ge(vsum_done, CREDIT + it * 6 + h * 3 + 3)
                    pe.wait_ge(pT_done, it * 2 * TT + h * TT + TT)
                    for t in range(TT):
                        for c in range(TT):
                            mm = pe.matmul(ps[:, 6 - 6 * h, t * HP:(t + 1) * HP], probT[h][:, c, t * P:(t + 1) * P],
                                           v[:, h, c, :], start=(c == 0), stop=(c == TT - 1))
                    mm.then_inc(o_psum, 1)

                def turn_outputs(h, e):
                    n = h * EP + e
                    if e == 0:
                        pe.wait_ge(og_done, CREDIT + it * OG + h * 2 + 2)
                    if n == 0:
                        pe.wait_ge(pT_done, it * 2 * TT + 2 * TT)
                    elif n >= 5:
                        pe.wait_ge(oT_low, it * 2 * EP + n - 4)
                    for t in range(TT):
                        mm = pe.transpose(ps[:, out_bank[n], t * P:(t + 1) * P], og[h][:, t, e * P:(e + 1) * P], ident[:, :])
                    mm.then_inc(oT_psum, 1)

                def project(h, e):
                    if h == 0 and e == 0:
                        pe.wait_ge(w_low["wo"], j + 1)
                    pe.wait_ge(oT_low, it * 2 * EP + h * EP + e + 1)
                    last = h == 1 and e == EP - 1
                    for c in range(KD):
                        mm = product(ps[:, 7 - c, :], lambda u: wo[u][:, h, e, c * P:(c + 1) * P], lambda u: ogT[u][:, e, :],
                                     h == 0 and e == 0, last)
                        if last:
                            mm.then_inc(out_psum, 1)
                    if not last:
                        mm.then_inc(e_psum, 1)

                pe.wait_ge(w_low["wv"], j + 1)
                values(0, range(TT))
                scores(0)
                values(1, (0, 1))
                scores(1)
                values(1, (2, 3))
                for h in range(2):
                    for c in range(TT):
                        turn_probabilities(h, c)
                attend(0)
                attend(1)
                for e in range(EP):
                    turn_outputs(0, e)
                project(0, 0)
                project(0, 1)
                project(0, 2)
                turn_outputs(1, 0)
                turn_outputs(1, 1)
                project(0, 3)
                turn_outputs(1, 2)
                project(1, 0)
                turn_outputs(1, 3)
                project(1, 1)
                project(1, 2)
                project(1, 3)

        @block.scalar
        def _(act):
            def high_x(it):
                act.wait_ge(xT_loaded, it * 16 + 16)
                act.wait_ge(v_psum, CREDIT + it * 2 * TT)
                act.activation(xT[0][:, :, :], xT_in[:, :, :], ACT.Copy).then_inc(xT_high, 1)

            high_x(0)
            with act.Fori(0, PAIRS) as j:
                for n, used, count in (("wqk", qk_psum, 4), ("wv", v_psum, 2 * TT), ("wo", out_psum, KD)):
                    act.wait_ge(w_loaded[n], j * 16 + 16)
                    act.wait_ge(used, CREDIT + j * NB * count)
                    act.activation(w[n][0][:], w_in[n][:], ACT.Copy).then_inc(w_high[n], 1)
                with act.Fori(0, NB) as b:
                    it = j * NB + b
                    for r, t in enumerate((q, k)):
                        act.wait_ge(qk_done, CREDIT + it * 2 + r + 1)
                        if r == 0:
                            act.wait_ge(s_psum, CREDIT + it * 2 * TT)
                        act.activation(t[0][:, :], qk_full[r][:, :], ACT.Copy).then_inc(qk_high, 1)

                    def exps(h):
                        for t in range(TT):
                            act.wait_ge(max_done, it * 2 * TT + h * TT + t + 1)
                            act.activation(prob[h][:, t, :], ps[:, t, :], ACT.Exp, bias=negmax[:, h, t:t + 1],
                                           accum_out=total[:, h, t:t + 1]).then_inc(exp_done, 1)

                    def keep(h):
                        for c in range(TT):
                            act.wait_ge(pT_psum, it * 2 * TT + h * TT + c + 1)
                            act.activation(probT[h][:, c, :], ps[:, turn_bank[h * TT + c], :], ACT.Copy).then_inc(pT_done, 1)

                    def high_outputs(h):
                        for e in range(EP):
                            act.wait_ge(oT_psum, it * 2 * EP + h * EP + e + 1)
                            if h == 1:
                                act.wait_ge(e_psum, CREDIT + it * (2 * EP - 1) + e + 1)
                            act.activation(ogT[0][:, e, :], ps[:, out_bank[h * EP + e], :], ACT.Copy).then_inc(oT_high, 1)

                    exps(0)
                    exps(1)
                    keep(0)
                    keep(1)
                    high_x(it + 1)
                    act.wait_ge(out_psum, CREDIT + it * KD)
                    high_outputs(0)
                    high_outputs(1)

        @block.vector
        def _(dve):
            dve.wait_ge(tables_loaded, 64)
            with dve.Fori(0, PAIRS) as j, dve.Fori(0, NB) as b:
                it = j * NB + b
                for r, table in enumerate((cos_q, sin_q, cos_k, sin_k)):
                    dve.wait_ge(qk_psum, CREDIT + it * 4 + r + 1)
                    if r == 0:
                        dve.wait_ge(qk_done, CREDIT + it * 2)
                    dve.tensor_tensor(rot[:, r, :], ps[:, r, :], table[:, :], ALU.mult).then_inc(rot_done, 1)

                def low_qk(r):
                    dve.wait_ge(qk_high, it * 2 + r + 1)
                    part = (q, k)[r]
                    dve.tensor_tensor(part[1][:, :], qk_full[r][:, :], part[0][:, :].bitcast(F32), ALU.subtract).then_inc(qk_low, 1)

                def gate_values(h, t):
                    if h == 0 and t == 0:
                        dve.wait_ge(gates_loaded, j * 16 + 16)
                    if t == 0:
                        dve.wait_ge(vsum_done, CREDIT + it * 6 + h)
                    dve.wait_ge(v_psum, CREDIT + it * 2 * TT + h * TT + t + 1)
                    dve.tensor_tensor(vg[:, t, :, :], ps[:, 4 + t % 2, :].rearrange("p (e n) -> p e n", e=E),
                                      gates[:, bass.ds(b * TT + t, 1), h * E:(h + 1) * E].rearrange("p a e -> p (a e)")
                                      .unsqueeze(2).to_broadcast([P, E, HP]), ALU.mult).then_inc(vg_done, 1)

                def maxima(h):
                    for t in range(TT):
                        dve.wait_ge(s_psum, CREDIT + it * 2 * TT + h * TT + t + 1)
                        dve.tensor_reduce(negmax[:, h, t:t + 1], ps[:, t, :], AX.X, ALU.max, negate=True).then_inc(max_done, 1)

                def output_gates(h):
                    at = it * 4 + h * 2
                    dve.wait_ge(exp_done, it * 2 * TT + h * TT + TT)
                    dve.reciprocal(share[:, h, :], total[:, h, :]).then_inc(share_step, 1)
                    dve.wait_ge(share_step, at + 1)
                    dve.tensor_tensor(og_gate[:, h, :, :], gates[:, bass.ds(b * TT, TT), 2 * E + h * E:2 * E + (h + 1) * E],
                                      share[:, h, :].unsqueeze(2).to_broadcast([P, TT, E]), ALU.mult).then_inc(share_step, 1)

                def gate_outputs(h, half):
                    if half == 0:
                        dve.wait_ge(share_step, it * 4 + h * 2 + 2)
                        dve.wait_ge(o_psum, CREDIT + it * 2 + h + 1)
                    at = slice(2 * half, 2 * half + 2)
                    dve.tensor_tensor(og[h][:, at, :].rearrange("p t (e n) -> p t e n", e=E),
                                      ps[:, 6 - 6 * h, 2 * half * HP:(2 * half + 2) * HP].rearrange("p (t n) -> p t n", t=2)
                                      .unsqueeze(2).to_broadcast([P, 2, E, HP]),
                                      og_gate[:, h, at, :].unsqueeze(3).to_broadcast([P, 2, E, HP]), ALU.mult).then_inc(og_done, 1)

                def low_outputs(h, e):
                    dve.wait_ge(oT_high, it * 2 * EP + h * EP + e + 1)
                    dve.tensor_tensor(ogT[1][:, e, :], ps[:, out_bank[h * EP + e], :], ogT[0][:, e, :].bitcast(F32), ALU.subtract).then_inc(oT_low, 1)

                gate_values(0, 0)
                gate_values(0, 1)
                low_qk(0)
                low_qk(1)
                gate_values(0, 2)
                gate_values(0, 3)
                maxima(0)
                gate_values(1, 0)
                gate_values(1, 1)
                maxima(1)
                gate_values(1, 2)
                gate_values(1, 3)
                output_gates(0)
                output_gates(1)
                gate_outputs(0, 0)
                gate_outputs(0, 1)
                low_outputs(0, 0)
                low_outputs(0, 1)
                gate_outputs(1, 0)
                low_outputs(0, 2)
                gate_outputs(1, 1)
                low_outputs(0, 3)
                for e in range(EP):
                    low_outputs(1, e)
                dve.wait_ge(acc_loaded, 16)
                for c in range(KD):
                    dve.wait_ge(out_psum, CREDIT + it * 2 + c + 1)
                    dve.tensor_tensor(acc[:, bass.ds(b, 1), c, :], acc[:, bass.ds(b, 1), c, :], ps[:, 7 - c, :].unsqueeze(1),
                                      ALU.add).then_inc(acc_done, 1)


def stage_c(nc, d, const, acc):
    with ExitStack() as ctx:
        def sb(name, shape):
            return ctx.enter_context(nc.sbuf_tensor(name, shape, F32))

        def sem(name):
            return ctx.enter_context(nc.semaphore(name))

        ps = ctx.enter_context(nc.psum_tensor("ps_c", [P, 8, S], F32))
        ident = const["ident"]
        w1, w2 = sb("w1", [P, KD, F]), sb("w2", [P, FB, D])
        b1, b2 = sb("b1", [P, FB]), sb("b2", [P, D])
        g1, h1, g2, h2 = (sb(n, [P, D]) for n in ("g1", "h1", "g2", "h2"))
        eps = sb("eps_c", [P, 1])
        accT = sb("accT", [P, KD, S])
        a, an = sb("a", [P, TT, D]), sb("an", [P, TT, D])
        ab = sb("ab", [P, TT, D])
        aT = sb("aT", [P, KD, S])
        hT = sb("hT", [P, FB, S])
        f, fn, on = (sb(n, [P, TT, D]) for n in ("f", "fn", "on"))
        x1 = sb("x1_c", [P, TT, D])
        o, y = sb("o", [P, TT, D]), sb("y", [P, TT, D])
        ln1, ln2, ln3 = (Norm(ctx, nc, n, eps[:, 0:1]) for n in ("ln_1", "ln_2", "ln_3"))
        consts = dict(w1=w1, w2=w2, b1=b1, b2=b2, g1=g1, h1=h1, g2=g2, h2=h2)
        ffn_loaded, fill = sem("ffn_loaded"), sem("fill_c")
        accT_done, acc_psum, aff1_done, a_done = sem("accT_done"), sem("acc_psum"), sem("aff1_done"), sem("a_rows")
        ab_done, aT_psum, aT_done = sem("ab_done"), sem("aT_psum"), sem("aT_done")
        h_psum, h_done, f_psum, f_done = sem("h_psum"), sem("h_done"), sem("f_psum"), sem("f_done")
        aff2_done, o_done, x1_loaded, y_done, y_stored = sem("aff2_done"), sem("o_done"), sem("x1_loaded"), sem("y_done"), sem("y_stored")
        block = ctx.enter_context(nc.Block())

        def half(bank, t):
            return ps[:, bank + t // 2, (t % 2) * D:(t % 2 + 1) * D]

        def rows(v):
            return v[:, :].unsqueeze(1).to_broadcast([P, TT, D])

        def h_bank(m):
            return 4 + (m + 2) % 4

        def turns(eng, turn):
            turn(0, False, True)
            with eng.Fori(0, NB - 2) as r:
                turn(r + 1, True, True)
            turn(NB - 1, True, False)

        @block.sync
        def _(sp):
            for s in (y_done, y_stored):
                sp.sem_inc(s, CREDIT)
            for n, t in consts.items():
                sp.dma_start(t[:], d[n].partition_broadcast(P) if n in ("b2", "g1", "h1", "g2", "h2") else d[n]).then_inc(ffn_loaded, 16)
            with sp.Fori(0, NB) as i:
                sp.wait_ge(y_done, CREDIT + i)
                sp.dma_start(x1[:, :, :].unsqueeze(1), d["x1"][bass.ds(i, 1)].rearrange("b (t p) c -> p b t c", p=P)).then_inc(x1_loaded, 16)
                sp.wait_ge(y_done, CREDIT + i + 1)
                sp.dma_start(d["out"][bass.ds(i, 1)].rearrange("b (t p) c -> p b t c", p=P), y[:, :, :].unsqueeze(1)).then_inc(y_stored, 16)
            sp.wait_ge(y_stored, CREDIT + 16 * NB)

        @block.gpsimd
        def _(pool):
            def take(b, first=False):
                if not first:
                    pool.wait_ge(acc_psum, b)
                pool.tensor_copy(accT[:, :, :].unsqueeze(1), acc[:, bass.ds(b, 1)]).then_inc(accT_done, 1)

            def add_bias(i, has_back):
                pool.wait_ge(a_done, i + 1)
                if has_back:
                    pool.wait_ge(f_done, i)
                pool.tensor_tensor(ab[:, :, :], a[:, :, :], rows(b2), ALU.add).then_inc(ab_done, 1)

            def finish(c):
                pool.wait_ge(ln3.out_done, c * TT + TT)
                pool.wait_ge(x1_loaded, c * 16 + 16)
                pool.wait_ge(y_stored, CREDIT + c * 16)
                pool.tensor_tensor(y[:, :, :], on[:, :, :], x1[:, :, :], ALU.add).then_inc(y_done, 1)

            def turn(i, has_back, has_front):
                if has_front:
                    take(i + 1)
                add_bias(i, has_back)
                if has_back:
                    finish(i - 1)

            pool.memset(eps[:, :], EPS).then_inc(fill, 1)
            take(0, first=True)
            pool.wait_ge(ffn_loaded, 16 * len(consts))
            turns(pool, turn)
            finish(NB - 1)

        @block.tensor
        def _(pe):
            def turn_acc(b, first=False):
                pe.wait_ge(accT_done, b + 1)
                if not first:
                    pe.wait_ge(ln1.out_done, b * TT)
                for t in range(TT):
                    for k in range(KD):
                        mm = pe.transpose(ps[:, t // 2, (t % 2) * D + k * P:(t % 2) * D + (k + 1) * P], accT[:, k, t * P:(t + 1) * P], ident[:, :])
                mm.then_inc(acc_psum, 1)

            def turn_a(b, first=False):
                pe.wait_ge(a_done, b + 1)
                if not first:
                    pe.wait_ge(aT_done, b)
                for k in range(KD):
                    for t in range(TT):
                        mm = pe.transpose(ps[:, 2 + k, t * P:(t + 1) * P], a[:, t, k * P:(k + 1) * P], ident[:, :])
                mm.then_inc(aT_psum, 1)

            def hidden(i, m, has_back):
                if m == 0:
                    pe.wait_ge(aT_done, i + 1)
                if m == 2 and has_back:
                    pe.wait_ge(f_done, i)
                if m >= 4:
                    pe.wait_ge(h_done, i * FB + m - 3)
                for k in range(KD):
                    mm = pe.matmul(ps[:, h_bank(m), :], w1[:, k, m * P:(m + 1) * P], aT[:, k, :], start=(k == 0), stop=(k == KD - 1))
                mm.then_inc(h_psum, 1)

            def outputs(i, t):
                if t == 0:
                    pe.wait_ge(h_done, i * FB + FB)
                for m in range(FB):
                    mm = pe.matmul(half(4, t), hT[:, m, t * P:(t + 1) * P], w2[:, m, :], start=(m == 0), stop=(m == FB - 1))
                if t == TT - 1:
                    mm.then_inc(f_psum, 1)

            def turn(i, has_back, has_front):
                hidden(i, 0, has_back)
                hidden(i, 1, has_back)
                if has_front:
                    turn_acc(i + 1)
                for m in range(2, FB):
                    hidden(i, m, has_back)
                outputs(i, 0)
                outputs(i, 1)
                outputs(i, 2)
                if has_front:
                    turn_a(i + 1)
                outputs(i, 3)

            turn_acc(0, first=True)
            turn_a(0, first=True)
            pe.wait_ge(ffn_loaded, 16 * len(consts))
            turns(pe, turn)

        @block.scalar
        def _(act):
            def keep_a(b):
                act.wait_ge(aT_psum, b + 1)
                act.activation(aT[:, :, :], ps[:, 2:4, :], ACT.Copy).then_inc(aT_done, 1)

            def relu(i, m):
                act.wait_ge(h_psum, i * FB + m + 1)
                act.activation(hT[:, m, :], ps[:, h_bank(m), :], ACT.Relu, bias=b1[:, m:m + 1]).then_inc(h_done, 1)

            def turn(i, has_back, has_front):
                relu(i, 0)
                relu(i, 1)
                if has_back:
                    ln2.first_guess(act, i - 1)
                relu(i, 2)
                relu(i, 3)
                if has_front:
                    ln1.first_guess(act, i + 1)
                for m in range(4, FB):
                    relu(i, m)
                if has_back:
                    ln3.first_guess(act, i - 1)
                if has_front:
                    keep_a(i + 1)

            act.wait_ge(fill, 1)
            act.preload_act_table_set("natural_log_exp_and_others")
            ln1.first_guess(act, 0)
            keep_a(0)
            act.wait_ge(ffn_loaded, 16 * len(consts))
            turns(act, turn)
            ln2.first_guess(act, NB - 1)
            ln3.first_guess(act, NB - 1)

        @block.vector
        def _(dve):
            rows_s, rows_an = (lambda t: half(0, t)), (lambda t: an[:, t, :])
            rows_f, rows_fn = (lambda t: f[:, t, :]), (lambda t: fn[:, t, :])
            rows_o, rows_on = (lambda t: o[:, t, :]), (lambda t: on[:, t, :])

            def stats1(b):
                dve.wait_ge(acc_psum, b + 1)
                ln1.statistics(dve, b, rows_s)

            def norm1(b, first=False):
                ln1.newton(dve, b)
                ln1.normalise(dve, rows_s, rows_an)
                dve.wait_ge(ln1.out_done, b * TT + TT)
                dve.tensor_tensor(an[:, :, :], an[:, :, :], rows(g1), ALU.mult).then_inc(aff1_done, 1)
                dve.wait_ge(aff1_done, b + 1)
                if not first:
                    dve.wait_ge(aT_psum, b)
                    dve.wait_ge(ab_done, b)
                dve.tensor_tensor(a[:, :, :], an[:, :, :], rows(h1), ALU.add).then_inc(a_done, 1)

            def stats2(c):
                dve.wait_ge(f_psum, c + 1)
                dve.wait_ge(ab_done, c + 1)
                dve.tensor_tensor(f[:, :, :], ps[:, 4:6, :].rearrange("p a (h n) -> p (a h) n", h=2), ab[:, :, :], ALU.add).then_inc(f_done, 1)
                dve.wait_ge(f_done, c + 1)
                ln2.statistics(dve, c, rows_f)

            def norm2(c):
                ln2.newton(dve, c)
                ln2.normalise(dve, rows_f, rows_fn)
                dve.wait_ge(ln2.out_done, c * TT + TT)
                dve.tensor_tensor(fn[:, :, :], fn[:, :, :], rows(g2), ALU.mult).then_inc(aff2_done, 1)
                dve.wait_ge(aff2_done, c + 1)
                dve.tensor_tensor(o[:, :, :], fn[:, :, :], rows(h2), ALU.add).then_inc(o_done, 1)

            def stats3(c):
                dve.wait_ge(o_done, c + 1)
                ln3.statistics(dve, c, rows_o)

            def norm3(c):
                ln3.newton(dve, c)
                dve.wait_ge(y_done, CREDIT + c)
                ln3.normalise(dve, rows_o, rows_on)

            def turn(i, has_back, has_front):
                b, c = i + 1, i - 1
                if has_back:
                    stats2(c)
                if has_front:
                    stats1(b)
                if has_back:
                    norm2(c)
                if has_front:
                    norm1(b)
                if has_back:
                    stats3(c)
                    norm3(c)

            stats1(0)
            dve.wait_ge(ffn_loaded, 16 * len(consts))
            norm1(0, first=True)
            turns(dve, turn)
            stats2(NB - 1)
            norm2(NB - 1)
            stats3(NB - 1)
            norm3(NB - 1)


def layout(inputs):
    g = {n: np.asarray(v) for n, v in inputs.items()}

    def rows(w, k):
        return np.ascontiguousarray(w.reshape(k, P, -1).transpose(1, 0, 2))

    def cols(v):
        return np.ascontiguousarray(v.reshape(-1, P).T)

    a = {n[len("L0_attn_"):]: v for n, v in g.items() if n.startswith("L0_attn_")}
    f = {n[len("L0_ffn_"):]: v for n, v in g.items() if n.startswith("L0_ffn_")}
    out = {"x": a["x"]}
    out["w_in"] = rows(a["in_proj_w"].T, KD)
    out["w_xp"] = rows(a["x_proj_w"].T, CB)
    w_dt = np.zeros((XP + 1, DI), np.float32)
    w_dt[0], w_dt[XP] = a["dt_proj_w"][:, 0], a["dt_proj_b"]
    out["w_dt"] = w_dt
    out["w_out"] = rows(a["out_proj_w"].T, CB)
    out["conv_w"] = rows(a["conv_w"][:, 0, :], CB)
    out["conv_b"], out["d_skip"] = cols(a["conv_b"]), cols(a["D"])
    out["a_log"] = rows(a["A_log"], CB).reshape(P, CB * NS)
    out["first"] = np.tile(np.arange(E, 0, -1, dtype=np.float32), (P, 1))
    out["ident"] = np.eye(P, dtype=np.float32)
    sel = np.concatenate([f["Wsel_v"].reshape(H * E, D), f["Wsel_o"].reshape(H * E, D)])
    sel = sel.reshape(2, PAIRS, 2, E, D).transpose(1, 0, 2, 3, 4).reshape(G, D)
    out["w_sel"] = rows(sel.T, KD)

    half = NROT // 2
    swap = np.concatenate([np.arange(half, NROT), np.arange(half), np.arange(NROT, HP)])
    wqk = np.stack([w[..., c] for w in (f["Wq"], f["Wk"]) for c in (np.arange(HP), swap)])
    wqk = wqk.reshape(4, PAIRS, 2, KD, P, HP).transpose(1, 4, 3, 0, 2, 5)
    out["wqk"] = np.ascontiguousarray(wqk).reshape(PAIRS, P, KD, 4, P)
    wv = f["Wv"].reshape(PAIRS, 2, E, KD, P, HP).transpose(0, 4, 1, 3, 2, 5)
    out["wv"] = np.ascontiguousarray(wv).reshape(PAIRS, P, 2, KD, E * HP)
    wo = f["Wo"].reshape(PAIRS, 2, EP, 2 * HP, D).transpose(0, 3, 1, 2, 4)
    out["wo"] = np.ascontiguousarray(wo)
    inv = np.float32(BASE) ** (-np.arange(half, dtype=np.float32) / np.float32(half))
    ang = np.arange(S, dtype=np.float32)[:, None] * inv[None, :]
    cos, sin = np.cos(ang).T.astype(np.float32), np.sin(ang).T.astype(np.float32)
    flat = np.ones((HP - NROT, S), np.float32)
    c = np.tile(np.concatenate([cos, cos, flat]), (2, 1))
    s = np.tile(np.concatenate([-sin, sin, 0 * flat]), (2, 1))
    scale = np.float32(HP ** -0.5)
    out["cos_k"], out["sin_k"], out["cos_q"], out["sin_q"] = c, s, c * scale, s * scale

    out["w1"], out["w2"] = rows(f["W1"], KD), rows(f["W2"], FB)
    out["b1"], out["b2"] = cols(f["b1"]), f["b2"]
    out["g1"], out["h1"], out["g2"], out["h2"] = f["ln1_g"], f["ln1_b"], f["ln2_g"], f["ln2_b"]
    return {n: np.ascontiguousarray(v) for n, v in out.items()}


def program(nc, d):
    d["xT"] = nc.dram_tensor("xT_scratch", (NB, P, KD, S), F32, kind="Internal").ap()
    d["x1"] = nc.dram_tensor("x1_scratch", (NB, S, D), F32, kind="Internal").ap()
    d["gates"] = nc.dram_tensor("gates_scratch", (PAIRS, P, NB, TT, GP), F32, kind="Internal").ap()
    with nc.sbuf_tensor("ident", [P, P], F32) as ident:
        const = {"ident": ident}
        stage_a(nc, d, const)
        with nc.sbuf_tensor("acc", [P, NB, KD, S], F32) as acc:
            stage_b(nc, d, const, acc)
            stage_c(nc, d, const, acc)


def kernel(**inputs):
    import concourse.bacc as bacc
    from concourse.bass_utils import run_bass_kernel_spmd

    nc = bacc.Bacc("TRN2", target_bir_lowering=False, num_devices=1)
    arrays = {f"in_{n}": v for n, v in layout(inputs).items()}
    d = {n[3:]: nc.dram_tensor(n, v.shape, mybir.dt.from_np(v.dtype), kind="ExternalInput").ap() for n, v in arrays.items()}
    d["out"] = nc.dram_tensor("out_0", (NB, S, D), F32, kind="ExternalOutput").ap()
    program(nc, d)
    result = run_bass_kernel_spmd(nc, [arrays], core_ids=[0])
    return result.results[0]["out_0"]
```

```python
from contextlib import ExitStack

import numpy as np

import concourse.bass as bass
from concourse import mybir

F32, F32R = mybir.dt.float32, mybir.dt.float32r
ALU = mybir.AluOpType
ACT = mybir.ActivationFunctionType
AX = mybir.AxisListType

P = 128
NB, S, D = 8, 512, 256
TT = S // P
KD = D // P
DI = 512
CB = DI // P
NS = 16
TAPS = 4
XP = 2 * NS + 1
H, E, HP, F = 16, 8, 64, 1024
PAIRS = H // 2
EP = E // 2
FB = F // P
NROT, BASE = 32, 10000.0
EPS = 1e-5
G = 2 * H * E
GP = G // PAIRS
BLOCKS = 2 * EP
LOW_ROW = P // 2
Q_SCALE = HP ** -0.5
CREDIT = 1


class Norm:

    def __init__(self, ctx, nc, name, eps):
        sem = lambda what: ctx.enter_context(nc.semaphore(f"{name}_{what}"))
        buf = lambda what, n: ctx.enter_context(nc.sbuf_tensor(f"{name}_{what}b", [P, n], F32))
        self.eps = eps
        self.stats_done, self.combine_done = sem("stats"), sem("combine")
        self.guess_done, self.newton_done = sem("guess"), sem("newton")
        self.out_done = sem("out")
        self.stats = buf("stats", TT * 6)
        self.avg, self.var, self.apart, self.spread = (buf(w, TT) for w in ("avg", "var", "apart", "spread"))
        self.logv, self.guess, self.step, self.rstd = (buf(w, TT) for w in ("log", "guess", "step", "rstd"))

    COMBINE = 6

    def mean(self, t):
        return self.avg[:, t:t + 1]

    def variances(self):
        return self.var[:, :]

    def statistics(self, dve, i, rows):
        for t in range(TT):
            dve.bn_stats(self.stats[:, 6 * t:6 * t + 6], rows(t)).then_inc(self.stats_done, 1)
        _, mean_e, m2_e, _, mean_o, m2_o = (self.stats[:, :].rearrange("p (t w) -> p w t", w=6)[:, w, :] for w in range(6))
        done, at = self.combine_done, i * self.COMBINE
        dve.wait_ge(self.stats_done, i * TT + TT)
        dve.tensor_tensor(self.avg[:, :], mean_e, mean_o, ALU.add).then_inc(done, 1)
        dve.tensor_tensor(self.apart[:, :], mean_e, mean_o, ALU.subtract).then_inc(done, 1)
        dve.tensor_tensor(self.spread[:, :], m2_e, m2_o, ALU.add).then_inc(done, 1)
        dve.wait_ge(done, at + 2)
        dve.scalar_tensor_tensor(self.apart[:, :], self.apart[:, :], D / 4.0, self.apart[:, :],
                                 ALU.mult, ALU.mult).then_inc(done, 1)
        dve.tensor_scalar(self.avg[:, :], self.avg[:, :], 0.5, None, ALU.mult).then_inc(done, 1)
        dve.wait_ge(done, at + 4)
        dve.tensor_tensor(self.var[:, :], self.spread[:, :], self.apart[:, :], ALU.add).then_inc(done, 1)

    def first_guess(self, act, i):
        act.wait_ge(self.combine_done, i * self.COMBINE + self.COMBINE)
        act.activation(self.logv[:, :], self.variances(), ACT.Ln, bias=self.eps, scale=1.0 / D).then_inc(self.guess_done, 1)
        act.wait_ge(self.guess_done, i * 2 + 1)
        act.activation(self.guess[:, :], self.logv[:, :], ACT.Exp, scale=-0.5).then_inc(self.guess_done, 1)

    def newton(self, dve, i):
        done, at = self.newton_done, i * 5
        dve.wait_ge(self.guess_done, i * 2 + 2)
        dve.tensor_scalar(self.step[:, :], self.variances(), 1.0 / D, EPS, ALU.mult, ALU.add).then_inc(done, 1)
        dve.wait_ge(done, at + 1)
        dve.tensor_tensor(self.step[:, :], self.step[:, :], self.guess[:, :], ALU.mult).then_inc(done, 1)
        dve.wait_ge(done, at + 2)
        dve.tensor_tensor(self.step[:, :], self.step[:, :], self.guess[:, :], ALU.mult).then_inc(done, 1)
        dve.wait_ge(done, at + 3)
        dve.tensor_scalar(self.step[:, :], self.step[:, :], -0.5, 1.5, ALU.mult, ALU.add).then_inc(done, 1)
        dve.wait_ge(done, at + 4)
        dve.tensor_tensor(self.rstd[:, :], self.guess[:, :], self.step[:, :], ALU.mult).then_inc(done, 1)
        dve.wait_ge(self.combine_done, i * self.COMBINE + self.COMBINE)
        dve.wait_ge(done, at + 5)

    def normalise(self, dve, rows, out):
        for t in range(TT):
            dve.tensor_scalar(out(t), rows(t), self.mean(t), self.rstd[:, t:t + 1],
                              ALU.subtract, ALU.mult).then_inc(self.out_done, 1)


def stage_a(nc, d, const):
    with ExitStack() as ctx:
        def sb(name, shape, dtype=F32):
            return ctx.enter_context(nc.sbuf_tensor(name, shape, dtype))

        def sem(name):
            return ctx.enter_context(nc.semaphore(name))

        ps = ctx.enter_context(nc.psum_tensor("ps_a", [P, 8, S], F32))
        ident = const["ident"]
        B_BANK, C_BANK, TAIL, HEAD = 4, 5, (6, 3), (7, 2)
        FIRST_BANK = dict(xnT=(6, 7), x=(0, 1, 2, 3), conv=(4, 5, 6, 7), xp=(0,), dt=(1, 2, 3, 0), z=(6, 7, 6, 7))
        w_in = sb("w_in", [P, KD, 2 * DI])
        w_xp = sb("w_xp", [P, CB, XP])
        w_dt = sb("w_dt", [XP + 1, DI])
        w_out = sb("w_out", [P, CB, D])
        w_sel = sb("w_sel", [P, KD, G])
        conv_w = sb("conv_w", [P, CB, TAPS])
        conv_b = sb("conv_b", [P, CB])
        conv_diag = sb("conv_diag", [P, CB * TAPS, P])
        ident_r = sb("ident_r", [P, P], F32R)
        d_skip = sb("d_skip", [P, CB])
        a_log = sb("a_log", [P, CB * NS])
        a_exp = sb("a_exp", [P, CB * NS])
        a_neg = sb("a_neg", [P, CB, NS])
        first = sb("first", [P, E])
        ones = sb("ones", [P, 1])
        eps = sb("eps_a", [P, 1])

        x_in = sb("x_in", [P, TT, D])
        xnT = sb("xnT", [P, KD, S])
        work = sb("work", [P, CB, S])
        xp = sb("xp", [XP + 1, S])
        xp_high, xp_low = ([sb(f"xp_{part}{n}", [XP, S], F32R) for n in range(2)] for part in ("high", "low"))
        xc, zs, dt, du = ([sb(f"{name}{n}", [P, CB, S]) for n in range(2)] for name in ("xc", "zs", "dt", "du"))
        dA, dBx, h = ([sb(f"{name}{n}", [P, CB, S]) for n in range(2)] for name in ("dA", "dBx", "state"))
        OWN = CB // 2
        c_copy = [sb(f"c_copy{n}", [P, S]) for n in range(2)]
        y_part = [sb(f"y_part{n}", [P, CB - OWN, S]) for n in range(2)]
        x1, mo = (sb(name, [P, TT, D]) for name in ("x1_a", "mo"))
        x2 = sb("x2", [P, TT, D])
        xn = x2
        x2T = sb("x2T", [P, KD, S])
        sg, left = sb("sg", [P, TT * G]), sb("left", [P, TT * G])
        pick = mo[:, :, :].rearrange("p t c -> p (t c)")
        rank = x2[:, :, :].rearrange("p t c -> p (t c)")
        best = sb("best", [P, TT * G // E])
        gate = sb("gate", [P, PAIRS, TT, GP])

        def groups(v):
            return v.rearrange("p (g e) -> p g e", e=E)

        def by_pair(v, t):
            return v[:, t * G:(t + 1) * G].rearrange("p (j c) -> p j c", j=PAIRS)

        best_e = best[:, :].unsqueeze(2).to_broadcast([P, TT * G // E, E])
        first_g = first[:, :].unsqueeze(1).to_broadcast([P, TT * G // E, E])

        ln_x, ln_m, ln_a = (Norm(ctx, nc, n, eps[:, 0:1]) for n in ("ln_x", "ln_m", "ln_a"))
        early_tiles = dict(ident=ident, w_in=w_in, conv_w=conv_w, conv_b=conv_b)
        const_tiles = dict(w_xp=w_xp, w_dt=w_dt, a_log=a_log, d_skip=d_skip, first=first, w_out=w_out, w_sel=w_sel)
        early_loaded, consts_loaded = sem("early_loaded"), sem("consts_loaded")
        all_early, all_consts = 16 * len(early_tiles), 16 * len(const_tiles)
        x_loaded, x_res_loaded = sem("x_loaded"), sem("x_res_loaded")
        fills, all_fills = sem("fills"), 5
        a_step, diag_done = sem("a_step"), sem("diag_done")
        xnT_psum, xnT_done, z_psum, zs_done = sem("xnT_psum"), sem("xnT_done"), sem("z_psum"), sem("zs_done")
        xs_psum, xs_done, conv_psum, xc_done = sem("xs_psum"), sem("xs_done"), sem("conv_psum"), sem("xc_done")
        xp_psum, xp_done, xp_low_done, dt_psum = sem("xp_psum"), sem("xp_done"), sem("xp_low_done"), sem("dt_psum")
        soft_done, relu_done, dt_done, du_done = sem("soft_done"), sem("relu_done"), sem("dt_done"), sem("du_done")
        b_psum, c_psum, c_copied = sem("b_psum"), sem("c_psum"), sem("c_copied")
        hc_part_done, y_part_done = sem("hc_part_done"), sem("y_part_done")
        dA_done, dBx_done, scan_done, hc_done = sem("dA_done"), sem("dBx_done"), sem("scan_done"), sem("hc_done")
        y_psum, skip_done, yz_done = sem("y_psum"), sem("skip_done"), sem("yz_done")
        mo_psum, mo_done, x1_done = sem("mo_psum"), sem("mo_done"), sem("x1_done")
        x2T_psum, x2T_done = sem("x2T_psum"), sem("x2T_done")
        sel_psum, sg_done, top_step, gate_done = sem("sel_psum"), sem("sg_done"), sem("top_step"), sem("gate_done")
        x1_stored, x2T_stored, gate_stored = sem("x1_stored"), sem("x2T_stored"), sem("gate_stored")
        TOP = 12
        Z = (12, 14)
        SOFT = CB + 2

        def head_bank(step, m, first):
            return FIRST_BANK[step][m] if first else HEAD[m % 2]

        def step_sizes(eng, b, par):
            eng.wait_ge(relu_done, b * CB + CB)
            eng.wait_ge(soft_done, b * SOFT + SOFT)
            eng.tensor_tensor(dt[par][:, :, :], dt[par][:, :, :], work[:, :, :], ALU.add).then_inc(dt_done, 1)

        def inputs_x(eng, b, par):
            eng.wait_ge(dt_done, b + 1)
            eng.tensor_tensor(du[par][:, :, :], dt[par][:, :, :], xc[par][:, :, :], ALU.mult).then_inc(du_done, 1)

        def turns(eng, turn):
            turn(0, 0, False, True)
            with eng.Fori(0, NB // 2 - 1) as pair:
                turn(pair * 2 + 1, 1, True, True)
                turn(pair * 2 + 2, 0, True, True)
            turn(NB - 1, 1, True, False)

        block = ctx.enter_context(nc.Block())

        @block.sync
        def _(sp):
            for s in (x1_done, x1_stored, x2T_stored, gate_stored, gate_done, sg_done):
                sp.sem_inc(s, CREDIT)

            def tiles(name, i):
                return d[name][bass.ds(i, 1)].rearrange("b (t p) c -> p b t c", p=P)

            def load_x(i):
                sp.dma_start(x_in[:, :, :].unsqueeze(1), tiles("x", i)).then_inc(x_loaded, 16)

            def tail(c):
                sp.wait_ge(x1_stored, CREDIT + c * 16)
                sp.dma_start(x1[:, :, :].unsqueeze(1), tiles("x", c)).then_inc(x_res_loaded, 16)
                sp.wait_ge(x1_done, CREDIT + c + 1)
                sp.dma_start(tiles("x1", c), x1[:, :, :].unsqueeze(1)).then_inc(x1_stored, 16)
                sp.wait_ge(x2T_done, c * KD + KD)
                sp.dma_start(d["xT"][bass.ds(c, 1)].rearrange("b p k s -> p b k s"), x2T[:, :, :].unsqueeze(1)).then_inc(x2T_stored, 16)
                sp.wait_ge(gate_done, CREDIT + c * TT + TT)
                sp.dma_start(d["gates"][:, :, bass.ds(c, 1)].rearrange("j p b t c -> p b j (t c)"),
                             gate[:, :, :, :].rearrange("p j t c -> p j (t c)").unsqueeze(1)).then_inc(gate_stored, 16)

            def turn(i, par, has_tail, has_head):
                if has_head:
                    sp.wait_ge(ln_x.out_done, i * TT + TT)
                    load_x(i + 1)
                if has_tail:
                    tail(i - 1)

            load_x(0)
            for n, t in early_tiles.items():
                sp.dma_start(t[:], d[n]).then_inc(early_loaded, 16)
            for n, t in const_tiles.items():
                sp.dma_start(t[:], d[n]).then_inc(consts_loaded, 16)
            turns(sp, turn)
            tail(NB - 1)
            sp.wait_ge(x1_stored, CREDIT + 16 * NB)
            sp.wait_ge(x2T_stored, CREDIT + 16 * NB)
            sp.wait_ge(gate_stored, CREDIT + 16 * NB)

        @block.gpsimd
        def _(pool):
            pool.memset(eps[:, :], EPS).then_inc(fills, 1)
            pool.memset(ones[:, :], 1.0).then_inc(fills, 1)
            pool.memset(xp[:, :], 1.0).then_inc(fills, 1)
            for n in range(2):
                pool.memset(dA[n][:, :, :], 0.0).then_inc(fills, 1)

            def low_xp(b, par):
                pool.wait_ge(xp_done, b * 2 + 2)
                pool.tensor_tensor(xp_low[par][:, :], xp[0:XP, :], xp_high[par][:, :].bitcast(F32), ALU.subtract).then_inc(xp_low_done, 1)

            def gate_y(c, par):
                pool.wait_ge(skip_done, c * CB + CB)
                pool.wait_ge(zs_done, c * CB + CB)
                pool.tensor_tensor(work[:, :, :], work[:, :, :], zs[par][:, :, :], ALU.mult).then_inc(yz_done, 1)

            def rank_picked(c, k):
                pool.wait_ge(top_step, c * TOP + k + 2)
                pool.tensor_tensor(groups(rank), groups(pick), first_g, ALU.mult).then_inc(top_step, 1)

            def weigh(i, n, par):
                c, y = c_copy[n % 2][:, :].unsqueeze(1).to_broadcast([P, CB - OWN, S]), y_part[par]
                state = h[n % 2][:, OWN:CB, :]
                pool.wait_ge(scan_done, i * NS + n + 1)
                pool.wait_ge(c_copied, i * NS + n + 1)
                if n == 0:
                    pool.tensor_tensor(y[:, :, :], state, c, ALU.mult).then_inc(y_part_done, 1)
                else:
                    pool.tensor_tensor(state, state, c, ALU.mult).then_inc(hc_part_done, 1)
                    pool.wait_ge(hc_part_done, i * (NS - 1) + n)
                    pool.wait_ge(y_part_done, i * NS + n)
                    pool.tensor_tensor(y[:, :, :], y[:, :, :], state, ALU.add).then_inc(y_part_done, 1)

            def turn(i, par, has_tail, has_head):
                for n in range(NS):
                    weigh(i, n, par)
                    if n == 0 and has_tail:
                        gate_y(i - 1, 1 - par)
                    if n in (11, 13) and has_tail:
                        rank_picked(i - 1, 3 * (n - 11))
                    if has_head:
                        if n == 9:
                            low_xp(i + 1, 1 - par)
                        elif n == 12:
                            step_sizes(pool, i + 1, 1 - par)
                        elif n == 13:
                            inputs_x(pool, i + 1, 1 - par)

            low_xp(0, 0)
            turns(pool, turn)
            gate_y(NB - 1, (NB - 1) % 2)
            rank_picked(NB - 1, 0)
            rank_picked(NB - 1, 6)

        @block.tensor
        def _(pe):
            def turn_input(b, first):
                pe.wait_ge(ln_x.out_done, b * TT + TT)
                for k in range(KD):
                    if k == 0 and not first:
                        pe.wait_ge(zs_done, b * CB)
                    for t in range(TT):
                        mm = pe.transpose(ps[:, head_bank("xnT", k, first), t * P:(t + 1) * P], xn[:, t, k * P:(k + 1) * P], ident[:, :])
                    mm.then_inc(xnT_psum, 1)

            def project_block(bank, block_of, done):
                for k in range(KD):
                    mm = pe.matmul(ps[:, bank, :], w_in[:, k, block_of * P:(block_of + 1) * P], xnT[:, k, :],
                                   start=(k == 0), stop=(k == KD - 1))
                mm.then_inc(done, 1)

            def project_x(b, m, first=False):
                if m == 0:
                    pe.wait_ge(xnT_done, b * KD + KD)
                elif m >= 2 and not first:
                    pe.wait_ge(xs_done, b * CB + m - 1)
                project_block(head_bank("x", m, first), m, xs_psum)

            def project_z(b, m, first=False):
                if m == 0:
                    pe.wait_ge(relu_done, b * CB + CB)
                elif m >= 2:
                    pe.wait_ge(zs_done, b * CB + m - 1)
                project_block(head_bank("z", m, first), CB + m, z_psum)

            def convolve(b, m, first=False):
                if first:
                    pe.wait_ge(xs_done, b * CB + m + 1)
                elif m >= 2:
                    pe.wait_ge(xc_done, b * CB + m - 1)
                elif m == 0:
                    pe.wait_ge(xs_done, b * CB + CB)
                for far in range(TAPS):
                    mm = pe.matmul(ps[:, head_bank("conv", m, first), far:S], conv_diag[:, m * TAPS + TAPS - 1 - far, :],
                                   work[:, m, 0:S - far], start=(far == 0), stop=(far == TAPS - 1))
                mm.then_inc(conv_psum, 1)

            def project_xp(b, par, first=False):
                pe.wait_ge(xc_done, b * CB + CB)
                for k in range(CB):
                    mm = pe.matmul(ps[0:XP, head_bank("xp", 0, first), :], w_xp[:, k, :], xc[par][:, k, :],
                                   start=(k == 0), stop=(k == CB - 1))
                mm.then_inc(xp_psum, 1)

            def project_dt(b, m, first=False):
                if m == 0:
                    pe.wait_ge(xp_done, b * 2 + 2)
                elif m >= 2 and not first:
                    pe.wait_ge(relu_done, b * CB + m - 1)
                pe.matmul(ps[:, head_bank("dt", m, first), :], w_dt[:, m * P:(m + 1) * P], xp[:, :],
                          start=True, stop=True).then_inc(dt_psum, 1)

            def spread(bank, r, par, done):
                one = ident_r[0:XP, r:r + 1].to_broadcast([XP, P])
                pe.matmul(ps[:, bank, :], one, xp_high[par][:, :], start=True, stop=False)
                pe.matmul(ps[:, bank, :], one, xp_low[par][:, :], start=False, stop=True).then_inc(done, 1)

            def spread_b(b, n, par, first=False):
                if n == 0:
                    pe.wait_ge(xp_low_done, b + 1)
                if not first:
                    pe.wait_ge(dBx_done, b * NS + n)
                spread(B_BANK, 1 + n, par, b_psum)

            def spread_c(b, n, par, first=False):
                if not first:
                    pe.wait_ge(hc_done, b * NS + n)
                spread(C_BANK, 1 + NS + n, par, c_psum)

            def sum_y(i, n, par, has_tail):
                pe.wait_ge(hc_done, i * NS + n + 1)
                if n == 0 and has_tail:
                    pe.wait_ge(skip_done, i * CB)
                for m in range(OWN):
                    mm = pe.matmul(ps[:, m, :], ident[:, :], h[n % 2][:, m, :], start=(n == 0), stop=(n == NS - 1))
                mm.then_inc(y_psum, 1)

            def project_out(c, half):
                if half == 0:
                    pe.wait_ge(yz_done, c + 1)
                    pe.wait_ge(sg_done, CREDIT + c * 2)
                for t in range(2):
                    at = slice((2 * half + t) * P, (2 * half + t + 1) * P)
                    for k in range(CB):
                        mm = pe.matmul(ps[:, TAIL[half], t * D:(t + 1) * D], work[:, k, at], w_out[:, k, :],
                                       start=(k == 0), stop=(k == CB - 1))
                mm.then_inc(mo_psum, 1)

            def turn_x2(c):
                pe.wait_ge(ln_a.out_done, c * TT + TT)
                pe.wait_ge(mo_done, c * 2 + 2)
                for k in range(KD):
                    for t in range(TT):
                        mm = pe.transpose(ps[:, TAIL[k], t * P:(t + 1) * P], x2[:, t, k * P:(k + 1) * P], ident[:, :])
                    mm.then_inc(x2T_psum, 1)

            def select(c, half):
                if half == 0:
                    pe.wait_ge(x2T_done, c * KD + KD)
                for t in range(2):
                    at = slice((2 * half + t) * P, (2 * half + t + 1) * P)
                    for k in range(KD):
                        mm = pe.matmul(ps[:, TAIL[half], t * G:(t + 1) * G], x2T[:, k, at], w_sel[:, k, :], start=(k == 0), stop=(k == KD - 1))
                mm.then_inc(sel_psum, 1)

            def turn(i, par, has_tail, has_head):
                b, c = i + 1, i - 1
                for n in range(NS):
                    if n + 2 < NS:
                        spread_b(i, n + 2, par)
                    elif has_head:
                        spread_b(b, n + 2 - NS, 1 - par)
                    if n + 1 < NS:
                        spread_c(i, n + 1, par)
                    elif has_head:
                        spread_c(b, 0, 1 - par)
                    if has_head:
                        if n in (3, 4):
                            project_x(b, 2 * n - 6)
                        elif n in (5, 6, 7, 8):
                            convolve(b, n - 5)
                        elif n == 9:
                            project_xp(b, 1 - par)
                        elif n == 10:
                            project_dt(b, 0)
                            project_dt(b, 1)
                        elif n in (12, 13):
                            project_z(b, n - 11)
                    sum_y(i, n, par, has_tail)
                    if has_head and n == 2:
                        turn_input(b, False)
                    if has_tail:
                        if n in (1, 2):
                            project_out(c, n - 1)
                        elif n == 6:
                            turn_x2(c)
                        elif n in (8, 9):
                            select(c, n - 8)
                    if has_head:
                        if n in (3, 4):
                            project_x(b, 2 * n - 5)
                        elif n == 10:
                            project_dt(b, 2)
                            project_dt(b, 3)
                        elif n in (11, 13):
                            project_z(b, 3 * (n - 11) // 2)

            pe.wait_ge(early_loaded, all_early)
            turn_input(0, True)
            for m in range(CB):
                project_x(0, m, first=True)
            pe.wait_ge(diag_done, 1)
            for m in range(CB):
                convolve(0, m, first=True)
            pe.wait_ge(consts_loaded, all_consts)
            pe.wait_ge(fills, all_fills)
            project_xp(0, 0, first=True)
            for m in range(CB):
                project_dt(0, m, first=True)
            for m in range(CB):
                project_z(0, m, first=True)
            pe.wait_ge(a_step, 3)
            spread_b(0, 0, 0, first=True)
            spread_c(0, 0, 0, first=True)
            spread_b(0, 1, 0)
            turns(pe, turn)
            project_out(NB - 1, 0)
            project_out(NB - 1, 1)
            turn_x2(NB - 1)
            select(NB - 1, 0)
            select(NB - 1, 1)

        @block.scalar
        def _(act):
            def exps():
                act.preload_act_table_set("natural_log_exp_and_others")

            def keep_input(b, first=False):
                for k in range(KD):
                    act.wait_ge(xnT_psum, b * KD + k + 1)
                    act.activation(xnT[:, k, :], ps[:, head_bank("xnT", k, first), :], ACT.Copy).then_inc(xnT_done, 1)

            def keep_x(b, m, first=False):
                act.wait_ge(xs_psum, b * CB + m + 1)
                act.activation(work[:, m, :], ps[:, head_bank("x", m, first), :], ACT.Copy).then_inc(xs_done, 1)

            def silu_z(b, m, par, bank, unused=False):
                if m == 0 and not unused:
                    act.wait_ge(yz_done, b - 1)
                act.wait_ge(z_psum, b * CB + m + 1)
                act.activation(zs[par][:, m, :], ps[:, bank, :], ACT.Silu).then_inc(zs_done, 1)

            def silu_x(b, m, par, first=False):
                act.wait_ge(conv_psum, b * CB + m + 1)
                act.activation(xc[par][:, m, :], ps[:, head_bank("conv", m, first), :], ACT.Silu, bias=conv_b[:, m:m + 1]).then_inc(xc_done, 1)

            def keep_xp(b, par, first=False):
                act.wait_ge(xp_psum, b + 1)
                bank = ps[0:XP, head_bank("xp", 0, first), :]
                act.activation(xp_high[par][:, :], bank, ACT.Copy).then_inc(xp_done, 1)
                act.activation(xp[0:XP, :], bank, ACT.Copy).then_inc(xp_done, 1)

            def magnitudes(b, m, par, first=False):
                act.wait_ge(dt_psum, b * CB + m + 1)
                bank = ps[:, head_bank("dt", m, first), :]
                act.activation(work[:, m, :], bank, ACT.Abs).then_inc(soft_done, 1)
                act.activation(dt[par][:, m, :], bank, ACT.Relu).then_inc(relu_done, 1)

            def softplus_exp(b):
                act.wait_ge(soft_done, b * SOFT + CB)
                act.activation(work[:, :, :], work[:, :, :], ACT.Exp, scale=-1.0).then_inc(soft_done, 1)

            def softplus_ln(b):
                act.wait_ge(soft_done, b * SOFT + CB + 1)
                act.activation(work[:, :, :], work[:, :, :], ACT.Ln, bias=ones[:, 0:1]).then_inc(soft_done, 1)

            def decay(b, n, par, first=False):
                if n == 0:
                    act.wait_ge(dt_done, b + 1)
                if not first:
                    act.wait_ge(scan_done, b * NS + n - 1)
                for m in range(CB):
                    act.activation(dA[n % 2][:, m, 1:S], dt[par][:, m, 1:S], ACT.Exp,
                                   scale=a_neg[:, m, n:n + 1]).then_inc(dA_done, 1)

            def copy_c(i, n, first=False):
                if not first:
                    act.wait_ge(y_part_done, i * NS + n - 1)
                act.wait_ge(c_psum, i * NS + n + 1)
                act.activation(c_copy[n % 2][:, :], ps[:, C_BANK, :], ACT.Copy).then_inc(c_copied, 1)

            def keep_out(c, half):
                if half == 0:
                    act.wait_ge(gate_done, CREDIT + c * TT)
                act.wait_ge(mo_psum, c * 2 + half + 1)
                act.activation(mo[:, 2 * half:2 * half + 2, :].rearrange("p t c -> p (t c)"), ps[:, TAIL[half], :], ACT.Copy).then_inc(mo_done, 1)

            def keep_x2(c):
                act.wait_ge(x2T_stored, CREDIT + c * 16)
                for k in range(KD):
                    act.wait_ge(x2T_psum, c * KD + k + 1)
                    act.activation(x2T[:, k, :], ps[:, TAIL[k], :], ACT.Copy).then_inc(x2T_done, 1)

            def sigmoid(c, half):
                act.wait_ge(sel_psum, c * 2 + half + 1)
                act.activation(sg[:, half * S:(half + 1) * S], ps[:, TAIL[half], :], ACT.Sigmoid).then_inc(sg_done, 1)

            def turn(i, par, has_tail, has_head):
                b, c = i + 1, i - 1
                for n in range(NS):
                    if n + 2 < NS:
                        decay(i, n + 2, par)
                    elif has_head:
                        decay(b, n + 2 - NS, 1 - par)
                    if n + 1 < NS:
                        copy_c(i, n + 1, first=not has_tail and n == 0)
                    elif has_head:
                        copy_c(b, 0)
                    if has_tail and n == 10:
                        sigmoid(c, 0)
                        sigmoid(c, 1)
                        exps()
                    if has_head:
                        if n in (3, 4):
                            keep_x(b, 2 * n - 6)
                        elif n == 8:
                            silu_x(b, 2, 1 - par)
                            silu_x(b, 3, 1 - par)
                        elif n == 9:
                            keep_xp(b, 1 - par)
                        elif n in (10, 11):
                            magnitudes(b, 2 * n - 20, 1 - par)
                            magnitudes(b, 2 * n - 19, 1 - par)
                    if has_head and n == 0:
                        ln_x.first_guess(act, b)
                    if has_tail:
                        if n == 4:
                            ln_m.first_guess(act, c)
                        elif n == 5:
                            ln_a.first_guess(act, c)
                    if has_tail:
                        if n in (2, 3):
                            keep_out(c, n - 2)
                        elif n == 7:
                            keep_x2(c)
                    if has_head:
                        if n == 2:
                            keep_input(b)
                        elif n in (3, 4):
                            keep_x(b, 2 * n - 5)
                        elif n == 6:
                            silu_x(b, 0, 1 - par)
                            silu_x(b, 1, 1 - par)
                        elif n == 11:
                            softplus_exp(b)
                            softplus_ln(b)
                        elif n in Z:
                            for m in (n - Z[0], n - Z[0] + 1):
                                silu_z(b, m, 1 - par, head_bank("z", m, False), unused=not has_tail)
                    if n in (6, 8) + Z:
                        exps()

            act.wait_ge(fills, all_fills)
            exps()
            ln_x.first_guess(act, 0)
            keep_input(0, first=True)
            for m in range(CB):
                keep_x(0, m, first=True)
            act.wait_ge(early_loaded, all_early)
            for m in range(CB):
                silu_x(0, m, 0, first=True)
            exps()
            act.wait_ge(consts_loaded, all_consts)
            act.activation(a_exp[:, :], a_log[:, :], ACT.Exp).then_inc(a_step, 1)
            act.wait_ge(a_step, 1)
            act.mul(a_neg[:, :, :].rearrange("p c n -> p (c n)"), a_exp[:, :], -1.0).then_inc(a_step, 1)
            act.activation(ident_r[:, :], ident[:, :], ACT.Copy).then_inc(a_step, 1)
            act.wait_ge(a_step, 2)
            keep_xp(0, 0, first=True)
            for m in range(CB):
                magnitudes(0, m, 0, first=True)
            softplus_exp(0)
            softplus_ln(0)
            for m in range(CB):
                silu_z(0, m, 0, head_bank("z", m, True), unused=True)
            exps()
            decay(0, 0, 0, first=True)
            decay(0, 1, 0, first=True)
            copy_c(0, 0, first=True)
            turns(act, turn)
            keep_out(NB - 1, 0)
            keep_out(NB - 1, 1)
            ln_m.first_guess(act, NB - 1)
            ln_a.first_guess(act, NB - 1)
            keep_x2(NB - 1)
            sigmoid(NB - 1, 0)
            sigmoid(NB - 1, 1)

        @block.vector
        def _(dve):
            rows_in, rows_n = (lambda t: x_in[:, t, :]), (lambda t: xn[:, t, :])
            rows_m, rows_1, rows_2 = (lambda t: mo[:, t, :]), (lambda t: x1[:, t, :]), (lambda t: x2[:, t, :])

            def stats_x(b):
                dve.wait_ge(x_loaded, b * 16 + 16)
                ln_x.statistics(dve, b, rows_in)

            def norm_x(b):
                ln_x.newton(dve, b)
                ln_x.normalise(dve, rows_in, rows_n)

            def inputs(b, n, par, first=False):
                if n == 0:
                    dve.wait_ge(du_done, b + 1)
                if not first:
                    dve.wait_ge(scan_done, b * NS + n - 1)
                dve.wait_ge(b_psum, b * NS + n + 1)
                dve.tensor_tensor(dBx[n % 2][:, :, :], du[par][:, :, :],
                                  ps[:, B_BANK, :].unsqueeze(1).to_broadcast([P, CB, S]), ALU.mult).then_inc(dBx_done, 1)

            def scan(i, n, first):
                dve.wait_ge(dA_done, (i * NS + n + 1) * CB)
                dve.wait_ge(dBx_done, i * NS + n + 1)
                if not (first and n < 2):
                    dve.wait_ge(y_psum, i * NS + n - 1)
                    dve.wait_ge(y_part_done, i * NS + n - 1)
                dve.tensor_tensor_scan(h[n % 2][:, :, :].rearrange("p c s -> p (c s)"),
                                       dA[n % 2][:, :, :].rearrange("p c s -> p (c s)"),
                                       dBx[n % 2][:, :, :].rearrange("p c s -> p (c s)"),
                                       0.0, ALU.mult, ALU.add).then_inc(scan_done, 1)

            def weigh(i, n):
                dve.wait_ge(scan_done, i * NS + n + 1)
                dve.wait_ge(c_copied, i * NS + n + 1)
                dve.tensor_tensor(h[n % 2][:, 0:OWN, :], h[n % 2][:, 0:OWN, :],
                                  ps[:, C_BANK, :].unsqueeze(1).to_broadcast([P, OWN, S]), ALU.mult).then_inc(hc_done, 1)

            def skip(c, par):
                dve.wait_ge(y_psum, c * NS + NS)
                dve.wait_ge(y_part_done, c * NS + NS)
                for m in range(CB):
                    dve.scalar_tensor_tensor(work[:, m, :], xc[par][:, m, :], d_skip[:, m:m + 1],
                                             ps[:, m, :] if m < OWN else y_part[par][:, m - OWN, :],
                                             ALU.mult, ALU.add).then_inc(skip_done, 1)

            def stats_m(c):
                dve.wait_ge(mo_done, c * 2 + 2)
                ln_m.statistics(dve, c, rows_m)

            def norm_m(c):
                ln_m.newton(dve, c)
                ln_m.normalise(dve, rows_m, rows_m)

            def stats_a(c):
                dve.wait_ge(ln_m.out_done, c * TT + TT)
                dve.wait_ge(x_res_loaded, c * 16 + 16)
                dve.tensor_tensor(x1[:, :, :], x1[:, :, :], mo[:, :, :], ALU.add).then_inc(x1_done, 1)
                dve.wait_ge(x1_done, CREDIT + c + 1)
                ln_a.statistics(dve, c, rows_1)

            def norm_a(c):
                ln_a.newton(dve, c)
                ln_a.normalise(dve, rows_1, rows_2)

            def best_of(c, src, k):
                step = c * TOP + k
                if k == 0:
                    dve.wait_ge(sg_done, CREDIT + c * 2 + 2)
                else:
                    dve.wait_ge(top_step, step)
                dve.tensor_reduce(best[:, :], groups(src), AX.X, ALU.max).then_inc(top_step, 1)
                dve.wait_ge(top_step, step + 1)
                dve.tensor_tensor(groups(pick), groups(src), best_e, ALU.is_equal).then_inc(top_step, 1)

            def first_of(c, src, k):
                step = c * TOP + k
                dve.wait_ge(top_step, step + 3)
                dve.tensor_reduce(best[:, :], groups(rank), AX.X, ALU.max).then_inc(top_step, 1)
                dve.wait_ge(top_step, step + 4)
                dve.tensor_tensor(groups(pick), groups(rank), best_e, ALU.is_equal).then_inc(top_step, 1)
                dve.wait_ge(top_step, step + 5)
                dve.scalar_tensor_tensor(left[:, :], pick, -2.0, src, ALU.mult, ALU.add).then_inc(top_step, 1)

            def gates(c):
                dve.wait_ge(top_step, c * TOP + TOP)
                dve.wait_ge(gate_stored, CREDIT + c * 16)
                for t in range(TT):
                    dve.scalar_tensor_tensor(gate[:, :, t, :], by_pair(left, t), 0.0, by_pair(sg, t),
                                             ALU.is_lt, ALU.mult).then_inc(gate_done, 1)

            def turn(i, par, has_tail, has_head):
                b, c = i + 1, i - 1
                for n in range(NS):
                    scan(i, n, not has_tail)
                    if n + 1 < NS:
                        inputs(i, n + 1, par, first=not has_tail and n == 0)
                    elif has_head:
                        inputs(b, 0, 1 - par)
                    weigh(i, n)
                    if has_head:
                        if n == 0:
                            stats_x(b)
                        elif n == 1:
                            norm_x(b)
                    if has_tail:
                        if n == 0:
                            skip(c, 1 - par)
                        elif n == 4:
                            stats_m(c)
                        elif n == 5:
                            norm_m(c)
                            stats_a(c)
                        elif n == 6:
                            norm_a(c)
                        elif n == 11:
                            best_of(c, sg[:, :], 0)
                        elif n == 12:
                            first_of(c, sg[:, :], 0)
                        elif n == 13:
                            best_of(c, left[:, :], 6)
                        elif n == 14:
                            first_of(c, left[:, :], 6)
                        elif n == 15:
                            gates(c)

            dve.wait_ge(fills, all_fills)
            stats_x(0)
            norm_x(0)
            dve.wait_ge(early_loaded, all_early)
            dve.tensor_tensor(conv_diag[:, :, :], ident[:, :].unsqueeze(1).to_broadcast([P, CB * TAPS, P]),
                              conv_w[:, :, :].rearrange("p m r -> p (m r)").unsqueeze(2).to_broadcast([P, CB * TAPS, P]),
                              ALU.mult).then_inc(diag_done, 1)
            step_sizes(dve, 0, 0)
            inputs_x(dve, 0, 0)
            dve.wait_ge(consts_loaded, all_consts)
            inputs(0, 0, 0, first=True)
            turns(dve, turn)
            last = NB - 1
            skip(last, last % 2)
            stats_m(last)
            norm_m(last)
            stats_a(last)
            norm_a(last)
            best_of(last, sg[:, :], 0)
            first_of(last, sg[:, :], 0)
            best_of(last, left[:, :], 6)
            first_of(last, left[:, :], 6)
            gates(last)


def stage_b(nc, d, const, acc):
    with ExitStack() as ctx:
        def sb(name, shape, dtype=F32):
            return ctx.enter_context(nc.sbuf_tensor(name, shape, dtype))

        def parts(name, shape):
            return [sb(f"{name}_{part}", shape, F32R) for part in ("high", "low")]

        def sem(name):
            return ctx.enter_context(nc.semaphore(name))

        ps = ctx.enter_context(nc.psum_tensor("ps_b", [P, 8, S], F32))
        ident = const["ident"]
        gates = sb("gates", [P, NB * TT, GP])
        shapes = dict(wqk=[P, KD, 2, P], wv=[P, 2, KD, E * HP], wo=[P, 2, EP, D])
        w_in = {n: sb(n, s) for n, s in shapes.items()}
        w = {n: parts(n, s) for n, s in shapes.items()}
        wqk, wv, wo = w["wqk"], w["wv"], w["wo"]
        cos, sin = sb("cos", [P, S]), sb("sin", [P, S])
        swap = sb("swap", [P, P], F32R)
        spread = sb("spread", [P, BLOCKS, P], F32R)
        xT_in = sb("xT", [P, KD, S])
        xT = parts("xT", [P, KD, S])
        raw = [parts(n, [P, S]) for n in ("q_raw", "k_raw")]
        qk_full = sb("qk_full", [P, 2, S])
        q, k = parts("q", [P, S]), parts("k", [P, S])
        vg = sb("vg", [P, TT, E, HP])
        v4 = qk_full[:, :, :].rearrange("p a s -> p (a s)").rearrange("p (t e n) -> p t e n", t=TT, e=E // 2)
        oT = qk_full
        v2 = sb("v2", [P, TT, E // 4, HP])
        v = sb("v", [P, 2, TT, HP])
        vv = parts("vv", [P, 2, TT, 2 * HP])
        negmax = sb("negmax", [P, 2, TT])
        total = sb("total", [P, 2, TT])
        share = sb("share", [P, 2, TT])
        out_gate = sb("out_gate", [P, TT, P])
        gT = sb("gT", [P, S], F32R)
        prob = [sb(f"prob{h}", [P, TT, S]) for h in range(2)]
        RING = 5
        probT = parts("probT", [P, RING, S])
        og = prob
        rot = prob[0]
        ogT = parts("ogT", [P, EP, S])

        consts_loaded, consts_done, zero_done = sem("consts_b_loaded"), sem("consts_b_done"), sem("zero_done")
        tables_loaded, gates_loaded, acc_loaded = sem("tables_loaded"), sem("gates_loaded"), sem("acc_loaded")
        w_loaded, w_high, w_low = ({n: sem(f"{n}_{what}") for n in shapes} for what in ("loaded", "high_done", "low_done"))
        xT_loaded, xT_high, xT_low = sem("xT_loaded"), sem("xT_high_done"), sem("xT_low_done")
        raw_psum, raw_high, raw_low, swap_psum = sem("raw_psum"), sem("raw_high"), sem("raw_low"), sem("swap_psum")
        rot_done, qk_done = sem("rot_done"), sem("qk_done")
        qk_high, qk_low = sem("qk_high_done"), sem("qk_low_done")
        v_psum, vg_done, vsum_done = sem("v_psum"), sem("vg_done"), sem("vsum_done")
        v_high, v_low = sem("v_high"), sem("v_low")
        s_psum, max_done, exp_done = sem("s_psum"), sem("max_done"), sem("exp_done")
        pT_psum, pT_high, pT_low, pv_psum = sem("pT_psum"), sem("pT_high"), sem("pT_low"), sem("pv_psum")
        gate_step, gT_psum, gT_high, gT_low = sem("gate_step"), sem("gT_psum"), sem("gT_high"), sem("gT_low")
        oT_done, spread_psum, og_done = sem("oT_done"), sem("spread_psum"), sem("og_done")
        oT_high, oT_low = sem("oT_high_done"), sem("oT_low_done")
        e_psum, out_psum, acc_done = sem("e_psum"), sem("out_psum"), sem("acc_done")
        N = BLOCKS
        VSUM = 2 * 2 * 3
        GATE = 1 + 2 * 2
        raw_bank, swap_bank = (0, 2), (1, 3)
        turn_bank = [7, 4, 5, 1, 2, 3, 4, 5]
        GT_BANK = 6

        def spread_bank(n):
            return 3 + n % 3

        block = ctx.enter_context(nc.Block())

        @block.sync
        def _(sp):
            for s in (raw_psum, v_psum, s_psum, out_psum, acc_done, qk_low, vsum_done, og_done, oT_low, xT_low, gate_step):
                sp.sem_inc(s, CREDIT)

            def load_weights(j):
                for n, t in w_in.items():
                    sp.dma_start(t[:].unsqueeze(1), d[n][bass.ds(j, 1)].rearrange("j p a b c -> p j a b c")).then_inc(w_loaded[n], 16)

            def load_xT(b):
                sp.dma_start(xT_in[:, :, :].unsqueeze(1), d["xT"][bass.ds(b, 1)].rearrange("b p k s -> p b k s")).then_inc(xT_loaded, 16)

            def pair(j, more):
                sp.wait_ge(gate_step, CREDIT + j * NB * GATE)
                sp.dma_start(gates[:, :, :].unsqueeze(1), d["gates"][bass.ds(j, 1)].rearrange("j p b t c -> p j (b t) c")).then_inc(gates_loaded, 16)
                if more:
                    for n in shapes:
                        sp.wait_ge(w_low[n], j * 2 + 2 if n == "wo" else j + 1)
                    load_weights(j + 1)
                with sp.Fori(0, NB - 1) as b:
                    sp.wait_ge(xT_low, CREDIT + j * NB + b + 1)
                    load_xT(b + 1)
                sp.wait_ge(xT_low, CREDIT + j * NB + NB)
                load_xT(0)

            sp.dma_start(vg[:, 0:2, :, :].rearrange("p t e n -> p (t e n)"), d["spread"]).then_inc(consts_loaded, 16)
            sp.dma_start(vg[:, 2, 0:2, :].rearrange("p e n -> p (e n)"), d["swap"]).then_inc(consts_loaded, 16)
            load_xT(0)
            load_weights(0)
            for n, t in (("cos", cos), ("sin", sin)):
                sp.dma_start(t[:, :], d[n]).then_inc(tables_loaded, 16)
            with sp.Fori(0, PAIRS - 1) as j:
                pair(j, True)
            pair(PAIRS - 1, False)

        def turns(eng, start, batch, pair_start=None):
            def pair(j, more):
                if pair_start:
                    pair_start(j)
                with eng.Fori(0, NB - 1) as b:
                    batch(j * NB + b, j, b, True, False)
                batch(j * NB + (NB - 1), j, NB - 1, False, more)

            start()
            with eng.Fori(0, PAIRS - 1) as j:
                pair(j, True)
            pair(PAIRS - 1, False)

        @block.gpsimd
        def _(pool):
            def low_x(it):
                pool.wait_ge(xT_high, it + 1)
                pool.tensor_tensor(xT[1][:, :, :], xT_in[:, :, :], xT[0][:, :, :].bitcast(F32), ALU.subtract).then_inc(xT_low, 1)

            def low_weights(j, n):
                pool.wait_ge(w_high[n], j + 1)
                pool.tensor_tensor(w[n][1][:], w_in[n][:], w[n][0][:].bitcast(F32), ALU.subtract).then_inc(w_low[n], 1)

            def low_wo(j, h):
                pool.wait_ge(w_high["wo"], j * 2 + h + 1)
                pool.tensor_tensor(wo[1][:, h], w_in["wo"][:, h], wo[0][:, h].bitcast(F32), ALU.subtract).then_inc(w_low["wo"], 1)

            def start():
                low_weights(0, "wqk")
                low_weights(0, "wv")
                low_wo(0, 0)
                low_wo(0, 1)

            def sum_values(it, h):
                for half in range(2):
                    at = slice(2 * half, 2 * half + 2)
                    step = CREDIT + it * VSUM + h * 6 + half * 3
                    pool.wait_ge(vg_done, it * 2 * TT + h * TT + 2 * half + 2)
                    pool.tensor_tensor(v4[:, at, :, :], vg[:, at, 0:4, :], vg[:, at, 4:8, :], ALU.add).then_inc(vsum_done, 1)
                    pool.wait_ge(vsum_done, step + 1)
                    pool.tensor_tensor(v2[:, at, :, :], v4[:, at, 0:2, :], v4[:, at, 2:4, :], ALU.add).then_inc(vsum_done, 1)
                    pool.wait_ge(vsum_done, step + 2)
                    pool.tensor_tensor(v[:, h, at, :], v2[:, at, 0, :], v2[:, at, 1, :], ALU.add).then_inc(vsum_done, 1)

            def low_values(it, h):
                pool.wait_ge(v_high, it * 2 + h + 1)
                pool.tensor_tensor(vv[1][:, h, :, :].rearrange("p t (c n) -> p t c n", c=2), v[:, h, :, :].unsqueeze(2).to_broadcast([P, TT, 2, HP]),
                                   vv[0][:, h, :, :].bitcast(F32).rearrange("p t (c n) -> p t c n", c=2), ALU.subtract).then_inc(v_low, 1)

            def batch(it, j, b, more, more_pairs):
                for r in range(2):
                    pool.wait_ge(rot_done, it * 4 + 3 + r)
                    if r == 0:
                        pool.wait_ge(qk_low, CREDIT + it * 2)
                        pool.wait_ge(vsum_done, CREDIT + it * VSUM)
                    pool.tensor_tensor(qk_full[:, r, :], rot[:, r, :], rot[:, 2 + r, :], ALU.add).then_inc(qk_done, 1)
                pool.wait_ge(qk_low, CREDIT + it * 2 + 2)
                sum_values(it, 0)
                low_values(it, 0)
                sum_values(it, 1)
                low_values(it, 1)
                low_x(it + 1)
                if more_pairs:
                    low_weights(j + 1, "wqk")
                    low_weights(j + 1, "wv")
                    low_wo(j + 1, 0)
                    low_wo(j + 1, 1)

            pool.memset(out_gate[:, :, :], 0.0).then_inc(zero_done, 1)
            low_x(0)
            pool.dma_start(acc[:, :, :, :], d["xT"].rearrange("b p k s -> p b k s")).then_inc(acc_loaded, 16)
            turns(pool, start, batch)

        @block.tensor
        def _(pe):
            def product(out, left, right, start, stop):
                pe.matmul(out, left(0), right(0), start=start, stop=False)
                pe.matmul(out, left(0), right(1), start=False, stop=False)
                return pe.matmul(out, left(1), right(0), start=False, stop=stop)

            def project_raw(it, r):
                if r == 0:
                    pe.wait_ge(xT_low, CREDIT + it + 1)
                for c in range(KD):
                    mm = product(ps[:, raw_bank[r], :], lambda u: wqk[u][:, c, r, :], lambda u: xT[u][:, c, :], c == 0, c == KD - 1)
                mm.then_inc(raw_psum, 1)

            def swap_halves(it, r):
                pe.wait_ge(raw_low, it * 2 + r + 1)
                for u in range(2):
                    mm = pe.matmul(ps[:, swap_bank[r], :], swap[:, :], raw[r][u][:, :], start=(u == 0), stop=(u == 1))
                mm.then_inc(swap_psum, 1)

            def values(it, h, tiles):
                for t in tiles:
                    if h or t >= 2:
                        pe.wait_ge(vg_done, it * 2 * TT + h * TT + t - 1)
                    for c in range(KD):
                        mm = product(ps[:, 4 + t % 2, :], lambda u: xT[u][:, c, t * P:(t + 1) * P], lambda u: wv[u][:, h, c, :],
                                     c == 0, c == KD - 1)
                    mm.then_inc(v_psum, 1)

            def scores(it, h):
                if h == 0:
                    pe.wait_ge(qk_low, CREDIT + it * 2 + 2)
                at = slice(h * HP, (h + 1) * HP)
                for t in range(TT):
                    if h:
                        pe.wait_ge(exp_done, it * 2 * TT + t + 1)
                    product(ps[:, t, :], lambda u: q[u][at, t * P:(t + 1) * P], lambda u: k[u][at, :],
                            True, True).then_inc(s_psum, 1)

            def turn_probabilities(it, n):
                h, c = divmod(n, TT)
                if c == 0:
                    pe.wait_ge(exp_done, it * 2 * TT + h * TT + TT)
                if n == 0:
                    pe.wait_ge(acc_done, CREDIT + it * 2)
                elif n in (1, 2):
                    pe.wait_ge(vg_done, it * 2 * TT + 2 * TT - 2 + n)
                elif n == 3:
                    pe.wait_ge(exp_done, it * 2 * TT + 2 * TT)
                elif n >= 6:
                    pe.wait_ge(pT_low, it * N + n - 4)
                for t in range(TT):
                    mm = pe.transpose(ps[:, turn_bank[n], t * P:(t + 1) * P], prob[h][:, t, c * P:(c + 1) * P], ident[:, :])
                mm.then_inc(pT_psum, 1)

            def turn_gates(it):
                pe.wait_ge(gate_step, CREDIT + it * GATE + GATE)
                for t in range(TT):
                    mm = pe.transpose(ps[:, GT_BANK, t * P:(t + 1) * P], out_gate[:, t, :], ident[:, :])
                mm.then_inc(gT_psum, 1)

            def attend(it, h):
                pe.wait_ge(v_low, it * 2 + h + 1)
                for c in range(TT):
                    n = h * TT + c
                    pe.wait_ge(pT_low, it * N + n + 1)
                    product(ps[:, h, :], lambda u: vv[u][:, h, c, :], lambda u: probT[u][:, n % RING, :],
                            c == 0, c == TT - 1).then_inc(pv_psum, 1)

            def spread_gates(it, n):
                if n == 0:
                    pe.wait_ge(gT_low, it + 1)
                if n < 3:
                    pe.wait_ge(pT_low, it * N + 6 + n)
                else:
                    pe.wait_ge(og_done, CREDIT + it * N + n - 2)
                pe.matmul(ps[:, spread_bank(n), :], spread[:, n, :], gT[:, :], start=True, stop=True).then_inc(spread_psum, 1)

            def project(it, j, n):
                h, e = divmod(n, EP)
                if n == 0:
                    pe.wait_ge(w_low["wo"], j * 2 + 2)
                pe.wait_ge(oT_low, CREDIT + it * N + n + 1)
                for c in range(KD):
                    mm = product(ps[:, 7 - c, :], lambda u: wo[u][:, h, e, c * P:(c + 1) * P], lambda u: ogT[u][:, e, :],
                                 n == 0, n == N - 1)
                    if n == N - 1:
                        mm.then_inc(out_psum, 1)
                if n < N - 1:
                    mm.then_inc(e_psum, 1)

            def start():
                pe.wait_ge(w_low["wqk"], 1)
                project_raw(0, 0)
                project_raw(0, 1)

            def batch(it, j, b, more, more_pairs):
                pe.wait_ge(og_done, CREDIT + it * N)
                swap_halves(it, 0)
                swap_halves(it, 1)
                pe.wait_ge(w_low["wv"], j + 1)
                values(it, 0, range(TT))
                scores(it, 0)
                values(it, 1, (0, 1))
                scores(it, 1)
                values(it, 1, (2, 3))
                for n in range(N):
                    turn_probabilities(it, n)
                turn_gates(it)
                attend(it, 0)
                spread_gates(it, 0)
                spread_gates(it, 1)
                attend(it, 1)
                spread_gates(it, 2)
                for n in range(N):
                    project(it, j, n)
                    if n + 3 < N:
                        spread_gates(it, n + 3)
                    if n == 3 and (more or more_pairs):
                        if more_pairs:
                            pe.wait_ge(w_low["wqk"], j + 2)
                        project_raw(it + 1, 0)
                        project_raw(it + 1, 1)

            pe.wait_ge(consts_done, 2)
            turns(pe, start, batch)

        @block.scalar
        def _(act):
            def high_x(it):
                act.wait_ge(xT_loaded, it * 16 + 16)
                act.wait_ge(v_psum, CREDIT + it * 2 * TT)
                act.activation(xT[0][:, :, :], xT_in[:, :, :], ACT.Copy).then_inc(xT_high, 1)

            def high_raw(it, r):
                act.wait_ge(raw_psum, CREDIT + it * 2 + r + 1)
                act.activation(raw[r][0][:, :], ps[:, raw_bank[r], :], ACT.Copy).then_inc(raw_high, 1)

            def high_weights(j, n, used, count):
                act.wait_ge(w_loaded[n], j * 16 + 16)
                act.wait_ge(used, CREDIT + j * NB * count)
                act.activation(w[n][0][:], w_in[n][:], ACT.Copy).then_inc(w_high[n], 1)

            def high_wo(j, h):
                act.wait_ge(w_loaded["wo"], j * 16 + 16)
                act.activation(wo[0][:, h], w_in["wo"][:, h], ACT.Copy).then_inc(w_high["wo"], 1)

            def exps(it, h):
                for t in range(TT):
                    act.wait_ge(max_done, it * 2 * TT + h * TT + t + 1)
                    act.activation(prob[h][:, t, :], ps[:, t, :], ACT.Exp, bias=negmax[:, h, t:t + 1],
                                   accum_out=total[:, h, t:t + 1]).then_inc(exp_done, 1)

            def high_values(it, h):
                act.wait_ge(vsum_done, CREDIT + it * VSUM + h * 6 + 6)
                act.activation(vv[0][:, h, :, :].rearrange("p t (c n) -> p t c n", c=2),
                               v[:, h, :, :].unsqueeze(2).to_broadcast([P, TT, 2, HP]), ACT.Copy).then_inc(v_high, 1)

            def high_probabilities(it, n):
                act.wait_ge(pT_psum, it * N + n + 1)
                if n >= RING:
                    act.wait_ge(pv_psum, it * N + n - RING + 1)
                act.activation(probT[0][:, n % RING, :], ps[:, turn_bank[n], :], ACT.Copy).then_inc(pT_high, 1)

            def high_gates(it):
                act.wait_ge(gT_psum, it + 1)
                act.activation(gT[:, :], ps[:, GT_BANK, :], ACT.Copy).then_inc(gT_high, 1)

            def keep_outputs(it, h):
                act.wait_ge(pv_psum, it * N + h * TT + TT)
                act.activation(oT[:, h, :], ps[:, h, :], ACT.Copy).then_inc(oT_done, 1)

            def high_outputs(it, n):
                h, e = divmod(n, EP)
                act.wait_ge(og_done, CREDIT + it * N + n + 1)
                if n == 0:
                    act.wait_ge(out_psum, CREDIT + it * KD)
                elif n >= EP:
                    act.wait_ge(e_psum, it * (N - 1) + n - EP + 1)
                act.activation(ogT[0][:, e, :], og[h][:, e, :], ACT.Copy).then_inc(oT_high, 1)

            def start():
                high_weights(0, "wqk", raw_psum, 2)
                high_weights(0, "wv", v_psum, 2 * TT)
                high_wo(0, 0)
                high_raw(0, 0)
                high_raw(0, 1)

            def pair_start(j):
                act.preload_act_table_set("natural_log_exp_and_others")
                act.wait_ge(out_psum, CREDIT + j * NB * KD)
                high_wo(j, 1)

            def batch(it, j, b, more, more_pairs):
                for r, t in enumerate((q, k)):
                    act.wait_ge(qk_done, it * 2 + r + 1)
                    if r == 0:
                        act.wait_ge(s_psum, CREDIT + it * 2 * TT)
                    act.activation(t[0][:, :], qk_full[:, r, :], ACT.Copy, scale=Q_SCALE if r == 0 else 1.0).then_inc(qk_high, 1)
                exps(it, 0)
                high_values(it, 0)
                exps(it, 1)
                for n in range(RING):
                    high_probabilities(it, n)
                high_values(it, 1)
                high_gates(it)
                for n in range(RING, N):
                    high_probabilities(it, n)
                keep_outputs(it, 0)
                high_x(it + 1)
                if more_pairs:
                    high_weights(j + 1, "wqk", raw_psum, 2)
                high_outputs(it, 0)
                keep_outputs(it, 1)
                for n in range(1, 5):
                    high_outputs(it, n)
                if more_pairs:
                    high_weights(j + 1, "wv", v_psum, 2 * TT)
                high_outputs(it, 5)
                high_outputs(it, 6)
                if more or more_pairs:
                    high_raw(it + 1, 0)
                    high_raw(it + 1, 1)
                high_outputs(it, 7)
                if more_pairs:
                    act.wait_ge(e_psum, it * (N - 1) + EP)
                    high_wo(j + 1, 0)

            act.wait_ge(consts_loaded, 32)
            act.activation(spread[:, :, :].rearrange("p b m -> p (b m)"), vg[:, 0:2, :, :].rearrange("p t e n -> p (t e n)"),
                           ACT.Copy).then_inc(consts_done, 1)
            act.activation(swap[:, :], vg[:, 2, 0:2, :].rearrange("p e n -> p (e n)"), ACT.Copy).then_inc(consts_done, 1)
            high_x(0)
            turns(act, start, batch, pair_start)

        @block.vector
        def _(dve):
            def low_raw(it, r):
                dve.wait_ge(raw_high, it * 2 + r + 1)
                bank = ps[:, raw_bank[r], :]
                dve.tensor_tensor(raw[r][1][:, :], bank, raw[r][0][:, :].bitcast(F32), ALU.subtract).then_inc(raw_low, 1)
                dve.tensor_tensor(rot[:, r, :], bank, cos[:, :], ALU.mult).then_inc(rot_done, 1)

            def rotate(it, r):
                dve.wait_ge(swap_psum, it * 2 + r + 1)
                dve.tensor_tensor(rot[:, 2 + r, :], ps[:, swap_bank[r], :], sin[:, :], ALU.mult).then_inc(rot_done, 1)

            def low_qk(it, r):
                dve.wait_ge(qk_high, it * 2 + r + 1)
                part = (q, k)[r]
                dve.scalar_tensor_tensor(part[1][:, :], qk_full[:, r, :], Q_SCALE if r == 0 else 1.0, part[0][:, :].bitcast(F32),
                                         ALU.mult, ALU.subtract).then_inc(qk_low, 1)

            def gate_values(it, j, b, h, t):
                if h == 0 and t == 0:
                    dve.wait_ge(gates_loaded, j * 16 + 16)
                if t % 2 == 0:
                    dve.wait_ge(vsum_done, CREDIT + it * VSUM + (t // 2 * 3 + 1 if h else 0))
                dve.wait_ge(v_psum, CREDIT + it * 2 * TT + h * TT + t + 1)
                dve.tensor_tensor(vg[:, t, :, :], ps[:, 4 + t % 2, :].rearrange("p (e n) -> p e n", e=E),
                                  gates[:, bass.ds(b * TT + t, 1), h * E:(h + 1) * E].rearrange("p a e -> p (a e)")
                                  .unsqueeze(2).to_broadcast([P, E, HP]), ALU.mult).then_inc(vg_done, 1)

            def maxima(it, h):
                for t in range(TT):
                    dve.wait_ge(s_psum, CREDIT + it * 2 * TT + h * TT + t + 1)
                    dve.tensor_reduce(negmax[:, h, t:t + 1], ps[:, t, :], AX.X, ALU.max, negate=True).then_inc(max_done, 1)

            def output_gates(it, b):
                dve.wait_ge(exp_done, it * 2 * TT + 2 * TT)
                dve.reciprocal(share[:, :, :], total[:, :, :]).then_inc(gate_step, 1)
                dve.wait_ge(gate_step, CREDIT + it * GATE + 1)
                for h in range(2):
                    for at in (h * E, LOW_ROW + h * E):
                        dve.tensor_tensor(out_gate[:, :, at:at + E], gates[:, bass.ds(b * TT, TT), 2 * E + h * E:2 * E + (h + 1) * E],
                                          share[:, h, :].unsqueeze(2).to_broadcast([P, TT, E]), ALU.mult).then_inc(gate_step, 1)

            def low_probabilities(it, n):
                dve.wait_ge(pT_high, it * N + n + 1)
                dve.tensor_tensor(probT[1][:, n % RING, :], ps[:, turn_bank[n], :], probT[0][:, n % RING, :].bitcast(F32),
                                  ALU.subtract).then_inc(pT_low, 1)

            def low_gates(it):
                dve.wait_ge(gT_high, it + 1)
                rows = slice(LOW_ROW, LOW_ROW + 2 * E)
                low = gT[rows, :]
                dve.tensor_tensor(low, ps[rows, GT_BANK, :], low.bitcast(F32), ALU.subtract).then_inc(gT_low, 1)

            def gate_outputs(it, n):
                h, e = divmod(n, EP)
                if e == 0:
                    dve.wait_ge(oT_done, it * 2 + h + 1)
                dve.wait_ge(spread_psum, it * N + n + 1)
                dve.tensor_tensor(og[h][:, e, :], oT[:, h, :], ps[:, spread_bank(n), :], ALU.mult).then_inc(og_done, 1)

            def low_outputs(it, n):
                h, e = divmod(n, EP)
                dve.wait_ge(oT_high, it * N + n + 1)
                dve.tensor_tensor(ogT[1][:, e, :], og[h][:, e, :], ogT[0][:, e, :].bitcast(F32), ALU.subtract).then_inc(oT_low, 1)

            def start():
                low_raw(0, 0)
                low_raw(0, 1)

            def batch(it, j, b, more, more_pairs):
                rotate(it, 0)
                rotate(it, 1)
                gate_values(it, j, b, 0, 0)
                gate_values(it, j, b, 0, 1)
                low_qk(it, 0)
                low_qk(it, 1)
                gate_values(it, j, b, 0, 2)
                gate_values(it, j, b, 0, 3)
                maxima(it, 0)
                gate_values(it, j, b, 1, 0)
                gate_values(it, j, b, 1, 1)
                maxima(it, 1)
                gate_values(it, j, b, 1, 2)
                gate_values(it, j, b, 1, 3)
                output_gates(it, b)
                for n in range(RING):
                    low_probabilities(it, n)
                low_gates(it)
                low_probabilities(it, 5)
                low_probabilities(it, 6)
                low_probabilities(it, 7)
                gate_outputs(it, 0)
                for n in range(1, 7):
                    gate_outputs(it, n)
                    low_outputs(it, n - 1)
                low_outputs(it, 6)
                if more or more_pairs:
                    dve.wait_ge(oT_low, CREDIT + it * N + EP)
                    low_raw(it + 1, 0)
                    low_raw(it + 1, 1)
                gate_outputs(it, 7)
                low_outputs(it, 7)
                dve.wait_ge(acc_loaded, 16)
                for c in range(KD):
                    dve.wait_ge(out_psum, CREDIT + it * 2 + c + 1)
                    dve.tensor_tensor(acc[:, bass.ds(b, 1), c, :], acc[:, bass.ds(b, 1), c, :], ps[:, 7 - c, :].unsqueeze(1),
                                      ALU.add).then_inc(acc_done, 1)

            dve.wait_ge(tables_loaded, 32)
            dve.wait_ge(consts_done, 2)
            dve.wait_ge(zero_done, 1)
            turns(dve, start, batch)


def stage_c(nc, d, const, acc):
    with ExitStack() as ctx:
        def sb(name, shape, dtype=F32):
            return ctx.enter_context(nc.sbuf_tensor(name, shape, dtype))

        def parts(name, shape):
            return [sb(f"{name}_{part}", shape, F32R) for part in ("high", "low")]

        def sem(name):
            return ctx.enter_context(nc.semaphore(name))

        ps = ctx.enter_context(nc.psum_tensor("ps_c", [P, 8, S], F32))
        ident = const["ident"]
        w1, w2 = sb("w1", [P, KD, F]), sb("w2", [P, FB, D])
        b1, b2 = sb("b1", [P, FB]), sb("b2", [P, D])
        g1, h1, g2, h2 = (sb(n, [P, D]) for n in ("g1", "h1", "g2", "h2"))
        eps = sb("eps_c", [P, 1])
        accT = sb("accT", [P, KD, S])
        a, an = sb("a", [P, TT, D]), sb("an", [P, TT, D])
        ab = sb("ab", [P, TT, D])
        w1_parts, w2_parts = parts("w1", [P, KD, F]), parts("w2", [P, FB, D])
        aT = parts("aT", [P, KD, S])
        h = sb("h", [P, 2, S])
        hT = parts("hT", [P, FB, S])
        f, fn, on = (sb(n, [P, TT, D]) for n in ("f", "fn", "on"))
        x1 = sb("x1_c", [P, TT, D])
        o, y = sb("o", [P, TT, D]), sb("y", [P, TT, D])
        ln1, ln2, ln3 = (Norm(ctx, nc, n, eps[:, 0:1]) for n in ("ln_1", "ln_2", "ln_3"))
        vectors = dict(g1=g1, h1=h1, b1=b1, b2=b2, g2=g2, h2=h2)
        vectors_loaded, ffn_loaded, fill = sem("vectors_loaded"), sem("ffn_loaded"), sem("fill_c")
        all_vectors = 16 * len(vectors)
        accT_done, acc_psum, aff1_done, a_done = sem("accT_done"), sem("acc_psum"), sem("aff1_done"), sem("a_rows")
        aT_low, h_high, h_low, w_high, w1_low = sem("aT_low"), sem("h_high"), sem("h_low"), sem("ffn_high"), sem("w1_low_done")
        w2_low = sem("w2_low_done")
        ab_done, aT_psum, aT_high = sem("ab_done"), sem("aT_psum"), sem("aT_high")
        h_psum, h_done, f_psum, f_done = sem("h_psum"), sem("h_done"), sem("f_psum"), sem("f_done")
        aff2_done, o_done, x1_loaded, y_done, y_stored = sem("aff2_done"), sem("o_done"), sem("x1_loaded"), sem("y_done"), sem("y_stored")
        block = ctx.enter_context(nc.Block())

        def half(bank, t):
            return ps[:, bank + t // 2, (t % 2) * D:(t % 2 + 1) * D]

        def rows(v):
            return v[:, :].unsqueeze(1).to_broadcast([P, TT, D])

        def h_bank(m):
            return 4 + (m + 2) % 4

        def turns(eng, turn):
            turn(0, False, True)
            with eng.Fori(0, NB - 2) as r:
                turn(r + 1, True, True)
            turn(NB - 1, True, False)

        @block.sync
        def _(sp):
            for s in (y_done, y_stored):
                sp.sem_inc(s, CREDIT)
            for n, t in vectors.items():
                sp.dma_start(t[:], d[n] if n == "b1" else d[n].partition_broadcast(P)).then_inc(vectors_loaded, 16)
            for n, t in (("w1", w1), ("w2", w2)):
                sp.dma_start(t[:], d[n]).then_inc(ffn_loaded, 16)
            with sp.Fori(0, NB) as i:
                sp.wait_ge(y_done, CREDIT + i)
                sp.dma_start(x1[:, :, :].unsqueeze(1), d["x1"][bass.ds(i, 1)].rearrange("b (t p) c -> p b t c", p=P)).then_inc(x1_loaded, 16)
                sp.wait_ge(y_done, CREDIT + i + 1)
                sp.dma_start(d["out"][bass.ds(i, 1)].rearrange("b (t p) c -> p b t c", p=P), y[:, :, :].unsqueeze(1)).then_inc(y_stored, 16)
            sp.wait_ge(y_stored, CREDIT + 16 * NB)

        @block.gpsimd
        def _(pool):
            def low_hidden(i, m):
                pool.wait_ge(h_high, i * FB + m + 1)
                pool.tensor_tensor(hT[1][:, m, :], h[:, m % 2, :], hT[0][:, m, :].bitcast(F32), ALU.subtract).then_inc(h_low, 1)

            def add_bias(i, has_back):
                pool.wait_ge(a_done, i + 1)
                if has_back:
                    pool.wait_ge(f_done, i)
                pool.tensor_tensor(ab[:, :, :], a[:, :, :], rows(b2), ALU.add).then_inc(ab_done, 1)

            def finish(c):
                pool.wait_ge(ln3.out_done, c * TT + TT)
                pool.wait_ge(x1_loaded, c * 16 + 16)
                pool.wait_ge(y_stored, CREDIT + c * 16)
                pool.tensor_tensor(y[:, :, :], on[:, :, :], x1[:, :, :], ALU.add).then_inc(y_done, 1)

            def turn(i, has_back, has_front):
                add_bias(i, has_back)
                for m in range(FB):
                    low_hidden(i, m)
                if has_back:
                    finish(i - 1)

            pool.memset(eps[:, :], EPS).then_inc(fill, 1)
            pool.wait_ge(vectors_loaded, all_vectors)
            pool.wait_ge(w_high, 2)
            pool.tensor_tensor(w2_parts[1][:, :, :], w2[:, :, :], w2_parts[0][:, :, :].bitcast(F32), ALU.subtract).then_inc(w2_low, 1)
            turns(pool, turn)
            finish(NB - 1)

        @block.tensor
        def _(pe):
            def product(out, left, right, start, stop):
                pe.matmul(out, left(0), right(0), start=start, stop=False)
                pe.matmul(out, left(0), right(1), start=False, stop=False)
                return pe.matmul(out, left(1), right(0), start=False, stop=stop)

            def turn_acc(b, first=False):
                pe.wait_ge(accT_done, b + 1)
                if not first:
                    pe.wait_ge(ln1.out_done, b * TT)
                for t in range(TT):
                    for k in range(KD):
                        mm = pe.transpose(ps[:, t // 2, (t % 2) * D + k * P:(t % 2) * D + (k + 1) * P], accT[:, k, t * P:(t + 1) * P], ident[:, :])
                mm.then_inc(acc_psum, 1)

            def turn_a(b, first=False):
                pe.wait_ge(a_done, b + 1)
                if not first:
                    pe.wait_ge(aT_low, b)
                for k in range(KD):
                    for t in range(TT):
                        mm = pe.transpose(ps[:, 2 + k, t * P:(t + 1) * P], a[:, t, k * P:(k + 1) * P], ident[:, :])
                mm.then_inc(aT_psum, 1)

            def hidden(i, m, has_back):
                if m == 0:
                    pe.wait_ge(aT_low, i + 1)
                if m == 2 and has_back:
                    pe.wait_ge(f_done, i)
                if m >= 4:
                    pe.wait_ge(h_done, i * FB + m - 3)
                for k in range(KD):
                    mm = product(ps[:, h_bank(m), :], lambda u: w1_parts[u][:, k, m * P:(m + 1) * P], lambda u: aT[u][:, k, :], k == 0, k == KD - 1)
                mm.then_inc(h_psum, 1)

            def outputs(i, t):
                for m in range(FB):
                    if t == 0:
                        pe.wait_ge(h_low, i * FB + m + 1)
                        if m == 0:
                            pe.wait_ge(h_done, i * FB + FB - 1)
                    if t == 2 and m == 0:
                        pe.wait_ge(h_done, i * FB + FB)
                    mm = product(half(4, t), lambda u: hT[u][:, m, t * P:(t + 1) * P], lambda u: w2_parts[u][:, m, :], m == 0, m == FB - 1)
                if t == TT - 1:
                    mm.then_inc(f_psum, 1)

            def turn(i, has_back, has_front):
                hidden(i, 0, has_back)
                hidden(i, 1, has_back)
                if has_front:
                    turn_acc(i + 1)
                for m in range(2, FB):
                    hidden(i, m, has_back)
                outputs(i, 0)
                outputs(i, 1)
                outputs(i, 2)
                if has_front:
                    turn_a(i + 1)
                outputs(i, 3)

            turn_acc(0, first=True)
            turn_a(0, first=True)
            pe.wait_ge(w1_low, 1)
            pe.wait_ge(w2_low, 1)
            turns(pe, turn)

        @block.scalar
        def _(act):
            def take(b):
                act.activation(accT[:, :, :].unsqueeze(1), acc[:, bass.ds(b, 1)], ACT.Copy).then_inc(accT_done, 1)

            def keep_a(b):
                act.wait_ge(aT_psum, b + 1)
                act.activation(aT[0][:, :, :], ps[:, 2:4, :], ACT.Copy).then_inc(aT_high, 1)

            def relu(i, m):
                act.wait_ge(h_psum, i * FB + m + 1)
                if m >= 2:
                    act.wait_ge(h_low, i * FB + m - 1)
                act.activation(h[:, m % 2, :], ps[:, h_bank(m), :], ACT.Relu, bias=b1[:, m:m + 1]).then_inc(h_done, 1)

            def high_hidden(i, m):
                act.wait_ge(h_done, i * FB + m + 1)
                act.activation(hT[0][:, m, :], h[:, m % 2, :], ACT.Copy).then_inc(h_high, 1)

            def hidden(i, blocks):
                for m in blocks:
                    relu(i, m)
                    high_hidden(i, m)

            def turn(i, has_back, has_front):
                if has_front:
                    take(i + 1)
                hidden(i, (0, 1))
                if has_back:
                    ln2.first_guess(act, i - 1)
                hidden(i, (2, 3))
                if has_front:
                    ln1.first_guess(act, i + 1)
                hidden(i, range(4, FB))
                if has_back:
                    ln3.first_guess(act, i - 1)
                if has_front:
                    keep_a(i + 1)

            act.wait_ge(fill, 1)
            act.preload_act_table_set("natural_log_exp_and_others")
            take(0)
            ln1.first_guess(act, 0)
            act.wait_ge(ffn_loaded, 32)
            for t, part in ((w1, w1_parts), (w2, w2_parts)):
                act.activation(part[0][:, :, :], t[:, :, :], ACT.Copy).then_inc(w_high, 1)
            keep_a(0)
            act.wait_ge(vectors_loaded, all_vectors)
            turns(act, turn)
            ln2.first_guess(act, NB - 1)
            ln3.first_guess(act, NB - 1)

        @block.vector
        def _(dve):
            rows_s, rows_an = (lambda t: half(0, t)), (lambda t: an[:, t, :])
            rows_f, rows_fn = (lambda t: f[:, t, :]), (lambda t: fn[:, t, :])
            rows_o, rows_on = (lambda t: o[:, t, :]), (lambda t: on[:, t, :])

            def stats1(b):
                dve.wait_ge(acc_psum, b + 1)
                ln1.statistics(dve, b, rows_s)

            def norm1(b, first=False):
                ln1.newton(dve, b)
                ln1.normalise(dve, rows_s, rows_an)
                dve.wait_ge(ln1.out_done, b * TT + TT)
                dve.tensor_tensor(an[:, :, :], an[:, :, :], rows(g1), ALU.mult).then_inc(aff1_done, 1)
                dve.wait_ge(aff1_done, b + 1)
                if not first:
                    dve.wait_ge(aT_psum, b)
                    dve.wait_ge(ab_done, b)
                dve.tensor_tensor(a[:, :, :], an[:, :, :], rows(h1), ALU.add).then_inc(a_done, 1)

            def low_a(b):
                dve.wait_ge(aT_high, b + 1)
                dve.tensor_tensor(aT[1][:, :, :], ps[:, 2:4, :], aT[0][:, :, :].bitcast(F32), ALU.subtract).then_inc(aT_low, 1)

            def stats2(c):
                dve.wait_ge(f_psum, c + 1)
                dve.wait_ge(ab_done, c + 1)
                dve.tensor_tensor(f[:, :, :], ps[:, 4:6, :].rearrange("p a (h n) -> p (a h) n", h=2), ab[:, :, :], ALU.add).then_inc(f_done, 1)
                dve.wait_ge(f_done, c + 1)
                ln2.statistics(dve, c, rows_f)

            def norm2(c):
                ln2.newton(dve, c)
                ln2.normalise(dve, rows_f, rows_fn)
                dve.wait_ge(ln2.out_done, c * TT + TT)
                dve.tensor_tensor(fn[:, :, :], fn[:, :, :], rows(g2), ALU.mult).then_inc(aff2_done, 1)
                dve.wait_ge(aff2_done, c + 1)
                dve.tensor_tensor(o[:, :, :], fn[:, :, :], rows(h2), ALU.add).then_inc(o_done, 1)

            def stats3(c):
                dve.wait_ge(o_done, c + 1)
                ln3.statistics(dve, c, rows_o)

            def norm3(c):
                ln3.newton(dve, c)
                dve.wait_ge(y_done, CREDIT + c)
                ln3.normalise(dve, rows_o, rows_on)

            def turn(i, has_back, has_front):
                b, c = i + 1, i - 1
                if has_back:
                    stats2(c)
                if has_front:
                    stats1(b)
                if has_back:
                    norm2(c)
                if has_front:
                    norm1(b)
                if has_back:
                    stats3(c)
                    norm3(c)
                if has_front:
                    low_a(b)

            stats1(0)
            dve.wait_ge(vectors_loaded, all_vectors)
            norm1(0, first=True)
            dve.wait_ge(w_high, 1)
            dve.tensor_tensor(w1_parts[1][:, :, :], w1[:, :, :], w1_parts[0][:, :, :].bitcast(F32), ALU.subtract).then_inc(w1_low, 1)
            low_a(0)
            turns(dve, turn)
            stats2(NB - 1)
            norm2(NB - 1)
            stats3(NB - 1)
            norm3(NB - 1)


def layout(inputs):
    g = {n: np.asarray(v) for n, v in inputs.items()}

    def rows(w, k):
        return np.ascontiguousarray(w.reshape(k, P, -1).transpose(1, 0, 2))

    def cols(v):
        return np.ascontiguousarray(v.reshape(-1, P).T)

    a = {n[len("L0_attn_"):]: v for n, v in g.items() if n.startswith("L0_attn_")}
    f = {n[len("L0_ffn_"):]: v for n, v in g.items() if n.startswith("L0_ffn_")}
    out = {"x": a["x"]}
    out["w_in"] = rows(a["in_proj_w"].T, KD)
    out["w_xp"] = rows(a["x_proj_w"].T, CB)
    w_dt = np.zeros((XP + 1, DI), np.float32)
    w_dt[0], w_dt[XP] = a["dt_proj_w"][:, 0], a["dt_proj_b"]
    out["w_dt"] = w_dt
    out["w_out"] = rows(a["out_proj_w"].T, CB)
    out["conv_w"] = rows(a["conv_w"][:, 0, :], CB)
    out["conv_b"], out["d_skip"] = cols(a["conv_b"]), cols(a["D"])
    out["a_log"] = rows(a["A_log"], CB).reshape(P, CB * NS)
    out["first"] = np.tile(np.arange(E, 0, -1, dtype=np.float32), (P, 1))
    out["ident"] = np.eye(P, dtype=np.float32)
    sel = np.concatenate([f["Wsel_v"].reshape(H * E, D), f["Wsel_o"].reshape(H * E, D)])
    sel = sel.reshape(2, PAIRS, 2, E, D).transpose(1, 0, 2, 3, 4).reshape(G, D)
    out["w_sel"] = rows(sel.T, KD)

    wqk = np.stack([f["Wq"], f["Wk"]]).reshape(2, PAIRS, 2, KD, P, HP).transpose(1, 4, 3, 0, 2, 5)
    out["wqk"] = np.ascontiguousarray(wqk).reshape(PAIRS, P, KD, 2, P)
    wv = f["Wv"].reshape(PAIRS, 2, E, KD, P, HP).transpose(0, 4, 1, 3, 2, 5)
    out["wv"] = np.ascontiguousarray(wv).reshape(PAIRS, P, 2, KD, E * HP)
    wo = f["Wo"].reshape(PAIRS, 2, EP, 2 * HP, D).transpose(0, 3, 1, 2, 4)
    out["wo"] = np.ascontiguousarray(wo)
    half = NROT // 2
    inv = np.float32(BASE) ** (-np.arange(half, dtype=np.float32) / np.float32(half))
    ang = np.arange(S, dtype=np.float32)[:, None] * inv[None, :]
    cos, sin = np.cos(ang).T.astype(np.float32), np.sin(ang).T.astype(np.float32)
    flat = np.ones((HP - NROT, S), np.float32)
    out["cos"] = np.tile(np.concatenate([cos, cos, flat]), (2, 1))
    out["sin"] = np.tile(np.concatenate([-sin, sin, 0 * flat]), (2, 1))
    other = np.concatenate([np.arange(half, NROT), np.arange(half), np.arange(NROT, HP)])
    out["swap"] = np.eye(P, dtype=np.float32)[:, np.concatenate([other, HP + other])]
    row = np.arange(BLOCKS)[:, None] * 2 + np.arange(P)[None, :] // HP
    takes = (np.arange(2 * E)[:, None, None] == row[None]).astype(np.float32).reshape(2 * E, BLOCKS * P)
    spread = np.zeros((P, BLOCKS * P), np.float32)
    spread[:2 * E] = spread[LOW_ROW:LOW_ROW + 2 * E] = takes
    out["spread"] = spread

    out["w1"], out["w2"] = rows(f["W1"], KD), rows(f["W2"], FB)
    out["b1"], out["b2"] = cols(f["b1"]), f["b2"]
    out["g1"], out["h1"], out["g2"], out["h2"] = f["ln1_g"], f["ln1_b"], f["ln2_g"], f["ln2_b"]
    return {n: np.ascontiguousarray(v) for n, v in out.items()}


def program(nc, d):
    d["xT"] = nc.dram_tensor("xT_scratch", (NB, P, KD, S), F32, kind="Internal").ap()
    d["x1"] = nc.dram_tensor("x1_scratch", (NB, S, D), F32, kind="Internal").ap()
    d["gates"] = nc.dram_tensor("gates_scratch", (PAIRS, P, NB, TT, GP), F32, kind="Internal").ap()
    with nc.sbuf_tensor("ident", [P, P], F32) as ident:
        const = {"ident": ident}
        stage_a(nc, d, const)
        with nc.sbuf_tensor("acc", [P, NB, KD, S], F32) as acc:
            stage_b(nc, d, const, acc)
            stage_c(nc, d, const, acc)


def kernel(**inputs):
    import concourse.bacc as bacc
    from concourse.bass_utils import run_bass_kernel_spmd

    nc = bacc.Bacc("TRN2", target_bir_lowering=False, num_devices=1)
    arrays = {f"in_{n}": v for n, v in layout(inputs).items()}
    d = {n[3:]: nc.dram_tensor(n, v.shape, mybir.dt.from_np(v.dtype), kind="ExternalInput").ap() for n, v in arrays.items()}
    d["out"] = nc.dram_tensor("out_0", (NB, S, D), F32, kind="ExternalOutput").ap()
    program(nc, d)
    result = run_bass_kernel_spmd(nc, [arrays], core_ids=[0])
    return result.results[0]["out_0"]
```
